# Optimizing a Trainium2 kernel written in Bass

```python
import numpy as np
import jax
import jax.numpy as jnp

def _softmax(x, axis=-1):
    return jax.nn.softmax(x, axis=axis)

def _gelu(x):
    return jax.nn.gelu(x, approximate=True)

def _silu(x):
    return jax.nn.silu(x)

def _sigmoid(x):
    return jax.nn.sigmoid(x)

def _layernorm(x, axis=-1, eps=1e-05):
    m = jnp.mean(x, axis=axis, keepdims=True)
    v = jnp.var(x, axis=axis, keepdims=True)
    return (x - m) / jnp.sqrt(v + eps)

def _scatter_add(tgt, idx, src, axis=0):
    return tgt.at[idx].add(src)

def _segment_sum(src, seg, n):
    return jax.ops.segment_sum(src, seg, n)
kernel_name = 'mk_lm_tower_d1_tok_ids768_r4_e337ef'

def setup_inputs(seed: int=0):
    np.random.seed(seed)
    _w = jnp.asarray

    def _rec_inputs():
        import jax
        import jax.numpy as jnp
        _rk = jax.random.key(seed)
        x = jax.random.randint(jax.random.fold_in(_rk, 1), (2, 2048), 0, 12564, jnp.int32)
        return x
    x = _rec_inputs()

    def _L0_tok_setup():
        import jax, jax.numpy as jnp
        import numpy as np
        BASE = 16

        def _digits(T):
            temp = np.arange(T, dtype=np.int64)
            digits = []
            while True:
                digits.append(temp % BASE)
                temp = temp // BASE
                if temp.max() == 0:
                    break
            return digits[::-1]
        key = jax.random.key(seed)
        k1, k2, k3, k4 = jax.random.split(key, 4)
        B, T, V, C = (8, 1024, 50257, 192)
        idx = jax.random.randint(k1, (B, T), 0, V, dtype=jnp.int64)
        tok_table = jax.random.normal(k2, (V, C), dtype=jnp.float32) * 0.02
        pos_table = jax.random.normal(k3, (BASE, C), dtype=jnp.float32) * 0.02
        carry_W = jax.random.normal(k4, (C, C), dtype=jnp.float32) * 0.02
        return {'idx': idx, 'tok_table': tok_table, 'pos_table': pos_table, 'carry_W': carry_W}
    _L0_tok_all = _L0_tok_setup()
    _L0_tok_in = {k: v for k, v in _L0_tok_all.items() if k in ('tok_table', 'pos_table', 'carry_W')}
    del _L0_tok_all

    def _L0_attn_setup():
        import jax, jax.numpy as jnp
        import numpy as np
        N_HEADS = 12
        key = jax.random.key(seed)
        k1, k2, k3 = jax.random.split(key, 3)
        B, S, W = (8, 256, 192)
        x = jax.random.normal(k1, (B, S, W), dtype=jnp.float32)
        w_qkv = jax.random.normal(k2, (W, 3 * W), dtype=jnp.float32) * W ** (-0.5)
        w_out = jax.random.normal(k3, (W, W), dtype=jnp.float32) * W ** (-0.5)
        return {'x': x, 'w_qkv': w_qkv, 'w_out': w_out}
    _L0_attn_all = _L0_attn_setup()
    _L0_attn_in = {k: v for k, v in _L0_attn_all.items() if k in ('w_qkv', 'w_out')}
    del _L0_attn_all

    def _L0_ffn_setup():
        import jax, jax.numpy as jnp
        import numpy as np
        B, N, D, E, F, K = (2, 512, 192, 8, 768, 2)
        V_MAX = 3.0
        FEAT_CLAMP = 10.0

        def bk_green_diag(a):
            aT = jnp.swapaxes(a, 0, 1)

            def step(c, ai):
                d = ai - 1.0 / c
                return (d, d)
            d0 = aT[0]
            _, d_rest = jax.lax.scan(step, d0, aT[1:])
            d = jnp.concatenate([d0[None], d_rest], axis=0)
            eN = aT[-1]
            _, e_rest = jax.lax.scan(step, eN, aT[:-1], reverse=True)
            e = jnp.concatenate([e_rest, eN[None]], axis=0)
            G = 1.0 / (d + e - aT)
            return jnp.swapaxes(G, 0, 1)
        key = jax.random.key(seed)
        ks = jax.random.split(key, 8)
        s = lambda k, shape, sc: jax.random.normal(k, shape, jnp.float32) * sc
        return {'x': s(ks[0], (B, N, D), 1.0), 'v_w': s(ks[1], (D,), 0.02), 'v_b': jnp.zeros((), jnp.float32), 'gate_w': s(ks[2], (D, E), 0.02), 'gate_b': jnp.zeros((E,), jnp.float32), 'w1': s(ks[3], (E, D, F), 0.02), 'b1': jnp.zeros((E, F), jnp.float32), 'w2': s(ks[4], (E, F, D), 0.02), 'b2': jnp.zeros((E, D), jnp.float32), 'out_w': s(ks[5], (2, D), 0.02), 'out_b': jnp.zeros((D,), jnp.float32), 'bk_scale': jnp.ones((D,), jnp.float32)}
    _L0_ffn_all = _L0_ffn_setup()
    _L0_ffn_in = {k: v for k, v in _L0_ffn_all.items() if k in ('v_w', 'v_b', 'gate_w', 'gate_b', 'w1', 'b1', 'w2', 'b2', 'out_w', 'out_b', 'bk_scale')}
    del _L0_ffn_all
    return {'x': x, 'L0_tok_tok_table': _L0_tok_in['tok_table'], 'L0_tok_pos_table': _L0_tok_in['pos_table'], 'L0_tok_carry_W': _L0_tok_in['carry_W'], 'L0_attn_w_qkv': _L0_attn_in['w_qkv'], 'L0_attn_w_out': _L0_attn_in['w_out'], 'L0_ffn_v_w': _L0_ffn_in['v_w'], 'L0_ffn_v_b': _L0_ffn_in['v_b'], 'L0_ffn_gate_w': _L0_ffn_in['gate_w'], 'L0_ffn_gate_b': _L0_ffn_in['gate_b'], 'L0_ffn_w1': _L0_ffn_in['w1'], 'L0_ffn_b1': _L0_ffn_in['b1'], 'L0_ffn_w2': _L0_ffn_in['w2'], 'L0_ffn_b2': _L0_ffn_in['b2'], 'L0_ffn_out_w': _L0_ffn_in['out_w'], 'L0_ffn_out_b': _L0_ffn_in['out_b'], 'L0_ffn_bk_scale': _L0_ffn_in['bk_scale']}

def reference(x, L0_tok_tok_table, L0_tok_pos_table, L0_tok_carry_W, L0_attn_w_qkv, L0_attn_w_out, L0_ffn_v_w, L0_ffn_v_b, L0_ffn_gate_w, L0_ffn_gate_b, L0_ffn_w1, L0_ffn_b1, L0_ffn_w2, L0_ffn_b2, L0_ffn_out_w, L0_ffn_out_b, L0_ffn_bk_scale):
    import jax
    import jax.numpy as jnp

    def _L0_tok_ref(idx, tok_table, pos_table, carry_W):
        import jax, jax.numpy as jnp
        import numpy as np
        BASE = 16

        def _digits(T):
            temp = np.arange(T, dtype=np.int64)
            digits = []
            while True:
                digits.append(temp % BASE)
                temp = temp // BASE
                if temp.max() == 0:
                    break
            return digits[::-1]
        B, T = idx.shape
        C = tok_table.shape[1]
        tok_emb = tok_table[idx]
        state = jnp.zeros((T, C), dtype=tok_table.dtype)
        for d in _digits(T):
            state = state @ carry_W.T + pos_table[jnp.asarray(d)]
        pos_emb = state[::-1]
        return tok_emb + pos_emb[None, :, :]

    def _L0_attn_ref(x, w_qkv, w_out):
        import jax, jax.numpy as jnp
        import numpy as np
        N_HEADS = 12
        B, S, W = x.shape
        H = N_HEADS
        D = W // H
        scale = W ** (-0.5)
        qkv = x @ w_qkv
        q, k, v = jnp.split(qkv, 3, axis=2)
        q = q.reshape(B, S, H, D)
        k = k.reshape(B, S, H, D)
        attn_score = jnp.einsum('binh,bjnh->bijn', q, k) * scale
        attn_weight = jax.nn.softmax(attn_score, axis=2)
        out = jnp.einsum('bijn,bjnh->binh', attn_weight, k)
        out = out.reshape(B, S, W)
        return out @ w_out

    def _L0_ffn_ref(x, v_w, v_b, gate_w, gate_b, w1, b1, w2, b2, out_w, out_b, bk_scale):
        import jax, jax.numpy as jnp
        import numpy as np
        B, N, D, E, F, K = (2, 512, 192, 8, 768, 2)
        V_MAX = 3.0
        FEAT_CLAMP = 10.0

        def bk_green_diag(a):
            aT = jnp.swapaxes(a, 0, 1)

            def step(c, ai):
                d = ai - 1.0 / c
                return (d, d)
            d0 = aT[0]
            _, d_rest = jax.lax.scan(step, d0, aT[1:])
            d = jnp.concatenate([d0[None], d_rest], axis=0)
            eN = aT[-1]
            _, e_rest = jax.lax.scan(step, eN, aT[:-1], reverse=True)
            e = jnp.concatenate([e_rest, eN[None]], axis=0)
            G = 1.0 / (d + e - aT)
            return jnp.swapaxes(G, 0, 1)
        v = jnp.clip(x @ v_w + v_b, -V_MAX, V_MAX)
        a = (-2.0 + v).astype(jnp.complex64) - 1j
        G = bk_green_diag(a)
        feats = jnp.stack([G.real, G.imag], axis=-1)
        logits = x @ gate_w + gate_b
        probs = jax.nn.softmax(logits, axis=-1)
        topv, topi = jax.lax.top_k(probs, K)
        topv = topv / jnp.sum(topv, axis=-1, keepdims=True)
        comb = jnp.sum(topv[..., None] * jax.nn.one_hot(topi, E, dtype=x.dtype), axis=2)
        h = jax.nn.gelu(jnp.einsum('bnd,edf->bnef', x, w1) + b1)
        y = jnp.einsum('bnef,efd->bned', h, w2) + b2
        ffn_out = jnp.einsum('bne,bned->bnd', comb, y)
        feats_c = jnp.clip(feats, -FEAT_CLAMP, FEAT_CLAMP)
        spec_out = feats_c @ out_w + out_b
        return ffn_out + bk_scale * spec_out
    h = _L0_tok_ref(x, L0_tok_tok_table, L0_tok_pos_table, L0_tok_carry_W)
    h = h + _L0_attn_ref(_layernorm(h, axis=-1), L0_attn_w_qkv, L0_attn_w_out)
    h = h + _L0_ffn_ref(_layernorm(h, axis=-1), L0_ffn_v_w, L0_ffn_v_b, L0_ffn_gate_w, L0_ffn_gate_b, L0_ffn_w1, L0_ffn_b1, L0_ffn_w2, L0_ffn_b2, L0_ffn_out_w, L0_ffn_out_b, L0_ffn_bk_scale)
    return h

_drawn_inputs = setup_inputs


def setup_inputs(seed=0):
    import zlib

    import numpy as np

    out = dict(_drawn_inputs(seed))
    spreads = {'L0_ffn_gate_b': (0.0, 0.1),
     'L0_ffn_b1': (0.0, 0.1),
     'L0_ffn_b2': (0.0, 0.1),
     'L0_ffn_out_b': (0.0, 0.1),
     'L0_ffn_bk_scale': (1.0, 0.2)}
    factors = {'L0_ffn_v_w': 5.399}
    for name, (base, spread) in spreads.items():
        noise = np.random.default_rng([zlib.crc32(name.encode()), seed]).standard_normal(out[name].shape)
        drawn = base * np.exp(spread * noise) if base else spread * noise
        out[name] = jnp.asarray(drawn.astype(out[name].dtype))
    for name, factor in factors.items():
        out[name] = (out[name] * factor).astype(out[name].dtype)
    return out
```

```python
import numpy as np

import concourse.bass as bass
from concourse import mybir
from contextlib import ExitStack

F32 = mybir.dt.float32
BF16 = mybir.dt.bfloat16
I32 = mybir.dt.int32
U32 = mybir.dt.uint32
ALU = mybir.AluOpType
ACT = mybir.ActivationFunctionType
AX = mybir.AxisListType

P = 128
B, S, C = 2, 2048, 192
H, D = 12, 16
E, F = 8, 768
N = B * S
CB = C - P
TB = S // P
NT = B * TB
CT = 4
CW = CT * P
NCH = N // CW
QC = S // CW
HG = 4
NG = B * (H // HG)
STEPS = NG * QC
KT = S // P
ET = (2 * N + E * (P - 1)) // P
EPS = 1e-5
SCALE = float(C) ** -0.5
V_MAX = 3.0
FEAT_CLAMP = 10.0

Q_PIECE = [0, 0, 0, 1, 1, 2]
K_PIECE = [0, 1, 2, 0, 1, 0]
KR = len(Q_PIECE) * D
MR = 3


class Tally:

    def __init__(self, sem, base=0):
        self.sem, self.base, self.n = sem, base, 0

    def add(self, ins, k=1):
        ins.then_inc(self.sem, k)
        self.n += k
        return self.base + self.n


def ds(start, n):
    return bass.ds(start, n)


def hold(eng, sem, value):
    eng.wait_ge(sem, value)
    eng.nop(nofuse=True)


class Chip:
    pass


def embed_and_project(nc, g, x, tok_table, pos_rev, pos_rev_t, carry_t, w_qkv):
    with ExitStack() as ctx:
        sb = lambda name, shape, dt=F32: ctx.enter_context(nc.sbuf_tensor(name, shape, dt))
        ps = lambda name, shape, dt=F32: ctx.enter_context(nc.psum_tensor(name, shape, dt))
        sem = lambda name: ctx.enter_context(nc.semaphore(name))

        idx = sb("token_ids", [P, B, TB], I32)
        wqk_a, wqk_b = sb("wqk_a", [P, 2 * C]), sb("wqk_b", [CB, 2 * C])
        ct_a, ct_b = sb("carry_a", [P, C]), sb("carry_b", [CB, C])
        prt_a, prt_b = sb("pos_t_a", [P, 16]), sb("pos_t_b", [CB, 16])
        prow = sb("pos_rows", [P, TB, C])
        zt_a, zt_b = sb("high_digit_a", [P, 8]), sb("high_digit_b", [CB, 8])
        yt_a, yt_b = sb("two_digits_a", [P, 8, 16]), sb("two_digits_b", [CB, 8, 16])
        pos = sb("pos_all", [P, TB, C])
        stats = sb("ln_stats", [P, CT, 6])
        mv = sb("ln_mean_var", [P, CT, 2])
        ve = sb("ln_var_eps", [P, CT])
        sd = sb("ln_sd", [P, CT])
        rstd = sb("ln_rstd", [P, CT])
        x1 = sb("x1", [P, CT, C])
        xa, xb = sb("x1_t_a", [P, CW]), sb("x1_t_b", [CB, CW])
        parts = sb("qk_parts_sb", [P, 3, 3, CW], BF16)
        rem = sb("qk_rem", [P, 3, CW])

        ps_ta, ps_tb = ps("ps_ta", [P, CW]), ps("ps_tb", [CB, CW])
        ps_qk = [ps(f"ps_qk{m}", [P, CW]) for m in range(3)]
        ps_v = [ps(f"ps_v{m}", [P, 2 * C]) for m in range(2)]

        loaded = sem("a_loaded")
        ids_in = sem("a_ids_in")
        gathered = [sem("a_gathered0"), sem("a_gathered1")]
        const_made = sem("a_const_made")
        pe_pos = sem("a_pe_pos")
        act_pos = sem("a_act_pos")
        v_chain = sem("a_v_chain")
        pos_ready = sem("a_pos_ready")
        pos_made = sem("a_pos_made")
        var_ready = sem("a_var_ready")
        sd_ready = sem("a_sd_ready")
        x1_ready = sem("a_x1_ready")
        turned = sem("a_turned")
        xt_ready = sem("a_xt_ready")
        projected = sem("a_projected")
        v_projected = sem("a_v_projected")
        piece1 = sem("a_piece1")
        rem1 = sem("a_rem1")
        piece2 = sem("a_piece2")
        piece3 = sem("a_piece3")
        v_copied = sem("a_v_copied")
        stored = sem("a_stored")

        with nc.Block() as block:

            @block.sync
            def _(sp):
                sp.dma_start(idx[:], x.rearrange("b (p c) -> p b c", c=TB)).then_inc(ids_in, 16)
                for dst, src in ((ct_a[:], carry_t[0:P]), (ct_b[:], carry_t[P:C]), (prt_a[:], pos_rev_t[0:P]),
                                 (prt_b[:], pos_rev_t[P:C]), (wqk_a[:], w_qkv[0:P, 0:2 * C]),
                                 (wqk_b[:], w_qkv[P:C, 0:2 * C])):
                    sp.dma_start(dst, src).then_inc(loaded, 16)
                sp.dma_start(prow[:].rearrange("p c n -> p (c n)"),
                             pos_rev.rearrange("(a c) n -> a (c n)", a=1).to_broadcast([P, TB * C])).then_inc(loaded, 16)
                with sp.Fori(0, NCH) as i:
                    for m in range(3):
                        sp.wait_ge(piece1, 3 * i + m + 1)
                        sp.wait_ge(piece2, 3 * i + m + 1)
                        sp.wait_ge(piece3, 3 * i + m + 1)
                        sp.dma_start(g.qk_parts[:, P * m:P * (m + 1), ds(i * CW, CW)].rearrange("t p n -> p t n"),
                                     parts[:, m]).then_inc(stored, 16)
                    hold(sp, stored, 48 * i + 48)

            @block.gpsimd
            def _(pool):
                pool.memset(g.ident[:], 0.0).then_inc(const_made, 1)
                pool.memset(g.spread[:], 0.0).then_inc(const_made, 1)
                pool.wait_ge(const_made, 2)
                pool.affine_select(out=g.ident[:], in_=g.ident[:], compare_op=ALU.not_equal, fill=1.0, base=0,
                                   pattern=[[-1, P]], channel_multiplier=1).then_inc(const_made, 1)
                sel = g.spread[:].rearrange("p (h r) -> p h r", h=HG)
                pool.affine_select(out=sel, in_=sel, compare_op=ALU.not_equal, fill=1.0, base=-D,
                                   pattern=[[-32, HG], [0, 32]], channel_multiplier=1).then_inc(const_made, 1)
                pool.wait_ge(ids_in, 16)
                for i in range(NCH):
                    if i >= 2:
                        pool.wait_ge(gathered[i % 2], 16 * CT * (i // 2))
                    for t in range(CT * i, CT * (i + 1)):
                        pool.indirect_dma_start(
                            out=g.h[:, t, :], out_offset=None, in_=tok_table,
                            in_offset=bass.IndirectOffsetOnAxis(ap=idx[:, t // TB, t % TB:t % TB + 1], axis=0),
                        ).then_inc(gathered[i % 2], 16)

            @block.tensor
            def _(pe):
                pe.wait_ge(loaded, 16 * 7)
                pe.wait_ge(const_made, 4)
                for dst, m0, m1 in ((ps_ta[:, 0:8], 0, P), (ps_tb[:, 0:8], P, C)):
                    nc.tensor.matmul(dst, ct_a[:, m0:m1], prt_a[:, 8:16], start=True, stop=False)
                    nc.tensor.matmul(dst, ct_b[:, m0:m1], prt_b[:, 8:16], start=False, stop=True).then_inc(pe_pos, 1)
                pe.wait_ge(pos_ready, 2)
                nc.tensor.matmul(ps_v[0][:, 0:C], yt_a[:].rearrange("p a r -> p (a r)"), ct_a[:], start=True, stop=False)
                nc.tensor.matmul(ps_v[0][:, 0:C], yt_b[:].rearrange("p a r -> p (a r)"), ct_b[:], start=False,
                                 stop=True).then_inc(pe_pos, 1)
                with pe.Fori(0, NCH) as i:
                    pe.wait_ge(x1_ready, i + 1)
                    for j in range(CT):
                        nc.tensor.transpose(ps_ta[:, j * P:(j + 1) * P], x1[:, j, 0:P], g.ident[:])
                        last = nc.tensor.transpose(ps_tb[:, j * P:(j + 1) * P], x1[:, j, P:C], g.ident[:])
                    last.then_inc(turned, 1)
                    pe.wait_ge(xt_ready, 2 * i + 2)
                    for m in range(3):
                        pe.wait_ge(rem1, 3 * i)
                        nc.tensor.matmul(ps_qk[m][:], wqk_a[:, m * P:(m + 1) * P], xa[:], start=True, stop=False)
                        nc.tensor.matmul(ps_qk[m][:], wqk_b[:, m * P:(m + 1) * P], xb[:], start=False,
                                         stop=True).then_inc(projected, 1)
                    pe.wait_ge(v_copied, 2 * i)
                    pe.wait_ge(pos_made, 1)
                    for j in range(CT):
                        dst = ps_v[j // 2][:, (j % 2) * C:(j % 2 + 1) * C]
                        nc.tensor.matmul(dst, xa[:, j * P:(j + 1) * P], wqk_a[:, C:2 * C], start=True, stop=False)
                        last = nc.tensor.matmul(dst, xb[:, j * P:(j + 1) * P], wqk_b[:, C:2 * C], start=False, stop=True)
                    last.then_inc(v_projected, 1)

            @block.scalar
            def _(act):
                act.wait_ge(pe_pos, 1)
                nc.scalar.activation(zt_a[:], ps_ta[:, 0:8], ACT.Copy).then_inc(act_pos, 1)
                act.wait_ge(pe_pos, 2)
                nc.scalar.activation(zt_b[:], ps_tb[:, 0:8], ACT.Copy).then_inc(act_pos, 1)
                with act.Fori(0, NCH) as i:
                    act.wait_ge(var_ready, i + 1)
                    nc.scalar.activation(sd[:], ve[:], ACT.Sqrt).then_inc(sd_ready, 1)
                    act.wait_ge(turned, i + 1)
                    act.wait_ge(v_projected, i)
                    nc.scalar.activation(xa[:], ps_ta[:], ACT.Copy).then_inc(xt_ready, 1)
                    nc.scalar.activation(xb[:], ps_tb[:], ACT.Copy).then_inc(xt_ready, 1)
                    act.wait_ge(stored, 48 * i)
                    for m in range(3):
                        act.wait_ge(projected, 3 * i + m + 1)
                        nc.scalar.activation(parts[:, m, 0, :], ps_qk[m][:], ACT.Copy).then_inc(piece1, 1)
                    for m in range(3):
                        act.wait_ge(rem1, 3 * i + m + 1)
                        nc.scalar.activation(parts[:, m, 1, :], rem[:, m, :], ACT.Copy).then_inc(piece2, 1)
                    act.wait_ge(v_projected, i + 1)
                    for m in range(2):
                        nc.scalar.activation(g.v[:, ds(CT * i + 2 * m, 2), :],
                                             ps_v[m][:].rearrange("p (j n) -> p j n", j=2), ACT.Copy).then_inc(v_copied, 1)

            @block.vector
            def _(dve):
                for k, (dst, z, r, n) in enumerate(((yt_a, zt_a, prt_a, P), (yt_b, zt_b, prt_b, CB))):
                    dve.wait_ge(act_pos, k + 1)
                    dve.wait_ge(loaded, 16 * 7)
                    nc.vector.tensor_tensor(dst[:], z[:].unsqueeze(2).to_broadcast([n, 8, 16]),
                                            r[:].unsqueeze(1).to_broadcast([n, 8, 16]), ALU.add).then_inc(pos_ready, 1)
                dve.wait_ge(pe_pos, 3)
                nc.vector.tensor_tensor(pos[:], ps_v[0][:, 0:C].unsqueeze(1).to_broadcast([P, TB, C]), prow[:],
                                        ALU.add).then_inc(pos_made, 1)
                dve.wait_ge(pos_made, 1)
                per_turn = 9 + CT
                with dve.Fori(0, NCH // 2) as k:
                    for r in range(2):
                        i = k * 2 + r
                        chain = Tally(v_chain, i * per_turn)
                        dve.wait_ge(gathered[r], 16 * CT * k + 16 * CT)
                        hc = g.h[:, ds(CT * i, CT), :]
                        n = chain.add(nc.vector.tensor_tensor(hc, hc, pos[:, ds((i % QC) * CT, CT), :], ALU.add))
                        hold(dve, chain.sem, n)
                        for j in range(CT):
                            n = chain.add(nc.vector.bn_stats(stats[:, j, :], g.h[:, ds(CT * i + j, 1), :]
                                                             .rearrange("p a n -> p (a n)")))
                        hold(dve, chain.sem, n)
                        for j in range(CT):
                            n = chain.add(nc.vector.bn_aggr(mv[:, j, :], stats[:, j, :]))
                        dve.wait_ge(chain.sem, n)
                        nc.vector.tensor_scalar_add(ve[:], mv[:, :, 1], EPS).then_inc(var_ready, 1)
                        dve.wait_ge(sd_ready, i + 1)
                        n = chain.add(nc.vector.reciprocal(rstd[:], sd[:]))
                        dve.wait_ge(chain.sem, n)
                        dve.wait_ge(turned, i)
                        for j in range(CT):
                            ins = nc.vector.tensor_scalar(x1[:, j, :], g.h[:, ds(CT * i + j, 1), :]
                                                          .rearrange("p a n -> p (a n)"),
                                                          mv[:, j, 0:1], rstd[:, j:j + 1], ALU.subtract, ALU.mult)
                            if j < CT - 1:
                                chain.add(ins)
                            else:
                                ins.then_inc(x1_ready, 1)
                        assert chain.n == per_turn
                        for m in range(3):
                            dve.wait_ge(piece1, 3 * i + m + 1)
                            nc.vector.tensor_tensor(rem[:, m, :], ps_qk[m][:], parts[:, m, 0, :],
                                                    ALU.subtract).then_inc(rem1, 1)
                        for m in range(3):
                            dve.wait_ge(piece2, 3 * i + m + 1)
                            nc.vector.tensor_tensor(parts[:, m, 2, :], rem[:, m, :], parts[:, m, 1, :],
                                                    ALU.subtract).then_inc(piece3, 1)


def attention(nc, g):
    TURN = KT * HG
    SWEEP = 2 * KT
    HALF = S // 2

    with ExitStack() as ctx:
        sb = lambda name, shape, dt=F32: ctx.enter_context(nc.sbuf_tensor(name, shape, dt))
        ps = lambda name, shape, dt=F32: ctx.enter_context(nc.psum_tensor(name, shape, dt))
        sem = lambda name: ctx.enter_context(nc.semaphore(name))

        k6 = sb("k_pieces", [P, 2, HG, S], BF16)
        q6 = sb("q_pieces", [P, 4, HG, CW], BF16)
        probs = sb("probs", [P, 2, HG, CW])
        vcur = sb("v_group", [P, KT, HG, 2 * D])
        half_max = sb("half_max", [P, KT, 2])
        row_max = sb("row_max", [P, KT])
        neg = sb("neg_rest", [KT, P])
        neg_parts = sb("neg_max_parts", [KT, 3, P], BF16)
        mixed = sb("mixed", [P, CW])
        inv = sb("inv_sum", [P, CW])

        ps_score = [ps(f"ps_score{k}", [P, CW]) for k in range(2)]
        ps_sweep = [ps(f"ps_sweep{k}", [P, HALF]) for k in range(2)]
        ps_out = ps("ps_out", [P, CW])
        ps_misc = ps("ps_misc", [P, CW])

        k_in, q_in, m_in = sem("b_k_in"), sem("b_q_in"), sem("b_m_in")
        ones_made = sem("b_ones_made")
        turn_done = sem("b_turn_done")
        scored = sem("b_scored")
        score_slots = sem("b_score_slots")
        prob_slots = sem("b_prob_slots")
        swept = sem("b_swept")
        sweep_slots = sem("b_sweep_slots")
        max_ready = sem("b_max_ready")
        max_turned = sem("b_max_turned")
        neg_chain = sem("b_neg_chain")
        neg_ready = sem("b_neg_ready")
        v_ready = sem("b_v_ready")
        out_copied = sem("b_out_copied")
        spread = sem("b_spread")
        inv_ready = sem("b_inv_ready")
        normed = sem("b_normed")

        def load_k(sp, gg):
            row = C + (gg % (NG // B)) * HG * D
            col = (gg // (NG // B)) * S
            for n, part in enumerate(K_PIECE):
                sp.dma_start(k6[n * D:(n + 1) * D, ds(gg % 2, 1), :, :].rearrange("r a h n -> r (a h) n"),
                             g.qk_parts[part, ds(row, HG * D), ds(col, S)].rearrange("(h r) n -> r h n", r=D)
                             ).then_inc(k_in, 16)
            hold(sp, k_in, (gg + 1) * 96)

        def load_q(sp, i):
            row = ((i // QC) % (NG // B)) * HG * D
            col = (i // STEPS_B) * S + (i % QC) * CW
            for n, part in enumerate(Q_PIECE):
                sp.dma_start(q6[n * D:(n + 1) * D, ds(i % 4, 1), :, :].rearrange("r a h n -> r (a h) n"),
                             g.qk_parts[part, ds(row, HG * D), ds(col, CW)].rearrange("(h r) n -> r h n", r=D)
                             ).then_inc(q_in, 16)
            hold(sp, q_in, (i + 1) * 96)

        STEPS_B = STEPS // B

        with nc.Block() as block:

            @block.sync
            def _(sp):
                load_k(sp, 0)
                load_q(sp, 0)
                load_q(sp, 1)
                load_k(sp, 1)
                load_q(sp, 2)
                load_q(sp, 3)
                with sp.Fori(1, NG - 1) as gg:
                    for r in range(QC):
                        sp.wait_ge(turn_done, gg * QC + r - 3)
                        load_q(sp, gg * QC + r)
                    load_k(sp, gg + 1)
                for r in range(QC):
                    sp.wait_ge(turn_done, (NG - 1) * QC + r - 3)
                    load_q(sp, (NG - 1) * QC + r)

            @block.gpsimd
            def _(pool):
                pool.memset(vcur[:, :, :, D:2 * D], 1.0).then_inc(ones_made, 1)

                def neg_rows(i):
                    pool.wait_ge(neg_ready, i + 1)
                    for part in range(MR):
                        pool.dma_start(q6[KR + part:KR + part + 1, ds(i % 4, 1), :, :].rearrange("r a h n -> r (a h n)"),
                                       neg_parts[:, part, :]).then_inc(m_in, 16)

                def copy_v(i, kt):
                    b, hg = i // STEPS_B, (i // QC) % (NG // B)
                    pool.tensor_copy(vcur[:, kt, :, 0:D],
                                     g.v[:, ds(b * TB + kt, 1), ds(hg * HG * D, HG * D)]
                                     .rearrange("p a (h d) -> p (a h) d", h=HG)).then_inc(v_ready, 1)

                for kt in range(KT):
                    copy_v(0, kt)
                neg_rows(0)

                def turn(i):
                    neg_rows(i + 1)
                    for kt in range(KT):
                        pool.wait_ge(prob_slots, 2 + i * KT + kt + 1)
                        copy_v(i + 1, kt)

                with pool.Fori(0, STEPS - 1) as i:
                    turn(i)

            @block.tensor
            def _(pe):
                pe.wait_ge(ones_made, 2)

                def score(i, kt, h):
                    u = i * TURN + kt * HG + h
                    pe.wait_ge(score_slots, u + 1)
                    nc.tensor.matmul(ps_score[h % 2][:],
                                     k6[0:KR + MR, ds((i // QC) % 2, 1), h, kt * P:(kt + 1) * P].rearrange("p a n -> p (a n)"),
                                     q6[0:KR + MR, ds(i % 4, 1), h, :].rearrange("p a n -> p (a n)"),
                                     start=True, stop=True).then_inc(scored, 1)

                def sweep(i, kt, half):
                    h, t = kt // CT, kt % CT
                    pe.wait_ge(sweep_slots, i * SWEEP + 2 * kt + half + 1)
                    for c in range(2):
                        k0 = half * HALF + c * CW
                        ins = nc.tensor.matmul(ps_sweep[half][:, c * CW:(c + 1) * CW],
                                               q6[0:KR, ds(i % 4, 1), h, t * P:(t + 1) * P].rearrange("p a n -> p (a n)"),
                                               k6[0:KR, ds((i // QC) % 2, 1), h, k0:k0 + CW].rearrange("p a n -> p (a n)"),
                                               start=True, stop=True)
                    ins.then_inc(swept, 1)

                def mix(i, kt):
                    pe.wait_ge(score_slots, 2 + i * TURN + (kt + 1) * HG)
                    pe.wait_ge(v_ready, i * KT + kt + 1)
                    if kt == 0:
                        pe.wait_ge(out_copied, i)
                    for h in range(HG):
                        ins = nc.tensor.matmul(ps_out[32 * h:32 * (h + 1), :], vcur[:, kt, h, :], probs[:, kt % 2, h, :],
                                               start=(kt == 0), stop=(kt == KT - 1))
                    ins.then_inc(prob_slots, 1)

                def turn_max(i):
                    pe.wait_ge(max_ready, i + 1)
                    nc.tensor.transpose(ps_misc[0:KT, 0:P], row_max[:], g.ident[:]).then_inc(max_turned, 1)

                def spread_sums(i):
                    pe.wait_ge(out_copied, i + 1)
                    nc.tensor.matmul(ps_misc[:], g.spread[:], mixed[:], start=True, stop=True).then_inc(spread, 1)

                def turn(i, first=False, ahead=True):
                    pe.wait_ge(m_in, (i + 1) * 48)
                    if ahead:
                        pe.wait_ge(q_in, (i + 3) * 96)
                        pe.wait_ge(k_in, ((i + 2) // QC + 1) * 96)
                    for kt in range(KT):
                        score(i, kt, 0)
                        if ahead:
                            sweep(i + 2, kt, 0)
                        score(i, kt, 1)
                        if kt > 0:
                            mix(i, kt - 1)
                        elif not first:
                            mix(i - 1, KT - 1)
                        score(i, kt, 2)
                        if ahead:
                            sweep(i + 2, kt, 1)
                        score(i, kt, 3)
                        if kt == 2 and (ahead or i == STEPS - 2):
                            if not first:
                                pe.wait_ge(inv_ready, i - 1)
                            turn_max(i + 1)
                        if kt == 5 and not first:
                            pe.wait_ge(neg_ready, i + 2 if ahead or i == STEPS - 2 else STEPS)
                            spread_sums(i - 1)
                    pe.drain().then_inc(turn_done, 1)

                pe.wait_ge(k_in, 96)
                for i in range(2):
                    pe.wait_ge(q_in, (i + 1) * 96)
                    for kt in range(KT):
                        sweep(i, kt, 0)
                        sweep(i, kt, 1)
                    if i == 0:
                        turn_max(0)
                turn(0, first=True)
                with pe.Fori(1, STEPS - 2) as i:
                    turn(i)
                turn(STEPS - 2, ahead=False)
                turn(STEPS - 1, ahead=False)
                mix(STEPS - 1, KT - 1)
                pe.wait_ge(inv_ready, STEPS - 1)
                spread_sums(STEPS - 1)

            @block.scalar
            def _(act):
                act.sem_inc(score_slots, 2)

                def copy_out(i):
                    act.wait_ge(prob_slots, 2 + (i + 1) * KT)
                    act.wait_ge(normed, i)
                    nc.scalar.activation(mixed[:], ps_out[:], ACT.Copy).then_inc(out_copied, 1)

                def turn(i, first=False):
                    for kt in range(KT):
                        act.wait_ge(prob_slots, i * KT + kt + 1)
                        for h in range(HG):
                            act.wait_ge(scored, i * TURN + kt * HG + h + 1)
                            nc.scalar.activation(probs[:, kt % 2, h, :], ps_score[h % 2][:], ACT.Exp,
                                                 scale=SCALE).then_inc(score_slots, 1)
                        if kt == 0 and not first:
                            copy_out(i - 1)

                turn(0, first=True)
                with act.Fori(1, STEPS) as i:
                    turn(i)
                copy_out(STEPS - 1)

            @block.vector
            def _(dve):
                nc.vector.memset(k6[KR:KR + MR, :, :, :], 1.0).then_inc(ones_made, 1)
                dve.sem_inc(sweep_slots, 2)
                dve.sem_inc(prob_slots, 2)

                def half_row(i, w):
                    if w == 0:
                        dve.wait_ge(max_ready, i)
                    dve.wait_ge(swept, i * SWEEP + w + 1)
                    nc.vector.tensor_reduce(half_max[:, w // 2, w % 2:w % 2 + 1], ps_sweep[w % 2][:], AX.X,
                                            ALU.max).then_inc(sweep_slots, 1)

                def whole_rows(i):
                    dve.wait_ge(sweep_slots, 2 + (i + 1) * SWEEP)
                    dve.wait_ge(max_turned, i)
                    nc.vector.tensor_reduce(row_max[:], half_max[:], AX.X, ALU.max).then_inc(max_ready, 1)

                def cut_max(i):
                    chain = Tally(neg_chain, i * 3)
                    dve.wait_ge(max_turned, i + 1)
                    dve.wait_ge(m_in, i * 48)
                    mt = ps_misc[0:KT, 0:P]
                    n = chain.add(nc.vector.tensor_scalar(neg_parts[:, 0, :], mt, -1.0, None, ALU.mult))
                    dve.wait_ge(neg_chain, n)
                    n = chain.add(nc.vector.scalar_tensor_tensor(out=neg[:], in0=mt, scalar=-1.0, in1=neg_parts[:, 0, :],
                                                                 op0=ALU.mult, op1=ALU.subtract))
                    dve.wait_ge(neg_chain, n)
                    n = chain.add(nc.vector.tensor_copy(neg_parts[:, 1, :], neg[:]))
                    dve.wait_ge(neg_chain, n)
                    nc.vector.tensor_tensor(neg_parts[:, 2, :], neg[:], neg_parts[:, 1, :],
                                            ALU.subtract).then_inc(neg_ready, 1)

                def normalise(i):
                    dve.wait_ge(spread, i + 1)
                    nc.vector.reciprocal(inv[:], ps_misc[:]).then_inc(inv_ready, 1)
                    dve.wait_ge(inv_ready, i + 1)
                    nc.vector.tensor_tensor(g.mixed[:, ds(i // QC, 1), ds((i % QC) * CW, CW)]
                                            .rearrange("p a n -> p (a n)"), mixed[:], inv[:], ALU.mult).then_inc(normed, 1)

                def turn(i, first=False, ahead=True):
                    for w in range(SWEEP):
                        if ahead:
                            half_row(i + 2, w)
                        if w == 5 and (ahead or i == STEPS - 2):
                            cut_max(i + 1)
                        if w == 11 and not first:
                            normalise(i - 1)
                    if ahead:
                        whole_rows(i + 2)

                for w in range(SWEEP):
                    half_row(0, w)
                whole_rows(0)
                cut_max(0)
                for w in range(SWEEP):
                    half_row(1, w)
                whole_rows(1)
                turn(0, first=True)
                with dve.Fori(1, STEPS - 2) as i:
                    turn(i)
                turn(STEPS - 2, ahead=False)
                turn(STEPS - 1, ahead=False)
                normalise(STEPS - 1)


def mix_heads_and_gate(nc, g, w_out, gate_rows, gate_bias, w1, b1, w2, b2_rows):
    with ExitStack() as ctx:
        sb = lambda name, shape, dt=F32: ctx.enter_context(nc.sbuf_tensor(name, shape, dt))
        ps = lambda name, shape, dt=F32: ctx.enter_context(nc.psum_tensor(name, shape, dt))
        sem = lambda name: ctx.enter_context(nc.semaphore(name))
        HGS = NG // B

        wo = sb("w_out_rows", [P, HGS, C])
        gw_a, gw_b = sb("gate_w_a", [P, E + 1]), sb("gate_w_b", [CB, E + 1])
        gb = sb("gate_b_rows", [P, E + 1])
        heads = sb("heads", [P, HGS, CW])
        stats, mv = sb("ln2_stats", [P, CT, 6]), sb("ln2_mean_var", [P, CT, 2])
        ve, sd, rstd = sb("ln2_var_eps", [P, CT]), sb("ln2_sd", [P, CT]), sb("ln2_rstd", [P, CT])
        x2 = sb("x2", [P, CT, C])
        xa, xb = sb("x2_t_a", [P, CW]), sb("x2_t_b", [CB, CW])
        zeros = sb("zero_rows", [P, C])

        ps_o = [ps(f"ps_o{k}", [P, 2 * C]) for k in range(2)]
        ps_ta, ps_tb = ps("ps2_ta", [P, CW]), ps("ps2_tb", [CB, CW])
        ps_l = ps("ps_logits", [P, CT * (E + 1)])

        loaded, weights_in = sem("c_loaded"), sem("c_weights_in")
        zeroed, zeros_made, sums_zeroed = sem("c_zeroed"), sem("c_zeros_made"), sem("c_sums_zeroed")
        heads_ready, mixed_out = sem("c_heads_ready"), sem("c_mixed_out")
        chained, var_ready, sd_ready = sem("c_chain"), sem("c_var_ready"), sem("c_sd_ready")
        x2_ready, turned, xt_ready = sem("c_x2_ready"), sem("c_turned"), sem("c_xt_ready")
        gated, gate_read, x2_stored = sem("c_gated"), sem("c_gate_read"), sem("c_x2_stored")

        with nc.Block() as block:

            @block.sync
            def _(sp):
                sp.wait_ge(zeroed, 1)
                for h in range(HG):
                    sp.dma_start(wo[32 * h:32 * h + D],
                                 w_out.rearrange("(a h r) n -> h r a n", h=HG, r=D)[h]).then_inc(loaded, 16)
                sp.dma_start(gw_a[:], gate_rows[0:P]).then_inc(loaded, 16)
                sp.dma_start(gw_b[:], gate_rows[P:C]).then_inc(loaded, 16)
                sp.dma_start(gb[:], gate_bias.to_broadcast([P, E + 1])).then_inc(loaded, 16)
                sp.dma_start(g.b2[:].rearrange("p e n -> p (e n)"), b2_rows.to_broadcast([P, E * C])).then_inc(weights_in, 16)
                sp.dma_start(g.w1_a[:], w1[:, 0:P, :].rearrange("e k f -> k e f")).then_inc(weights_in, 16)
                sp.dma_start(g.w1_b[0:CB], w1[:, P:C, :].rearrange("e k f -> k e f")).then_inc(weights_in, 16)
                sp.dma_start(g.w1_b[CB:CB + 1], b1.rearrange("(a e) f -> a e f", a=1)).then_inc(weights_in, 16)
                for e in range(E):
                    sp.dma_start(g.w2[:, e], w2[e].rearrange("(j k) n -> k j n", k=P)).then_inc(weights_in, 16)
                sp.wait_ge(zeros_made, 1)
                sp.dma_start(g.sums[0:N].rearrange("(t p) n -> p t n", p=P),
                             zeros[:].unsqueeze(1).to_broadcast([P, NT, C])).then_inc(sums_zeroed, 16)
                sp.dma_start(g.sums[N:N + P], zeros[:]).then_inc(sums_zeroed, 16)
                sp.dma_start(g.x2_rows[N:N + P], zeros[:]).then_inc(sums_zeroed, 16)
                with sp.Fori(0, NCH) as i:
                    sp.wait_ge(x2_ready, i + 1)
                    sp.dma_start(g.x2_rows[ds(i * CW, CW)].rearrange("(t p) n -> p t n", p=P), x2[:]).then_inc(x2_stored, 16)
                    hold(sp, x2_stored, 16 * i + 16)
                sp.wait_ge(sums_zeroed, 48)
                sp.wait_ge(weights_in, 16 * (4 + E))

            @block.gpsimd
            def _(pool):
                pool.memset(wo[:], 0.0).then_inc(zeroed, 1)
                pool.memset(zeros[:], 0.0).then_inc(zeros_made, 1)

            @block.scalar
            def _(act):
                with act.Fori(0, NCH) as i:
                    act.wait_ge(mixed_out, i)
                    nc.scalar.activation(heads[:], g.mixed[:, ds((i // QC) * HGS, HGS), ds((i % QC) * CW, CW)],
                                         ACT.Copy).then_inc(heads_ready, 1)
                    act.wait_ge(var_ready, i + 1)
                    nc.scalar.activation(sd[:], ve[:], ACT.Sqrt).then_inc(sd_ready, 1)
                    act.wait_ge(turned, i + 1)
                    act.wait_ge(gated, i)
                    nc.scalar.activation(xa[:], ps_ta[:], ACT.Copy).then_inc(xt_ready, 1)
                    nc.scalar.activation(xb[:], ps_tb[:], ACT.Copy).then_inc(xt_ready, 1)

            @block.tensor
            def _(pe):
                pe.wait_ge(loaded, 16 * 7)
                with pe.Fori(0, NCH) as i:
                    pe.wait_ge(heads_ready, i + 1)
                    pe.wait_ge(x2_ready, i)
                    for j in range(CT):
                        for a in range(HGS):
                            last = nc.tensor.matmul(ps_o[j // 2][:, (j % 2) * C:(j % 2 + 1) * C],
                                                    heads[:, a, j * P:(j + 1) * P], wo[:, a, :],
                                                    start=(a == 0), stop=(a == HGS - 1))
                    last.then_inc(mixed_out, 1)
                    pe.wait_ge(x2_ready, i + 1)
                    for j in range(CT):
                        nc.tensor.transpose(ps_ta[:, j * P:(j + 1) * P], x2[:, j, 0:P], g.ident[:])
                        last = nc.tensor.transpose(ps_tb[:, j * P:(j + 1) * P], x2[:, j, P:C], g.ident[:])
                    last.then_inc(turned, 1)
                    pe.wait_ge(xt_ready, 2 * i + 2)
                    pe.wait_ge(gate_read, i)
                    for j in range(CT):
                        dst = ps_l[:, j * (E + 1):(j + 1) * (E + 1)]
                        nc.tensor.matmul(dst, xa[:, j * P:(j + 1) * P], gw_a[:], start=True, stop=False)
                        last = nc.tensor.matmul(dst, xb[:, j * P:(j + 1) * P], gw_b[:], start=False, stop=True)
                    last.then_inc(gated, 1)

            @block.vector
            def _(dve):
                per_turn = 2 + 2 * CT + 1 + CT - 1
                with dve.Fori(0, NCH) as i:
                    chain = Tally(chained, i * per_turn)
                    dve.wait_ge(mixed_out, i + 1)
                    for k in range(2):
                        hk = g.h[:, ds(CT * i + 2 * k, 2), :]
                        n = chain.add(nc.vector.tensor_tensor(hk, ps_o[k][:].rearrange("p (j n) -> p j n", j=2), hk, ALU.add))
                    hold(dve, chain.sem, n)
                    for j in range(CT):
                        n = chain.add(nc.vector.bn_stats(stats[:, j, :], g.h[:, ds(CT * i + j, 1), :]
                                                         .rearrange("p a n -> p (a n)")))
                    hold(dve, chain.sem, n)
                    for j in range(CT):
                        n = chain.add(nc.vector.bn_aggr(mv[:, j, :], stats[:, j, :]))
                    dve.wait_ge(chain.sem, n)
                    nc.vector.tensor_scalar_add(ve[:], mv[:, :, 1], EPS).then_inc(var_ready, 1)
                    dve.wait_ge(sd_ready, i + 1)
                    n = chain.add(nc.vector.reciprocal(rstd[:], sd[:]))
                    dve.wait_ge(chain.sem, n)
                    dve.wait_ge(turned, i)
                    dve.wait_ge(x2_stored, 16 * i)
                    for j in range(CT):
                        ins = nc.vector.tensor_scalar(x2[:, j, :], g.h[:, ds(CT * i + j, 1), :]
                                                      .rearrange("p a n -> p (a n)"),
                                                      mv[:, j, 0:1], rstd[:, j:j + 1], ALU.subtract, ALU.mult)
                        if j < CT - 1:
                            chain.add(ins)
                        else:
                            ins.then_inc(x2_ready, 1)
                    assert chain.n == per_turn
                    dve.wait_ge(gated, i + 1)
                    dve.wait_ge(loaded, 16 * 7)
                    nc.vector.tensor_tensor(g.logits[:, ds(CT * i, CT), :],
                                            ps_l[:].rearrange("p (j n) -> p j n", j=CT),
                                            gb[:].unsqueeze(1).to_broadcast([P, CT, E + 1]), ALU.add).then_inc(gate_read, 1)


class Chain:

    def __init__(self, eng, sem):
        self.eng, self.sem, self.n = eng, sem, 0

    def step(self, ins):
        ins.then_inc(self.sem, 1)
        self.n += 1
        self.eng.wait_ge(self.sem, self.n)


def route(nc, g):
    with ExitStack() as ctx:
        sb = lambda name, shape, dt=F32: ctx.enter_context(nc.sbuf_tensor(name, shape, dt))
        ps = lambda name, shape, dt=F32: ctx.enter_context(nc.psum_tensor(name, shape, dt))
        sem = lambda name: ctx.enter_context(nc.semaphore(name))

        sh = [P, NT, E]
        ex, pr, eq, sc = sb("r_ex", sh), sb("r_prob", sh), sb("r_eq", sh), sb("r_score", sh)
        pick = [sb(f"r_pick{k}", sh) for k in range(2)]
        top = [sb(f"r_top{k}", [P, NT]) for k in range(2)]
        m = sb("r_max", [P, NT])
        first = sb("r_first", [P, NT])
        prefer = sb("r_prefer", [P, E])
        by_expert = sb("r_by_expert", [P, E, NT])
        before = sb("r_before", [P, P])
        ones = sb("r_ones", [P, P])
        go_on = sb("r_go_on", [P, E, NT])
        total = sb("r_total", [P, E, NT])
        upto = sb("r_upto", [P, E, NT])
        slot = sb("r_slot", [P, E, NT])
        tiles_f, tiles_i = sb("r_tiles_f", [P, E]), sb("r_tiles_i", [P, E], I32)
        tiles_end, tiles_start = sb("r_tiles_end", [P, E]), sb("r_tiles_start", [P, E])
        dest_f = sb("r_dest_f", [P, 2, NT])
        dest_i = sb("r_dest_i", [P, 2, NT], I32)
        part_i = sb("r_dest_part_i", [P, 2, NT], I32)
        lane, tile = sb("r_lane", [P, 2, NT]), sb("r_tile", [P, 2, NT])
        ids1 = sb("r_token_plus1", [P, NT])
        iota = sb("r_iota", [P, P])
        dummy = sb("r_dummy", [P, 1])
        hot = [sb(f"r_hot{k}", [P, P]) for k in range(2)]
        what = [sb(f"r_what{k}", [P, 2, ET]) for k in range(2)]
        over = sb("r_over", [P, ET, E])
        eid_f = sb("r_eid_f", [P, ET])
        idf, unused = sb("r_id_f", [P, ET]), sb("r_unused", [P, ET])
        ps_rank, ps_total = ps("ps_rank", [P, E * NT]), ps("ps_total", [P, E * NT])
        ps_slots = ps("ps_slots", [P, 2 * ET])

        const, v_chain, v_const = sem("r_const"), sem("r_chain"), sem("r_v_const")
        shifted, exped = sem("r_shifted"), sem("r_exped")
        picked, ranked = sem("r_picked"), sem("r_ranked")
        hot_ready = sem("r_hot_ready")
        hot_slots = sem("r_hot_slots")

        with nc.Block() as block:

            @block.gpsimd
            def _(pool):
                pool.iota(iota[:], [[1, P]], base=0, channel_multiplier=0,
                          allow_small_or_imprecise_dtypes=True).then_inc(const, 1)
                pool.iota(prefer[:], [[-1, E]], base=E, channel_multiplier=0,
                          allow_small_or_imprecise_dtypes=True).then_inc(const, 1)
                pool.iota(ids1[:], [[P, NT]], base=1, channel_multiplier=1,
                          allow_small_or_imprecise_dtypes=True).then_inc(const, 1)
                pool.iota(dummy[:], [[1, 1]], base=N + 1, channel_multiplier=1,
                          allow_small_or_imprecise_dtypes=True).then_inc(const, 1)
                pool.memset(before[:], 1.0).then_inc(const, 1)
                pool.memset(ones[:], 1.0).then_inc(const, 1)
                pool.memset(go_on[:], 1.0).then_inc(const, 1)
                pool.wait_ge(const, 7)
                pool.affine_select(out=before[:], in_=before[:], compare_op=ALU.is_gt, fill=0.0, base=0,
                                   pattern=[[1, P]], channel_multiplier=-1).then_inc(const, 1)
                pool.memset(go_on[:, :, 0:1], 0.0).then_inc(const, 1)

            @block.scalar
            def _(act):
                act.wait_ge(shifted, 1)
                nc.scalar.activation(ex[:], pr[:], ACT.Exp).then_inc(exped, 1)

            @block.tensor
            def _(pe):
                pe.wait_ge(const, 9)
                pe.wait_ge(picked, 1)
                mask = by_expert[:].rearrange("p e t -> p (e t)")
                nc.tensor.matmul(ps_rank[:], before[:], mask, start=True, stop=True)
                nc.tensor.matmul(ps_total[:], ones[:], mask, start=True, stop=True).then_inc(ranked, 1)

                def place(t, first=False, last=False):
                    for k in range(2):
                        pe.wait_ge(hot_ready, 2 * t + k + 1)
                        nc.tensor.matmul(ps_slots[:], hot[k][:], what[k][:].rearrange("p a j -> p (a j)"),
                                         start=(first and k == 0), stop=(last and k == 1)).then_inc(hot_slots, 1)

                place(0, first=True)
                with pe.Fori(1, NT - 1) as t:
                    place(t)
                place(NT - 1, last=True)

            @block.vector
            def _(dve):
                v = nc.vector
                c = Chain(dve, v_chain)
                wide = lambda a: a.unsqueeze(2).to_broadcast(sh)
                lg = g.logits[:, :, 0:E]
                c.step(v.tensor_reduce(m[:], lg, AX.X, ALU.max))
                v.tensor_tensor(pr[:], lg, wide(m[:]), ALU.subtract).then_inc(shifted, 1)
                dve.wait_ge(exped, 1)
                c.step(v.tensor_reduce(m[:], ex[:], AX.X, ALU.add))
                c.step(v.reciprocal(first[:], m[:]))
                c.step(v.tensor_tensor(pr[:], ex[:], wide(first[:]), ALU.mult))
                dve.wait_ge(const, 9)
                for k in range(2):
                    c.step(v.tensor_reduce(top[k][:], pr[:], AX.X, ALU.max))
                    c.step(v.tensor_tensor(eq[:], pr[:], wide(top[k][:]), ALU.is_equal))
                    c.step(v.tensor_tensor(sc[:], eq[:], prefer[:].unsqueeze(1).to_broadcast(sh), ALU.mult))
                    c.step(v.tensor_reduce(first[:], sc[:], AX.X, ALU.max))
                    c.step(v.tensor_tensor(pick[k][:], sc[:], wide(first[:]), ALU.is_equal))
                    if k == 0:
                        c.step(v.scalar_tensor_tensor(out=pr[:], in0=pick[0][:], scalar=-2.0, in1=pr[:],
                                                      op0=ALU.mult, op1=ALU.add))
                v.tensor_tensor(by_expert[:].rearrange("p e t -> p t e"), pick[0][:], pick[1][:],
                                ALU.add).then_inc(picked, 1)
                c.step(v.tensor_tensor(m[:], top[0][:], top[1][:], ALU.add))
                c.step(v.reciprocal(first[:], m[:]))
                c.step(v.tensor_tensor(top[0][:], top[0][:], first[:], ALU.mult))
                c.step(v.tensor_tensor(top[1][:], top[1][:], first[:], ALU.mult))
                dve.wait_ge(ranked, 1)
                flat = lambda a: a.rearrange("p e t -> p (e t)")
                c.step(v.tensor_copy(flat(total[:]), ps_total[:]))
                c.step(v.tensor_tensor_scan(flat(upto[:]), flat(go_on[:]), flat(total[:]), 0.0, ALU.mult, ALU.add))
                c.step(v.tensor_scalar(tiles_i[:], upto[:, :, NT - 1], float(P - 1), None, ALU.add))
                c.step(v.tensor_scalar(tiles_i[:], tiles_i[:], 7, None, ALU.arith_shift_right))
                c.step(v.tensor_copy(tiles_f[:], tiles_i[:]))
                c.step(v.tensor_tensor_scan(tiles_end[:], ones[:, 0:E], tiles_f[:], 0.0, ALU.mult, ALU.add))
                c.step(v.tensor_tensor(tiles_start[:], tiles_end[:], tiles_f[:], ALU.subtract))
                c.step(v.tensor_tensor(slot[:], upto[:], total[:], ALU.subtract))
                c.step(v.tensor_tensor(flat(slot[:]), flat(slot[:]), ps_rank[:], ALU.add))
                c.step(v.scalar_tensor_tensor(out=slot[:], in0=tiles_start[:].unsqueeze(2).to_broadcast([P, E, NT]),
                                              scalar=float(P), in1=slot[:], op0=ALU.mult, op1=ALU.add))
                for k in range(2):
                    c.step(v.tensor_tensor(eq[:], pick[k][:], slot[:].rearrange("p e t -> p t e"), ALU.mult))
                    c.step(v.tensor_reduce(dest_f[:, k, :], eq[:], AX.X, ALU.add))
                c.step(v.tensor_copy(dest_i[:], dest_f[:]))
                c.step(v.tensor_scalar(part_i[:], dest_i[:], 7, None, ALU.arith_shift_right))
                c.step(v.tensor_copy(tile[:], part_i[:]))
                c.step(v.tensor_scalar(part_i[:], dest_i[:], P - 1, None, ALU.bitwise_and))
                c.step(v.tensor_copy(lane[:], part_i[:]))
                c.step(v.tensor_tensor(over[:], iota[:, 0:ET].unsqueeze(2).to_broadcast([P, ET, E]),
                                       tiles_end[:].unsqueeze(1).to_broadcast([P, ET, E]), ALU.is_ge))
                c.step(v.tensor_reduce(eid_f[:], over[:], AX.X, ALU.add))
                c.step(v.tensor_scalar(g.expert_of[:], eid_f[:], float(E - 1), None, ALU.min))
                dve.sem_inc(hot_slots, 2)
                with dve.Fori(0, NT) as t:
                    for k in range(2):
                        dve.wait_ge(hot_slots, 2 * t + k + 1)
                        at = tile[:, k, ds(t, 1)]
                        v.tensor_scalar(hot[k][:], iota[:], lane[:, k, ds(t, 1)], None, ALU.is_equal)
                        v.tensor_scalar(what[k][:, 0, :], iota[:, 0:ET], at, ids1[:, ds(t, 1)], ALU.is_equal, ALU.mult)
                        v.tensor_scalar(what[k][:, 1, :], iota[:, 0:ET], at, top[k][:, ds(t, 1)],
                                        ALU.is_equal, ALU.mult).then_inc(hot_ready, 1)
                dve.wait_ge(hot_slots, 2 + 2 * NT)
                c.step(v.tensor_copy(idf[:], ps_slots[:, 0:ET]))
                c.step(v.tensor_copy(g.slot_weight[:], ps_slots[:, ET:2 * ET]))
                c.step(v.tensor_scalar(unused[:], idf[:], 0.0, dummy[:, 0:1], ALU.is_equal, ALU.mult))
                c.step(v.tensor_tensor(idf[:], idf[:], unused[:], ALU.add))
                c.step(v.tensor_scalar(g.slot_token[:], idf[:], -1.0, None, ALU.add))


def experts(nc, g):
    with ExitStack() as ctx:
        sb = lambda name, shape, dt=F32: ctx.enter_context(nc.sbuf_tensor(name, shape, dt))
        ps = lambda name, shape, dt=F32: ctx.enter_context(nc.psum_tensor(name, shape, dt))
        sem = lambda name: ctx.enter_context(nc.semaphore(name))
        FT = F // P

        ids_in, ids_out = sb("e_ids_gather", [P, 1], I32), sb("e_ids_scatter", [P, 1], I32)
        xg = sb("e_x", [P, C])
        xa, xb = sb("e_x_t_a", [P, P]), sb("e_x_t_b", [CB + 1, P])
        hid, hid_t = sb("e_hidden", [P, F]), sb("e_hidden_t", [P, F])
        y = sb("e_y", [P, C])
        yw = sb("e_y_weighted", [P, C])
        ps_x = ps("ps_x", [P, 2 * P])
        ps_h = ps("ps_h", [P, 1024])
        ps_ht = ps("ps_ht", [P, 1024])
        ps_y = ps("ps_y", [P, C])

        ones_made = sem("e_ones")
        id1, id2 = sem("e_ids_gather_ready"), sem("e_ids_scatter_ready")
        gathered, x_turned, xt_ready = sem("e_gathered"), sem("e_x_turned"), sem("e_xt_ready")
        hidden, gelu_done, h_turned, ht_ready = sem("e_hidden_done"), sem("e_gelu"), sem("e_h_turned"), sem("e_ht_ready")
        y_done, y_ready, yw_ready, added = sem("e_y_done"), sem("e_y_ready"), sem("e_yw_ready"), sem("e_added")

        with nc.Block() as block:

            @block.gpsimd
            def _(pool):
                pool.memset(xb[CB:CB + 1, :], 1.0).then_inc(ones_made, 1)
                pool.wait_ge(ones_made, 1)

                def gather(j):
                    pool.wait_ge(x_turned, j)
                    pool.tensor_copy(ids_in[:], g.slot_token[:, ds(j, 1)]).then_inc(id1, 1)
                    hold(pool, id1, j + 1)
                    pool.indirect_dma_start(out=xg[:], out_offset=None, in_=g.x2_rows[:],
                                            in_offset=bass.IndirectOffsetOnAxis(ap=ids_in[:, 0:1], axis=0)
                                            ).then_inc(gathered, 16)

                def add(j):
                    pool.wait_ge(added, 16 * j)
                    pool.tensor_copy(ids_out[:], g.slot_token[:, ds(j, 1)]).then_inc(id2, 1)
                    pool.wait_ge(id2, j + 1)
                    hold(pool, yw_ready, j + 1)
                    pool.indirect_dma_start(out=g.sums[:], in_=yw[:], in_offset=None,
                                            out_offset=bass.IndirectOffsetOnAxis(ap=ids_out[:, 0:1], axis=0),
                                            compute_op=ALU.add).then_inc(added, 16)

                gather(0)
                gather(1)
                with pool.Fori(0, ET - 2) as j:
                    gather(j + 2)
                    add(j)
                add(ET - 2)
                add(ET - 1)
                pool.wait_ge(added, 16 * ET)

            @block.tensor
            def _(pe):
                def turn_x(j):
                    pe.wait_ge(gathered, 16 * j + 16)
                    pe.wait_ge(xt_ready, 2 * j)
                    nc.tensor.transpose(ps_x[:, 0:P], xg[:, 0:P], g.ident[:])
                    nc.tensor.transpose(ps_x[0:CB, P:2 * P], xg[:, P:C], g.ident[:]).then_inc(x_turned, 1)

                def up(j, e):
                    pe.wait_ge(xt_ready, 2 * j + 2)
                    pe.wait_ge(gelu_done, j)
                    for c0, c1 in ((0, 512), (512, F)):
                        nc.tensor.matmul(ps_h[:, c0:c1], xa[:], g.w1_a[:, ds(e, 1), c0:c1].rearrange("p a n -> p (a n)"),
                                         start=True, stop=False)
                        last = nc.tensor.matmul(ps_h[:, c0:c1], xb[:],
                                                g.w1_b[:, ds(e, 1), c0:c1].rearrange("p a n -> p (a n)"),
                                                start=False, stop=True)
                    last.then_inc(hidden, 1)

                def turn_h(j):
                    pe.wait_ge(gelu_done, j + 1)
                    pe.wait_ge(ht_ready, j)
                    for k in range(FT):
                        last = nc.tensor.transpose(ps_ht[:, k * P:(k + 1) * P], hid[:, k * P:(k + 1) * P], g.ident[:])
                    last.then_inc(h_turned, 1)

                def down(j, e):
                    pe.wait_ge(ht_ready, j + 1)
                    pe.wait_ge(y_ready, j)
                    for k in range(FT):
                        last = nc.tensor.matmul(ps_y[:], hid_t[:, k * P:(k + 1) * P],
                                                g.w2[:, ds(e, 1), k, :].rearrange("p a n -> p (a n)"),
                                                start=(k == 0), stop=(k == FT - 1))
                    last.then_inc(y_done, 1)

                expert = lambda j: pe.value_load(g.expert_of[0:1, ds(j, 1)], min_val=0, max_val=E - 1)
                pe.wait_ge(ones_made, 1)
                turn_x(0)
                up(0, expert(0))
                turn_x(1)
                turn_h(0)
                with pe.Fori(1, ET - 1) as j:
                    up(j, expert(j))
                    turn_x(j + 1)
                    down(j - 1, expert(j - 1))
                    turn_h(j)
                up(ET - 1, expert(ET - 1))
                down(ET - 2, expert(ET - 2))
                turn_h(ET - 1)
                down(ET - 1, expert(ET - 1))

            @block.scalar
            def _(act):
                def copy_x(j):
                    act.wait_ge(x_turned, j + 1)
                    act.wait_ge(hidden, j)
                    nc.scalar.activation(xa[:], ps_x[:, 0:P], ACT.Copy).then_inc(xt_ready, 1)
                    nc.scalar.activation(xb[0:CB, :], ps_x[0:CB, P:2 * P], ACT.Copy).then_inc(xt_ready, 1)

                def gelu(j):
                    act.wait_ge(hidden, j + 1)
                    act.wait_ge(h_turned, j)
                    nc.scalar.activation(hid[:], ps_h[:, 0:F], ACT.Gelu_apprx_tanh).then_inc(gelu_done, 1)

                copy_x(0)
                with act.Fori(0, ET - 1) as j:
                    gelu(j)
                    copy_x(j + 1)
                gelu(ET - 1)

            @block.vector
            def _(dve):
                with dve.Fori(0, ET) as j:
                    dve.wait_ge(h_turned, j + 1)
                    dve.wait_ge(y_done, j)
                    nc.vector.tensor_copy(hid_t[:], ps_ht[:, 0:F]).then_inc(ht_ready, 1)
                    e = dve.value_load(g.expert_of[0:1, ds(j, 1)], min_val=0, max_val=E - 1)
                    dve.wait_ge(y_done, j + 1)
                    dve.wait_ge(yw_ready, j)
                    nc.vector.tensor_tensor(y[:], ps_y[:], g.b2[:, ds(e, 1), :].rearrange("p a n -> p (a n)"),
                                            ALU.add).then_inc(y_ready, 1)
                    dve.wait_ge(y_ready, j + 1)
                    dve.wait_ge(added, 16 * j)
                    nc.vector.tensor_scalar(yw[:], y[:], g.slot_weight[:, ds(j, 1)], None, ALU.mult).then_inc(yw_ready, 1)


def spectral(nc, g, out_rows):
    with ExitStack() as ctx:
        sb = lambda name, shape, dt=F32: ctx.enter_context(nc.sbuf_tensor(name, shape, dt))
        ps = lambda name, shape, dt=F32: ctx.enter_context(nc.psum_tensor(name, shape, dt))
        sem = lambda name: ctx.enter_context(nc.semaphore(name))
        L = 2 * B
        HI = 32 + B

        a = sb("s_a", [P, L, TB])
        y = sb("s_y", [P, TB + 2, 2, 2, L])
        t = sb("s_t", [P, 2, 2, L])
        flip = sb("s_flip", [P, P])
        mats = sb("s_mats", [HI, P, 3, 5])
        w = sb("s_w", [HI, 2])
        num, nd = sb("s_num", [HI, 5]), sb("s_nd", [HI, 5])
        sq, norm, rnorm = sb("s_sq", [HI, 2]), sb("s_norm", [HI, 1]), sb("s_rnorm", [HI, 1])
        carry = sb("s_carry", [HI, 2, P])
        back = sb("s_back", [P, 2, B])
        win = sb("s_w_in", [P, 2, L])
        d = sb("s_d", [P, 2, TB, L])
        sqw, qw = sb("s_sq_wide", [P, 2, L]), sb("s_q_wide", [P, L])
        z = sb("s_z", [P, 2, B, TB])
        z2, zn = sb("s_z_sq", [P, 2, B, TB]), sb("s_z_norm", [P, B, TB])
        rows = sb("s_rows", [P, 4, C])
        rows_s = sb("s_rows_scaled", [P, 3, C])
        ps_m = ps("ps_mats", [HI, 1024])
        ps_w, ps_wb = ps("ps_carry", [P, 2, B]), ps("ps_carry_back", [P, 2, B])
        ps_f = ps("ps_flip", [P, 2 * B])

        const, loaded = sem("s_const"), sem("s_loaded")
        chained = sem("s_chain")
        maps_made, maps_turned, carried, carry_back, back_read, flipped = (
            sem("s_maps_made"), sem("s_maps_turned"), sem("s_carried"), sem("s_carry_back"), sem("s_back_read"),
            sem("s_flipped"))
        finished = sem("s_finished")

        with nc.Block() as block:

            @block.sync
            def _(sp):
                sp.dma_start(rows[:].rearrange("p a n -> p (a n)"), out_rows.to_broadcast([P, 4 * C])).then_inc(loaded, 16)

            @block.gpsimd
            def _(pool):
                pool.memset(flip[:], 0.0).then_inc(const, 1)
                pool.wait_ge(const, 1)
                pool.affine_select(out=flip[:], in_=flip[:], compare_op=ALU.not_equal, fill=1.0, base=-(P - 1),
                                   pattern=[[1, P]], channel_multiplier=1).then_inc(const, 1)

            @block.tensor
            def _(pe):
                pe.wait_ge(const, 2)
                pe.wait_ge(maps_made, 1)
                for s in range(2):
                    for col in range(2):
                        for ri in range(2):
                            q = (s * 2 + col) * 2 + ri
                            src = y[:, TB + s, ri, col, :]
                            nc.tensor.matmul(ps_m[0:B, q * P:(q + 1) * P], src[:, 0:B], g.ident[:], start=True, stop=True)
                            last = nc.tensor.matmul(ps_m[32:32 + B, q * P:(q + 1) * P], src[:, B:L], flip[:], start=True, stop=True)
                last.then_inc(maps_turned, 1)
                pe.wait_ge(carried, 1)
                for ri in range(2):
                    nc.tensor.matmul(ps_w[:, ri, :], carry[0:B, ri, :], g.ident[0:B, 0:B], start=True, stop=True)
                    last = nc.tensor.matmul(ps_wb[:, ri, :], carry[32:32 + B, ri, :], g.ident[32:32 + B, 32:32 + B], start=True, stop=True)
                last.then_inc(carry_back, 1)
                pe.wait_ge(back_read, 1)
                nc.tensor.matmul(ps_f[:], flip[:], back[:].rearrange("p r b -> p (r b)"), start=True, stop=True).then_inc(flipped, 1)

            @block.vector
            def _(dve):
                v = nc.vector
                c = Chain(dve, chained)
                logit = g.logits[:, :, E].rearrange("p (b c) -> p b c", b=B)
                for lanes, src in ((a[:, 0:B, :], logit), (a[:, B:L, :], logit[:, :, ::-1])):
                    c.step(v.tensor_scalar(lanes, src, V_MAX, -V_MAX, ALU.min, ALU.max))
                c.step(v.tensor_scalar(a[:], a[:], -2.0, None, ALU.add))
                c.step(v.memset(y[:, 0:2], 0.0))
                c.step(v.memset(y[:, 0, 0, 1, :], 1.0))
                c.step(v.memset(y[:, 1, 0, 0, :], 1.0))
                for s in range(TB):
                    rows_of = lambda k: y[:, k].rearrange("p r c l -> p (r c) l")
                    c.step(v.tensor_tensor(t[:].rearrange("p r c l -> p (r c) l"), rows_of(s + 1),
                                           a[:, :, s].unsqueeze(1).to_broadcast([P, 4, L]), ALU.mult))
                    c.step(v.tensor_tensor(t[:], t[:], y[:, s], ALU.subtract))
                    c.step(v.tensor_tensor(y[:, s + 2, 0], t[:, 0], y[:, s + 1, 1], ALU.add))
                    ins = v.tensor_tensor(y[:, s + 2, 1], t[:, 1], y[:, s + 1, 0], ALU.subtract)
                    if s < TB - 1:
                        c.step(ins)
                    else:
                        ins.then_inc(maps_made, 1)
                c.step(v.memset(mats[:], 1.0))
                c.step(v.memset(w[:], 0.0))
                c.step(v.memset(num[:], 1.0))
                c.step(v.memset(nd[:], 1.0))
                c.step(v.memset(carry[:], 0.0))
                dve.wait_ge(maps_turned, 1)
                for p0 in (0, 32):
                    lane = slice(p0, p0 + B)
                    at = lambda s, col, ri: ps_m[lane, ((s * 2 + col) * 2 + ri) * P:((s * 2 + col) * 2 + ri + 1) * P]
                    for s, e0 in ((0, 0), (1, 3)):
                        for ri in range(2):
                            c.step(v.tensor_copy(mats[lane, :, 0, e0 + ri], at(s, 0, ri)))
                            c.step(v.tensor_copy(mats[lane, :, 1, e0 + ri], at(s, 1, ri)))
                        c.step(v.tensor_scalar(mats[lane, :, 2, e0], at(s, 1, 1), -1.0, None, ALU.mult))
                        c.step(v.tensor_copy(mats[lane, :, 2, e0 + 1], at(s, 1, 0)))
                    for k in range(3):
                        c.step(v.tensor_scalar(mats[lane, :, k, 2], mats[lane, :, k, 0], -1.0, None, ALU.mult))
                per_turn = 7
                base = c.n
                with dve.Fori(0, P - 1) as n:
                    chain = Tally(chained, base + n * per_turn)
                    of = lambda k: mats[:, ds(n, 1), k, :].rearrange("p a e -> p (a e)")
                    m = chain.add(v.scalar_tensor_tensor(out=num[:], in0=of(1), scalar=w[:, 0:1], in1=of(0), op0=ALU.mult, op1=ALU.add))
                    dve.wait_ge(chained, m)
                    m = chain.add(v.scalar_tensor_tensor(out=nd[:], in0=of(2), scalar=w[:, 1:2], in1=num[:], op0=ALU.mult, op1=ALU.add))
                    dve.wait_ge(chained, m)
                    m = chain.add(v.tensor_tensor_reduce(sq[:], nd[:, 3:5], nd[:, 3:5], 1.0, 0.0, ALU.mult, ALU.add, norm[:]))
                    dve.wait_ge(chained, m)
                    m = chain.add(v.reciprocal(rnorm[:], norm[:]))
                    dve.wait_ge(chained, m)
                    m = chain.add(v.tensor_tensor_reduce(sq[:], nd[:, 0:2], nd[:, 3:5], rnorm[:, 0:1], 0.0, ALU.mult, ALU.add, w[:, 0:1]))
                    dve.wait_ge(chained, m)
                    m = chain.add(v.tensor_tensor_reduce(sq[:], nd[:, 1:3], nd[:, 3:5], rnorm[:, 0:1], 0.0, ALU.mult, ALU.add, w[:, 1:2]))
                    dve.wait_ge(chained, m)
                    m = chain.add(v.tensor_copy(carry[:, :, ds(n + 1, 1)].rearrange("p r a -> p (r a)"), w[:]))
                    dve.wait_ge(chained, m)
                    assert chain.n == per_turn
                c.n = base + per_turn * (P - 1)
                v.memset(sq[:], 0.0).then_inc(carried, 1)
                dve.wait_ge(carry_back, 1)
                c.step(v.tensor_copy(win[:, :, 0:B], ps_w[:]))
                v.tensor_copy(back[:], ps_wb[:]).then_inc(back_read, 1)
                dve.wait_ge(flipped, 1)
                c.step(v.tensor_copy(win[:, :, B:L], ps_f[:].rearrange("p (r b) -> p r b", r=2)))
                for s in range(TB):
                    re, im = d[:, 0, s, :], d[:, 1, s, :]
                    c.step(v.tensor_tensor(re, a[:, :, s], win[:, 0, :], ALU.subtract))
                    c.step(v.tensor_scalar(im, win[:, 1, :], -1.0, -1.0, ALU.mult, ALU.add))
                    if s < TB - 1:
                        c.step(v.tensor_tensor(sqw[:], d[:, :, s, :], d[:, :, s, :], ALU.mult))
                        c.step(v.tensor_tensor(qw[:], sqw[:, 0, :], sqw[:, 1, :], ALU.add))
                        c.step(v.reciprocal(qw[:], qw[:]))
                        c.step(v.tensor_tensor(win[:, 0, :], re, qw[:], ALU.mult))
                        c.step(v.scalar_tensor_tensor(out=win[:, 1, :], in0=im, scalar=-1.0, in1=qw[:], op0=ALU.mult, op1=ALU.mult))
                for ri in range(2):
                    c.step(v.tensor_tensor(z[:, ri], d[:, ri, :, 0:B].rearrange("p s b -> p b s"),
                                           d[:, ri, ::-1, B:L].rearrange("p s b -> p b s"), ALU.add))
                c.step(v.tensor_tensor(z[:, 0], z[:, 0], a[:, 0:B, :], ALU.subtract))
                c.step(v.tensor_scalar(z[:, 1], z[:, 1], 1.0, None, ALU.add))
                c.step(v.tensor_tensor(z2[:], z[:], z[:], ALU.mult))
                c.step(v.tensor_tensor(zn[:], z2[:, 0], z2[:, 1], ALU.add))
                c.step(v.reciprocal(zn[:], zn[:]))
                c.step(v.tensor_tensor(z[:, 0], z[:, 0], zn[:], ALU.mult))
                c.step(v.scalar_tensor_tensor(out=z[:, 1], in0=z[:, 1], scalar=-1.0, in1=zn[:], op0=ALU.mult, op1=ALU.mult))
                c.step(v.tensor_scalar(z[:], z[:], FEAT_CLAMP, -FEAT_CLAMP, ALU.min, ALU.max))
                dve.wait_ge(loaded, 16)
                c.step(v.tensor_tensor(rows_s[:], rows[:, 0:3], rows[:, 3:4].to_broadcast([P, 3, C]), ALU.mult))
                c.step(v.tensor_tensor(g.h[:], g.h[:], rows_s[:, 2:3].to_broadcast([P, NT, C]), ALU.add))
                with dve.Fori(0, NT) as tt:
                    hr = g.h[:, ds(tt, 1), :].rearrange("p a n -> p (a n)")
                    zf = z[:].rearrange("p r b c -> p r (b c)")
                    v.scalar_tensor_tensor(out=hr, in0=rows_s[:, 0, :], scalar=zf[:, 0, ds(tt, 1)], in1=hr,
                                           op0=ALU.mult, op1=ALU.add).then_inc(finished, 1)
                    dve.wait_ge(finished, 2 * tt + 1)
                    v.scalar_tensor_tensor(out=hr, in0=rows_s[:, 1, :], scalar=zf[:, 1, ds(tt, 1)], in1=hr,
                                           op0=ALU.mult, op1=ALU.add).then_inc(finished, 1)
                    dve.wait_ge(finished, 2 * tt + 2)


def finish(nc, g, out):
    with ExitStack() as ctx:
        sem = lambda name: ctx.enter_context(nc.semaphore(name))
        part = ctx.enter_context(nc.sbuf_tensor("f_sums", [P, NCH, CT, C], F32))
        sums_in = [sem(f"f_sums_in{i}") for i in range(NCH)]
        done, stored = sem("f_done"), sem("f_stored")
        with nc.Block() as block:

            @block.sync
            def _(sp):
                for i in range(NCH):
                    sp.dma_start(part[:, i], g.sums[i * CW:(i + 1) * CW].rearrange("(t p) n -> p t n", p=P)).then_inc(sums_in[i], 16)
                for i in range(NCH):
                    b, c0 = i // QC, (i % QC) * CT
                    sp.wait_ge(done, i + 1)
                    sp.dma_start(out[b].rearrange("(p c) n -> p c n", c=TB)[:, c0:c0 + CT, :],
                                 g.h[:, i * CT:(i + 1) * CT, :]).then_inc(stored, 16)
                sp.wait_ge(stored, 16 * NCH)

            @block.vector
            def _(dve):
                for i in range(NCH):
                    dve.wait_ge(sums_in[i], 16)
                    hc = g.h[:, i * CT:(i + 1) * CT, :]
                    nc.vector.tensor_tensor(hc, hc, part[:, i], ALU.add).then_inc(done, 1)


def build(nc, x, tok_table, pos_rev, pos_rev_t, carry_t, w_qkv, w_out, gate_rows, gate_bias, w1, b1, w2, b2_rows,
          out_rows, out):
    g = Chip()
    g.qk_parts = nc.dram_tensor("qk_parts", [3, 2 * C, N], BF16)
    g.x2_rows = nc.dram_tensor("x2_rows", [N + P, C], F32)
    g.sums = nc.dram_tensor("expert_sums", [N + P, C], F32)
    with ExitStack() as keep:
        sb = lambda ctx, name, shape, dt=F32: ctx.enter_context(nc.sbuf_tensor(name, shape, dt))
        g.ident = sb(keep, "ident", [P, P])
        g.h = sb(keep, "h", [P, NT, C])
        g.logits = sb(keep, "logits", [P, NT, E + 1])
        g.expert_of = sb(keep, "expert_of", [P, ET], I32)
        g.slot_token = sb(keep, "slot_token", [P, ET], I32)
        g.slot_weight = sb(keep, "slot_weight", [P, ET])
        g.mixed = sb(keep, "mixed_all", [P, NG, S])
        with ExitStack() as attn:
            g.spread = sb(attn, "spread", [P, P])
            g.v = sb(attn, "v_all", [P, NT, C])
            embed_and_project(nc, g, x, tok_table, pos_rev, pos_rev_t, carry_t, w_qkv)
            attention(nc, g)
        g.b2 = sb(keep, "b2_all", [P, E, C])
        g.w1_a, g.w1_b = sb(keep, "w1_a", [P, E, F]), sb(keep, "w1_b", [CB + 1, E, F])
        g.w2 = sb(keep, "w2_all", [P, E, F // P, C])
        mix_heads_and_gate(nc, g, w_out, gate_rows, gate_bias, w1, b1, w2, b2_rows)
        route(nc, g)
        spectral(nc, g, out_rows)
        experts(nc, g)
        finish(nc, g, out)


def kernel(**inputs):
    import numpy as _np
    import concourse.bacc as _bacc
    from concourse import mybir as _mybir
    from concourse.bass_utils import run_bass_kernel_spmd as _run

    I = {k: _np.asarray(v) for k, v in inputs.items()}
    pos = I["L0_tok_pos_table"][::-1]
    feeds = {
        "x": I["x"],
        "tok_table": I["L0_tok_tok_table"],
        "pos_rev": pos,
        "pos_rev_t": pos.T,
        "carry_t": I["L0_tok_carry_W"].T,
        "w_qkv": I["L0_attn_w_qkv"],
        "w_out": I["L0_attn_w_out"],
        "gate_rows": _np.concatenate([I["L0_ffn_gate_w"], I["L0_ffn_v_w"][:, None]], axis=1),
        "gate_bias": _np.concatenate([I["L0_ffn_gate_b"], I["L0_ffn_v_b"].reshape(1)])[None, :],
        "w1": I["L0_ffn_w1"],
        "b1": I["L0_ffn_b1"],
        "w2": I["L0_ffn_w2"],
        "b2_rows": I["L0_ffn_b2"].reshape(1, -1),
        "out_rows": _np.concatenate([I["L0_ffn_out_w"], I["L0_ffn_out_b"][None], I["L0_ffn_bk_scale"][None]]).reshape(1, -1),
    }
    nc = _bacc.Bacc("TRN2", target_bir_lowering=False, num_devices=1)
    arrays, args = {}, []
    for name, a in feeds.items():
        a = _np.ascontiguousarray(a)
        arrays[f"in_{name}_dram"] = a
        args.append(nc.dram_tensor(f"in_{name}_dram", a.shape, _mybir.dt.from_np(a.dtype), kind="ExternalInput").ap())
    args.append(nc.dram_tensor("out_0_dram", (B, S, C), _mybir.dt.from_np(_np.dtype("float32")), kind="ExternalOutput").ap())
    build(nc, *args)
    r = _run(nc, [arrays], core_ids=[0])
    return r.results[0]["out_0_dram"]
```

```python
import numpy as np

import concourse.bass as bass
from concourse import mybir
from contextlib import ExitStack

F32 = mybir.dt.float32
BF16 = mybir.dt.bfloat16
I32 = mybir.dt.int32
U32 = mybir.dt.uint32
ALU = mybir.AluOpType
ACT = mybir.ActivationFunctionType
AX = mybir.AxisListType

P = 128
B, S, C = 2, 2048, 192
H, D = 12, 16
E, F = 8, 768
N = B * S
CB = C - P
TB = S // P
NT = B * TB
CT = 4
CW = CT * P
NCH = N // CW
QC = S // CW
HG = 4
NG = B * (H // HG)
STEPS = NG * QC
KT = S // P
ET = (2 * N + E * (P - 1)) // P
EPS = 1e-5
SCALE = float(C) ** -0.5
V_MAX = 3.0
FEAT_CLAMP = 10.0

Q_PIECE = [0, 0, 0, 1, 1, 2]
K_PIECE = [0, 1, 2, 0, 1, 0]
KR = len(Q_PIECE) * D
MR = 3


class Tally:

    def __init__(self, sem, base=0):
        self.sem, self.base, self.n = sem, base, 0

    def add(self, ins, k=1):
        ins.then_inc(self.sem, k)
        self.n += k
        return self.base + self.n


def ds(start, n):
    return bass.ds(start, n)


def hold(eng, sem, value):
    eng.wait_ge(sem, value)
    eng.nop(nofuse=True)


class Chip:
    pass


def embed_and_project(nc, g, x, tok_table, pos_rev, pos_rev_t, carry_t, w_qkv):
    with ExitStack() as ctx:
        sb = lambda name, shape, dt=F32: ctx.enter_context(nc.sbuf_tensor(name, shape, dt))
        ps = lambda name, shape, dt=F32: ctx.enter_context(nc.psum_tensor(name, shape, dt))
        sem = lambda name: ctx.enter_context(nc.semaphore(name))

        idx = sb("token_ids", [P, B, TB], I32)
        wqk_a, wqk_b = sb("wqk_a", [P, 2 * C]), sb("wqk_b", [CB, 2 * C])
        ct_a, ct_b = sb("carry_a", [P, C]), sb("carry_b", [CB, C])
        prt_a, prt_b = sb("pos_t_a", [P, 16]), sb("pos_t_b", [CB, 16])
        prow = sb("pos_rows", [P, TB, C])
        zt_a, zt_b = sb("high_digit_a", [P, 8]), sb("high_digit_b", [CB, 8])
        yt_a, yt_b = sb("two_digits_a", [P, 8, 16]), sb("two_digits_b", [CB, 8, 16])
        pos = sb("pos_all", [P, TB, C])
        stats = sb("ln_stats", [P, CT, 6])
        mv = sb("ln_mean_var", [P, CT, 2])
        ve = sb("ln_var_eps", [P, CT])
        sd = sb("ln_sd", [P, CT])
        rstd = sb("ln_rstd", [P, CT])
        x1 = sb("x1", [P, 2, CT, C])
        xa, xb = sb("x1_t_a", [P, 2, CW]), sb("x1_t_b", [CB, 2, CW])
        parts = sb("qk_parts_sb", [P, 2, 3, 3, CW], BF16)
        rem = sb("qk_rem", [P, 3, CW])

        ps_ta, ps_tb = ps("ps_ta", [P, CW]), ps("ps_tb", [CB, CW])
        ps_qk = [ps(f"ps_qk{m}", [P, CW]) for m in range(3)]
        ps_v = [ps(f"ps_v{m}", [P, 2 * C]) for m in range(2)]

        loaded, pos_loaded = sem("a_loaded"), sem("a_pos_loaded")
        ids_in = sem("a_ids_in")
        gathered = [sem("a_gathered0"), sem("a_gathered1")]
        const_made = sem("a_const_made")
        pe_pos = sem("a_pe_pos")
        act_pos = sem("a_act_pos")
        v_chain = sem("a_v_chain")
        pos_ready = sem("a_pos_ready")
        pos_made = sem("a_pos_made")
        var_ready = sem("a_var_ready")
        sd_ready = sem("a_sd_ready")
        x1_ready = sem("a_x1_ready")
        turned = sem("a_turned")
        xt_ready = sem("a_xt_ready")
        projected = sem("a_projected")
        v_projected = sem("a_v_projected")
        piece1 = sem("a_piece1")
        rem1 = sem("a_rem1")
        piece2 = sem("a_piece2")
        piece3 = sem("a_piece3")
        v_copied = sem("a_v_copied")
        stored = sem("a_stored")

        with nc.Block() as block:

            @block.sync
            def _(sp):
                sp.dma_start(idx[:], x.rearrange("b (p c) -> p b c", c=TB)).then_inc(ids_in, 16)
                for dst, src in ((ct_a[:], carry_t[0:P]), (ct_b[:], carry_t[P:C]), (prt_a[:], pos_rev_t[0:P]),
                                 (prt_b[:], pos_rev_t[P:C])):
                    sp.dma_start(dst, src).then_inc(pos_loaded, 16)
                sp.dma_start(prow[:].rearrange("p c n -> p (c n)"),
                             pos_rev.rearrange("(a c) n -> a (c n)", a=1).to_broadcast([P, TB * C])).then_inc(loaded, 16)
                for dst, src in ((wqk_a[:], w_qkv[0:P, 0:2 * C]), (wqk_b[:], w_qkv[P:C, 0:2 * C])):
                    sp.dma_start(dst, src).then_inc(loaded, 16)
                with sp.Fori(0, NCH) as i:
                    for m in range(3):
                        sp.wait_ge(piece1, 3 * i + m + 1)
                        sp.wait_ge(piece2, 3 * i + m + 1)
                        sp.wait_ge(piece3, 3 * i + m + 1)
                        sp.dma_start(g.qk_parts[:, P * m:P * (m + 1), ds(i * CW, CW)].rearrange("t p n -> p t n"),
                                     parts[:, ds(i % 2, 1), m].rearrange("p a t n -> p (a t) n")).then_inc(stored, 16)
                    hold(sp, stored, 48 * i + 48)

            @block.gpsimd
            def _(pool):
                pool.memset(g.ident[:], 0.0).then_inc(const_made, 1)
                pool.memset(g.spread[:], 0.0).then_inc(const_made, 1)
                pool.wait_ge(const_made, 2)
                pool.affine_select(out=g.ident[:], in_=g.ident[:], compare_op=ALU.not_equal, fill=1.0, base=0,
                                   pattern=[[-1, P]], channel_multiplier=1).then_inc(const_made, 1)
                sel = g.spread[:].rearrange("p (h r) -> p h r", h=HG)
                pool.affine_select(out=sel, in_=sel, compare_op=ALU.not_equal, fill=1.0, base=-D,
                                   pattern=[[-32, HG], [0, 32]], channel_multiplier=1).then_inc(const_made, 1)
                pool.wait_ge(ids_in, 16)
                for i in range(NCH):
                    if i >= 2:
                        pool.wait_ge(gathered[i % 2], 16 * CT * (i // 2))
                    for t in range(CT * i, CT * (i + 1)):
                        pool.indirect_dma_start(
                            out=g.h[:, t, :], out_offset=None, in_=tok_table,
                            in_offset=bass.IndirectOffsetOnAxis(ap=idx[:, t // TB, t % TB:t % TB + 1], axis=0),
                        ).then_inc(gathered[i % 2], 16)

            @block.tensor
            def _(pe):
                pe.wait_ge(pos_loaded, 16 * 4)
                pe.wait_ge(const_made, 4)
                for dst, m0, m1 in ((ps_ta[:, 0:8], 0, P), (ps_tb[:, 0:8], P, C)):
                    nc.tensor.matmul(dst, ct_a[:, m0:m1], prt_a[:, 8:16], start=True, stop=False)
                    nc.tensor.matmul(dst, ct_b[:, m0:m1], prt_b[:, 8:16], start=False, stop=True).then_inc(pe_pos, 1)
                pe.wait_ge(pos_ready, 2)
                nc.tensor.matmul(ps_v[0][:, 0:C], yt_a[:].rearrange("p a r -> p (a r)"), ct_a[:], start=True, stop=False)
                nc.tensor.matmul(ps_v[0][:, 0:C], yt_b[:].rearrange("p a r -> p (a r)"), ct_b[:], start=False,
                                 stop=True).then_inc(pe_pos, 1)

                def turn_x(i, r):
                    pe.wait_ge(x1_ready, i + 1)
                    pe.wait_ge(xt_ready, 2 * i)
                    for j in range(CT):
                        nc.tensor.transpose(ps_ta[:, j * P:(j + 1) * P], x1[:, r, j, 0:P], g.ident[:])
                        last = nc.tensor.transpose(ps_tb[:, j * P:(j + 1) * P], x1[:, r, j, P:C], g.ident[:])
                    last.then_inc(turned, 1)

                def project(i, r, first=False, more=True):
                    pe.wait_ge(xt_ready, 2 * i + 2)
                    for m in range(3):
                        if not first:
                            pe.wait_ge(rem1, 3 * (i - 1) + m + 1)
                        nc.tensor.matmul(ps_qk[m][:], wqk_a[:, m * P:(m + 1) * P], xa[:, r], start=True, stop=False)
                        nc.tensor.matmul(ps_qk[m][:], wqk_b[:, m * P:(m + 1) * P], xb[:, r], start=False,
                                         stop=True).then_inc(projected, 1)
                    if more:
                        turn_x(i + 1, 1 - r)
                    pe.wait_ge(v_copied, 2 * i)
                    for j in range(CT):
                        dst = ps_v[j // 2][:, (j % 2) * C:(j % 2 + 1) * C]
                        nc.tensor.matmul(dst, xa[:, r, j * P:(j + 1) * P], wqk_a[:, C:2 * C], start=True, stop=False)
                        last = nc.tensor.matmul(dst, xb[:, r, j * P:(j + 1) * P], wqk_b[:, C:2 * C], start=False, stop=True)
                    last.then_inc(v_projected, 1)

                pe.wait_ge(loaded, 16 * 3)
                pe.wait_ge(pos_made, 1)
                turn_x(0, 0)
                project(0, 0, first=True)
                with pe.Fori(0, (NCH - 2) // 2) as k:
                    project(k * 2 + 1, 1)
                    project(k * 2 + 2, 0)
                project(NCH - 1, 1, more=False)

            @block.scalar
            def _(act):
                act.wait_ge(pe_pos, 1)
                nc.scalar.activation(zt_a[:], ps_ta[:, 0:8], ACT.Copy).then_inc(act_pos, 1)
                act.wait_ge(pe_pos, 2)
                nc.scalar.activation(zt_b[:], ps_tb[:, 0:8], ACT.Copy).then_inc(act_pos, 1)

                def root(i):
                    act.wait_ge(var_ready, i + 1)
                    nc.scalar.activation(sd[:], ve[:], ACT.Sqrt).then_inc(sd_ready, 1)

                def copy_x(i):
                    act.wait_ge(turned, i + 1)
                    if not isinstance(i, int):
                        act.wait_ge(v_projected, i - 1)
                    row = lambda a: a[:, ds(i % 2, 1), :].rearrange("p a n -> p (a n)")
                    nc.scalar.activation(row(xa), ps_ta[:], ACT.Copy).then_inc(xt_ready, 1)
                    nc.scalar.activation(row(xb), ps_tb[:], ACT.Copy).then_inc(xt_ready, 1)

                def chunk(i, first=False, more=True):
                    part = lambda m, n: parts[:, ds(i % 2, 1), m, n, :].rearrange("p a n -> p (a n)")
                    if more:
                        root(i + 1)
                    if not first:
                        act.wait_ge(stored, 48 * (i - 1))
                    for m in range(3):
                        act.wait_ge(projected, 3 * i + m + 1)
                        nc.scalar.activation(part(m, 0), ps_qk[m][:], ACT.Copy).then_inc(piece1, 1)
                    if more:
                        copy_x(i + 1)
                    for m in range(3):
                        act.wait_ge(rem1, 3 * i + m + 1)
                        nc.scalar.activation(part(m, 1), rem[:, m, :], ACT.Copy).then_inc(piece2, 1)
                    act.wait_ge(v_projected, i + 1)
                    for m in range(2):
                        nc.scalar.activation(g.v[:, ds(CT * i + 2 * m, 2), :],
                                             ps_v[m][:].rearrange("p (j n) -> p j n", j=2), ACT.Copy).then_inc(v_copied, 1)

                root(0)
                copy_x(0)
                chunk(0, first=True)
                with act.Fori(1, NCH - 1) as i:
                    chunk(i)
                chunk(NCH - 1, more=False)

            @block.vector
            def _(dve):
                for k, (dst, z, r, n) in enumerate(((yt_a, zt_a, prt_a, P), (yt_b, zt_b, prt_b, CB))):
                    dve.wait_ge(act_pos, k + 1)
                    dve.wait_ge(pos_loaded, 16 * 4)
                    nc.vector.tensor_tensor(dst[:], z[:].unsqueeze(2).to_broadcast([n, 8, 16]),
                                            r[:].unsqueeze(1).to_broadcast([n, 8, 16]), ALU.add).then_inc(pos_ready, 1)
                dve.wait_ge(pe_pos, 3)
                dve.wait_ge(loaded, 16 * 3)
                nc.vector.tensor_tensor(pos[:], ps_v[0][:, 0:C].unsqueeze(1).to_broadcast([P, TB, C]), prow[:],
                                        ALU.add).then_inc(pos_made, 1)
                dve.wait_ge(pos_made, 1)
                per_turn = 9 + CT

                def embed(i, r):
                    chain = Tally(v_chain, i * per_turn)
                    dve.wait_ge(gathered[r], (i - r) * 8 * CT + 16 * CT)
                    hc = g.h[:, ds(CT * i, CT), :]
                    n = chain.add(nc.vector.tensor_tensor(hc, hc, pos[:, ds((i % QC) * CT, CT), :], ALU.add))
                    hold(dve, chain.sem, n)
                    for j in range(CT):
                        n = chain.add(nc.vector.bn_stats(stats[:, j, :], g.h[:, ds(CT * i + j, 1), :]
                                                         .rearrange("p a n -> p (a n)")))
                    hold(dve, chain.sem, n)
                    for j in range(CT):
                        n = chain.add(nc.vector.bn_aggr(mv[:, j, :], stats[:, j, :]))
                    dve.wait_ge(chain.sem, n)
                    nc.vector.tensor_scalar_add(ve[:], mv[:, :, 1], EPS).then_inc(var_ready, 1)
                    dve.wait_ge(sd_ready, i + 1)
                    n = chain.add(nc.vector.reciprocal(rstd[:], sd[:]))
                    dve.wait_ge(chain.sem, n)
                    if not isinstance(i, int):
                        dve.wait_ge(turned, i - 1)
                    for j in range(CT):
                        ins = nc.vector.tensor_scalar(x1[:, r, j, :], g.h[:, ds(CT * i + j, 1), :]
                                                      .rearrange("p a n -> p (a n)"),
                                                      mv[:, j, 0:1], rstd[:, j:j + 1], ALU.subtract, ALU.mult)
                        if j < CT - 1:
                            chain.add(ins)
                        else:
                            ins.then_inc(x1_ready, 1)
                    assert chain.n == per_turn

                def cut(i, r):
                    dve.wait_ge(piece3, 3 * i)
                    for m in range(3):
                        dve.wait_ge(piece1, 3 * i + m + 1)
                        nc.vector.tensor_tensor(rem[:, m, :], ps_qk[m][:], parts[:, r, m, 0, :],
                                                ALU.subtract).then_inc(rem1, 1)
                    for m in range(3):
                        dve.wait_ge(piece2, 3 * i + m + 1)
                        nc.vector.tensor_tensor(parts[:, r, m, 2, :], rem[:, m, :], parts[:, r, m, 1, :],
                                                ALU.subtract).then_inc(piece3, 1)

                embed(0, 0)
                embed(1, 1)
                cut(0, 0)
                with dve.Fori(0, (NCH - 2) // 2) as k:
                    embed(k * 2 + 2, 0)
                    cut(k * 2 + 1, 1)
                    embed(k * 2 + 3, 1)
                    cut(k * 2 + 2, 0)
                cut(NCH - 1, 1)


def attention(nc, g):
    TURN = KT * HG
    SWEEP = 2 * KT
    HALF = S // 2
    LEAD = KT // 2

    with ExitStack() as ctx:
        sb = lambda name, shape, dt=F32: ctx.enter_context(nc.sbuf_tensor(name, shape, dt))
        ps = lambda name, shape, dt=F32: ctx.enter_context(nc.psum_tensor(name, shape, dt))
        sem = lambda name: ctx.enter_context(nc.semaphore(name))

        k6 = sb("k_pieces", [P, 2, HG, S], BF16)
        q6 = sb("q_pieces", [P, 4, HG, CW], BF16)
        probs = sb("probs", [P, 2, HG, CW])
        vcur = sb("v_group", [P, KT, HG, 2 * D])
        half_max = sb("half_max", [P, KT, 2])
        row_max = sb("row_max", [P, KT])
        neg = sb("neg_rest", [KT, P])
        neg_parts = sb("neg_max_parts", [KT, 3, P], BF16)
        mixed = sb("mixed", [P, CW])
        zeros = sb("zero_rows", [P, C])
        sums, inv = sb("weight_sums", [P, CW // 32]), sb("inv_sums", [P, CW // 32])
        inv_rows = sb("inv_sum_rows", [P, CW])

        ps_score = [ps(f"ps_score{k}", [P, CW]) for k in range(2)]
        ps_sweep = [ps(f"ps_sweep{k}", [P, HALF]) for k in range(2)]
        ps_out = ps("ps_out", [P, CW])
        ps_misc = ps("ps_misc", [P, CW])

        k_in, q_in, m_in = sem("b_k_in"), sem("b_q_in"), sem("b_m_in")
        ones_made = sem("b_ones_made")
        zeros_made, sums_zeroed = sem("b_zeros_made"), sem("b_sums_zeroed")
        scored = sem("b_scored")
        score_slots = sem("b_score_slots")
        prob_slots = sem("b_prob_slots")
        swept = sem("b_swept")
        sweep_slots = sem("b_sweep_slots")
        max_ready = sem("b_max_ready")
        max_turned = sem("b_max_turned")
        neg_chain = sem("b_neg_chain")
        neg_ready = sem("b_neg_ready")
        v_ready = sem("b_v_ready")
        out_copied = sem("b_out_copied")
        sums_in, inv_ready, inv_back = sem("b_sums_in"), sem("b_inv_ready"), sem("b_inv_back")
        spread = sem("b_spread")
        normed = sem("b_normed")

        def load_k(sp, gg):
            row = C + (gg % (NG // B)) * HG * D
            col = (gg // (NG // B)) * S
            for n, part in enumerate(K_PIECE):
                sp.dma_start(k6[n * D:(n + 1) * D, ds(gg % 2, 1), :, :].rearrange("r a h n -> r (a h) n"),
                             g.qk_parts[part, ds(row, HG * D), ds(col, S)].rearrange("(h r) n -> r h n", r=D)
                             ).then_inc(k_in, 16)
            hold(sp, k_in, (gg + 1) * 96)

        def load_q(sp, i):
            row = ((i // QC) % (NG // B)) * HG * D
            col = (i // STEPS_B) * S + (i % QC) * CW
            for n, part in enumerate(Q_PIECE):
                sp.dma_start(q6[n * D:(n + 1) * D, ds(i % 4, 1), :, :].rearrange("r a h n -> r (a h) n"),
                             g.qk_parts[part, ds(row, HG * D), ds(col, CW)].rearrange("(h r) n -> r h n", r=D)
                             ).then_inc(q_in, 16)
            hold(sp, q_in, (i + 1) * 96)

        STEPS_B = STEPS // B

        def invert_sums(sp, m):
            hold(sp, out_copied, m + 1)
            for h in range(HG):
                sp.dma_start(sums[32 * h:32 * (h + 1), :], mixed[32 * h + D:32 * h + D + 1, :]).then_inc(sums_in, 16)
            hold(sp, inv_ready, m + 1)
            hold(sp, spread, m)
            for h in range(HG):
                sp.dma_start(inv_rows[32 * h + D:32 * h + D + 1, :], inv[32 * h:32 * (h + 1), :]).then_inc(inv_back, 16)

        with nc.Block() as block:

            @block.sync
            def _(sp):
                load_k(sp, 0)
                load_q(sp, 0)
                load_q(sp, 1)
                load_k(sp, 1)
                load_q(sp, 2)
                load_q(sp, 3)
                sp.wait_ge(zeros_made, 1)
                sp.dma_start(g.sums[0:N].rearrange("(t p) n -> p t n", p=P),
                             zeros[:].unsqueeze(1).to_broadcast([P, NT, C])).then_inc(sums_zeroed, 16)
                sp.dma_start(g.sums[N:N + P], zeros[:]).then_inc(sums_zeroed, 16)
                sp.dma_start(g.x2_rows[N:N + P], zeros[:]).then_inc(sums_zeroed, 16)

                def turn(i):
                    hold(sp, scored, (i - 3) * TURN)
                    load_q(sp, i)
                    invert_sums(sp, i - 4)

                with sp.Fori(1, NG - 1) as gg:
                    for r in range(QC):
                        turn(gg * QC + r)
                    load_k(sp, gg + 1)
                with sp.Fori(STEPS - QC, STEPS) as i:
                    turn(i)
                with sp.Fori(STEPS - QC, STEPS) as i:
                    invert_sums(sp, i)
                sp.wait_ge(sums_zeroed, 48)

            @block.gpsimd
            def _(pool):
                pool.memset(vcur[:, :, :, D:2 * D], 1.0).then_inc(ones_made, 1)
                pool.memset(inv_rows[:], 0.0).then_inc(ones_made, 1)
                pool.memset(zeros[:], 0.0).then_inc(zeros_made, 1)

                def neg_rows(i):
                    pool.wait_ge(neg_ready, i + 1)
                    for part in range(MR):
                        pool.dma_start(q6[KR + part:KR + part + 1, ds(i % 4, 1), :, :].rearrange("r a h n -> r (a h n)"),
                                       neg_parts[:, part, :]).then_inc(m_in, 16)

                def copy_v(i, kt):
                    b, hg = i // STEPS_B, (i // QC) % (NG // B)
                    pool.tensor_copy(vcur[:, kt, :, 0:D],
                                     g.v[:, ds(b * TB + kt, 1), ds(hg * HG * D, HG * D)]
                                     .rearrange("p a (h d) -> p (a h) d", h=HG)).then_inc(v_ready, 1)

                for kt in range(KT):
                    copy_v(0, kt)
                pool.wait_ge(v_ready, KT)
                pool.memset(k6[KR:KR + MR, :, :, :], 1.0).then_inc(ones_made, 1)
                pool.wait_ge(ones_made, 3)
                neg_rows(0)

                with pool.Fori(0, STEPS - 1) as i:
                    for kt in range(KT):
                        pool.wait_ge(prob_slots, 2 + i * KT + kt + 1)
                        copy_v(i + 1, kt)
                        if kt == 11:
                            neg_rows(i + 1)

            @block.tensor
            def _(pe):
                def score(i, kt, h):
                    u = i * TURN + kt * HG + h
                    pe.wait_ge(score_slots, u + 1)
                    nc.tensor.matmul(ps_score[h % 2][:],
                                     k6[0:KR + MR, ds((i // QC) % 2, 1), h, kt * P:(kt + 1) * P].rearrange("p a n -> p (a n)"),
                                     q6[0:KR + MR, ds(i % 4, 1), h, :].rearrange("p a n -> p (a n)"),
                                     start=True, stop=True).then_inc(scored, 1)

                def sweep(i, kt):
                    h, t = kt // CT, kt % CT
                    for half in range(2):
                        pe.wait_ge(sweep_slots, i * SWEEP + 2 * kt + half + 1)
                        for c in range(2):
                            k0 = half * HALF + c * CW
                            ins = nc.tensor.matmul(ps_sweep[half][:, c * CW:(c + 1) * CW],
                                                   q6[0:KR, ds(i % 4, 1), h, t * P:(t + 1) * P].rearrange("p a n -> p (a n)"),
                                                   k6[0:KR, ds((i // QC) % 2, 1), h, k0:k0 + CW].rearrange("p a n -> p (a n)"),
                                                   start=True, stop=True)
                        ins.then_inc(swept, 1)

                def mix(i, kt):
                    pe.wait_ge(score_slots, 2 + i * TURN + (kt + 1) * HG)
                    pe.wait_ge(v_ready, i * KT + kt + 1)
                    if kt == 0:
                        pe.wait_ge(out_copied, i)
                    for h in range(HG):
                        ins = nc.tensor.matmul(ps_out[32 * h:32 * (h + 1), :], vcur[:, kt, h, :], probs[:, kt % 2, h, :],
                                               start=(kt == 0), stop=(kt == KT - 1))
                    ins.then_inc(prob_slots, 1)

                def turn_max(i):
                    pe.wait_ge(max_ready, i + 1)
                    nc.tensor.transpose(ps_misc[0:KT, 0:P], row_max[:], g.ident[:]).then_inc(max_turned, 1)

                def spread_sums(i):
                    pe.wait_ge(inv_back, 64 * (i + 1))
                    nc.tensor.matmul(ps_misc[:], g.spread[:], inv_rows[:], start=True, stop=True).then_inc(spread, 1)

                def turn(i, first=False, ahead=2):
                    pe.wait_ge(m_in, (i + 1) * 48)
                    for kt in range(KT):
                        score(i, kt, 0)
                        score(i, kt, 1)
                        if kt > 0:
                            mix(i, kt - 1)
                        elif not first:
                            mix(i - 1, KT - 1)
                        score(i, kt, 2)
                        score(i, kt, 3)
                        if kt < KT - LEAD:
                            if ahead >= 1:
                                sweep(i + 1, kt + LEAD)
                        elif ahead == 2:
                            if kt == KT - LEAD:
                                pe.wait_ge(q_in, (i + 3) * 96)
                                pe.wait_ge(k_in, ((i + 2) // QC + 1) * 96)
                            sweep(i + 2, kt - (KT - LEAD))
                        if kt == 6 and not first:
                            pe.wait_ge(neg_ready, i + 1)
                            spread_sums(i - 1)
                        if kt == 10 and ahead >= 1:
                            if not first:
                                pe.wait_ge(normed, 2 * i)
                            turn_max(i + 1)

                pe.wait_ge(k_in, 96)
                pe.wait_ge(q_in, 96)
                for kt in range(KT):
                    sweep(0, kt)
                pe.wait_ge(q_in, 192)
                for kt in range(LEAD):
                    sweep(1, kt)
                    if kt == 1:
                        turn_max(0)
                pe.wait_ge(ones_made, 3)
                turn(0, first=True)
                with pe.Fori(0, (STEPS - 4) // 2) as k:
                    turn(k * 2 + 1)
                    turn(k * 2 + 2)
                turn(STEPS - 3)
                turn(STEPS - 2, ahead=1)
                turn(STEPS - 1, ahead=0)
                mix(STEPS - 1, KT - 1)
                spread_sums(STEPS - 1)

            @block.scalar
            def _(act):
                act.sem_inc(score_slots, 2)

                def copy_out(i):
                    act.wait_ge(prob_slots, 2 + (i + 1) * KT)
                    act.wait_ge(normed, 2 * i)
                    nc.scalar.activation(mixed[:], ps_out[:], ACT.Copy).then_inc(out_copied, 1)

                def turn(i, first=False):
                    for kt in range(KT):
                        act.wait_ge(prob_slots, i * KT + kt + 1)
                        for h in range(HG):
                            act.wait_ge(scored, i * TURN + kt * HG + h + 1)
                            nc.scalar.activation(probs[:, kt % 2, h, :], ps_score[h % 2][:], ACT.Exp,
                                                 scale=SCALE).then_inc(score_slots, 1)
                        if kt == 0 and not first:
                            copy_out(i - 1)

                turn(0, first=True)
                turn(1)
                with act.Fori(1, STEPS // 2) as k:
                    turn(k * 2)
                    turn(k * 2 + 1)
                copy_out(STEPS - 1)

            @block.vector
            def _(dve):
                dve.sem_inc(sweep_slots, 2)
                dve.sem_inc(prob_slots, 2)

                def row_tile(i, kt):
                    if kt == 0:
                        dve.wait_ge(max_ready, i)
                    for half in range(2):
                        dve.wait_ge(swept, i * SWEEP + 2 * kt + half + 1)
                        nc.vector.tensor_reduce(half_max[:, kt, half:half + 1], ps_sweep[half][:], AX.X,
                                                ALU.max).then_inc(sweep_slots, 1)

                def whole_rows(i):
                    dve.wait_ge(sweep_slots, 2 + (i + 1) * SWEEP)
                    dve.wait_ge(max_turned, i)
                    nc.vector.tensor_reduce(row_max[:], half_max[:], AX.X, ALU.max).then_inc(max_ready, 1)

                def cut_max(i, first_half):
                    chain = Tally(neg_chain, i * 3 + (0 if first_half else 2))
                    mt = ps_misc[0:KT, 0:P]
                    if first_half:
                        dve.wait_ge(max_turned, i + 1)
                        dve.wait_ge(m_in, i * 48)
                        n = chain.add(nc.vector.tensor_scalar(neg_parts[:, 0, :], mt, -1.0, None, ALU.mult))
                        dve.wait_ge(neg_chain, n)
                        n = chain.add(nc.vector.scalar_tensor_tensor(out=neg[:], in0=mt, scalar=-1.0, in1=neg_parts[:, 0, :],
                                                                     op0=ALU.mult, op1=ALU.subtract))
                        dve.wait_ge(neg_chain, n)
                    else:
                        n = chain.add(nc.vector.tensor_copy(neg_parts[:, 1, :], neg[:]))
                        dve.wait_ge(neg_chain, n)
                        nc.vector.tensor_tensor(neg_parts[:, 2, :], neg[:], neg_parts[:, 1, :],
                                                ALU.subtract).then_inc(neg_ready, 1)

                def invert(i):
                    dve.wait_ge(sums_in, 64 * (i + 1))
                    dve.wait_ge(inv_back, 64 * i)
                    nc.vector.reciprocal(inv[:], sums[:]).then_inc(inv_ready, 1)

                def normalise(i, half):
                    dve.wait_ge(spread, i + 1)
                    h0, w = half * (CW // 2), CW // 2
                    nc.vector.tensor_tensor(g.mixed[:, ds(i // QC, 1), ds((i % QC) * CW + h0, w)]
                                            .rearrange("p a n -> p (a n)"), mixed[:, h0:h0 + w], ps_misc[:, h0:h0 + w],
                                            ALU.mult).then_inc(normed, 1)

                def turn(i, first=False, ahead=2):
                    for kt in range(KT):
                        if kt < KT - LEAD:
                            if ahead >= 1:
                                row_tile(i + 1, kt + LEAD)
                                if kt == KT - LEAD - 1:
                                    whole_rows(i + 1)
                        elif ahead == 2:
                            row_tile(i + 2, kt - (KT - LEAD))
                        if not first:
                            if kt == 2:
                                invert(i - 1)
                            if kt in (7, 8):
                                normalise(i - 1, kt - 7)
                        if ahead >= 1 and kt in (11, 12):
                            cut_max(i + 1, kt == 11)

                for kt in range(KT):
                    row_tile(0, kt)
                whole_rows(0)
                for kt in range(LEAD):
                    row_tile(1, kt)
                    if kt in (1, 2):
                        cut_max(0, kt == 1)
                turn(0, first=True)
                with dve.Fori(0, (STEPS - 4) // 2) as k:
                    turn(k * 2 + 1)
                    turn(k * 2 + 2)
                turn(STEPS - 3)
                turn(STEPS - 2, ahead=1)
                turn(STEPS - 1, ahead=0)
                invert(STEPS - 1)
                normalise(STEPS - 1, 0)
                normalise(STEPS - 1, 1)


def mix_heads_and_gate(nc, g, w_out, gate_rows, gate_bias, w1, b1, b2_rows):
    with ExitStack() as ctx:
        sb = lambda name, shape, dt=F32: ctx.enter_context(nc.sbuf_tensor(name, shape, dt))
        ps = lambda name, shape, dt=F32: ctx.enter_context(nc.psum_tensor(name, shape, dt))
        sem = lambda name: ctx.enter_context(nc.semaphore(name))
        HGS = NG // B

        wo = sb("w_out_rows", [P, HGS, C])
        gw_a, gw_b = sb("gate_w_a", [P, E + 1]), sb("gate_w_b", [CB, E + 1])
        gb = sb("gate_b_rows", [P, E + 1])
        heads = sb("heads", [P, HGS, CW])
        stats, mv = sb("ln2_stats", [P, CT, 6]), sb("ln2_mean_var", [P, CT, 2])
        ve, sd, rstd = sb("ln2_var_eps", [P, CT]), sb("ln2_sd", [P, CT]), sb("ln2_rstd", [P, CT])
        x2 = sb("x2", [P, 2, CT, C])
        xa, xb = sb("x2_t_a", [P, CW]), sb("x2_t_b", [CB, CW])

        ps_o = [[ps(f"ps_o{r}{k}", [P, 2 * C]) for k in range(2)] for r in range(2)]
        ps_ta, ps_tb = ps("ps2_ta", [P, CW]), ps("ps2_tb", [CB, CW])
        ps_l = ps("ps_logits", [P, CT * (E + 1)])

        loaded, weights_in = sem("c_loaded"), sem("c_weights_in")
        zeroed = sem("c_zeroed")
        heads_ready, mixed_out = sem("c_heads_ready"), sem("c_mixed_out")
        chained, var_ready, sd_ready = sem("c_chain"), sem("c_var_ready"), sem("c_sd_ready")
        x2_ready, turned, xt_ready = sem("c_x2_ready"), sem("c_turned"), sem("c_xt_ready")
        gated, gate_read, x2_stored = sem("c_gated"), sem("c_gate_read"), sem("c_x2_stored")

        with nc.Block() as block:

            @block.sync
            def _(sp):
                sp.wait_ge(zeroed, 1)
                for h in range(HG):
                    sp.dma_start(wo[32 * h:32 * h + D],
                                 w_out.rearrange("(a h r) n -> h r a n", h=HG, r=D)[h]).then_inc(loaded, 16)
                sp.dma_start(gw_a[:], gate_rows[0:P]).then_inc(loaded, 16)
                sp.dma_start(gw_b[:], gate_rows[P:C]).then_inc(loaded, 16)
                sp.dma_start(gb[:], gate_bias.to_broadcast([P, E + 1])).then_inc(loaded, 16)
                sp.dma_start(g.b2[:].rearrange("p e n -> p (e n)"), b2_rows.to_broadcast([P, E * C])).then_inc(weights_in, 16)
                sp.dma_start(g.w1_b[CB:CB + 1], b1.rearrange("(a e) f -> a e f", a=1)).then_inc(weights_in, 16)
                assert E == NCH
                with sp.Fori(0, NCH) as i:
                    hold(sp, x2_ready, i + 1)
                    sp.dma_start(g.x2_rows[ds(i * CW, CW)].rearrange("(t p) n -> p t n", p=P),
                                 x2[:, ds(i % 2, 1)].rearrange("p a t n -> p (a t) n")).then_inc(x2_stored, 16)
                    sp.dma_start(g.w1_a[:, ds(i, 1), :], w1[ds(i, 1), 0:P, :].rearrange("e k f -> k e f")).then_inc(weights_in, 16)
                    sp.dma_start(g.w1_b[0:CB, ds(i, 1), :], w1[ds(i, 1), P:C, :].rearrange("e k f -> k e f")).then_inc(weights_in, 16)
                    hold(sp, x2_stored, 16 * i + 16)
                sp.wait_ge(weights_in, 16 * (2 + 2 * E))

            @block.gpsimd
            def _(pool):
                pool.memset(wo[:], 0.0).then_inc(zeroed, 1)

            @block.scalar
            def _(act):
                def copy_heads(i):
                    act.wait_ge(mixed_out, i)
                    nc.scalar.activation(heads[:], g.mixed[:, ds((i // QC) * HGS, HGS), ds((i % QC) * CW, CW)],
                                         ACT.Copy).then_inc(heads_ready, 1)

                def root(i):
                    act.wait_ge(var_ready, i + 1)
                    nc.scalar.activation(sd[:], ve[:], ACT.Sqrt).then_inc(sd_ready, 1)

                def copy_x(i):
                    act.wait_ge(turned, i + 1)
                    act.wait_ge(gated, i)
                    nc.scalar.activation(xa[:], ps_ta[:], ACT.Copy).then_inc(xt_ready, 1)
                    nc.scalar.activation(xb[:], ps_tb[:], ACT.Copy).then_inc(xt_ready, 1)

                copy_heads(0)
                copy_heads(1)
                root(0)
                copy_heads(2)
                with act.Fori(0, NCH - 3) as i:
                    root(i + 1)
                    copy_x(i)
                    copy_heads(i + 3)
                for i in range(NCH - 3, NCH):
                    if i < NCH - 1:
                        root(i + 1)
                    copy_x(i)

            @block.tensor
            def _(pe):
                def mix(i, r):
                    pe.wait_ge(heads_ready, i + 1)
                    if not isinstance(i, int):
                        pe.wait_ge(x2_ready, i - 1)
                    for j in range(CT):
                        for a in range(HGS):
                            last = nc.tensor.matmul(ps_o[r][j // 2][:, (j % 2) * C:(j % 2 + 1) * C],
                                                    heads[:, a, j * P:(j + 1) * P], wo[:, a, :],
                                                    start=(a == 0), stop=(a == HGS - 1))
                    last.then_inc(mixed_out, 1)

                def turn_x(i, r):
                    pe.wait_ge(x2_ready, i + 1)
                    pe.wait_ge(xt_ready, 2 * i)
                    for j in range(CT):
                        nc.tensor.transpose(ps_ta[:, j * P:(j + 1) * P], x2[:, r, j, 0:P], g.ident[:])
                        last = nc.tensor.transpose(ps_tb[:, j * P:(j + 1) * P], x2[:, r, j, P:C], g.ident[:])
                    last.then_inc(turned, 1)

                def gate(i):
                    pe.wait_ge(xt_ready, 2 * i + 2)
                    pe.wait_ge(gate_read, i)
                    for j in range(CT):
                        dst = ps_l[:, j * (E + 1):(j + 1) * (E + 1)]
                        nc.tensor.matmul(dst, xa[:, j * P:(j + 1) * P], gw_a[:], start=True, stop=False)
                        last = nc.tensor.matmul(dst, xb[:, j * P:(j + 1) * P], gw_b[:], start=False, stop=True)
                    last.then_inc(gated, 1)

                pe.wait_ge(loaded, 16 * 7)
                mix(0, 0)
                mix(1, 1)
                with pe.Fori(0, (NCH - 2) // 2) as k:
                    for r in range(2):
                        turn_x(k * 2 + r, r)
                        mix(k * 2 + r + 2, r)
                        gate(k * 2 + r)
                for r in range(2):
                    turn_x(NCH - 2 + r, r)
                    gate(NCH - 2 + r)

            @block.vector
            def _(dve):
                per_turn = 2 + 2 * CT + 1 + CT - 1

                def norm(i, r):
                    chain = Tally(chained, i * per_turn)
                    dve.wait_ge(mixed_out, i + 1)
                    for k in range(2):
                        hk = g.h[:, ds(CT * i + 2 * k, 2), :]
                        n = chain.add(nc.vector.tensor_tensor(hk, ps_o[r][k][:].rearrange("p (j n) -> p j n", j=2), hk, ALU.add))
                    hold(dve, chain.sem, n)
                    for j in range(CT):
                        n = chain.add(nc.vector.bn_stats(stats[:, j, :], g.h[:, ds(CT * i + j, 1), :]
                                                         .rearrange("p a n -> p (a n)")))
                    hold(dve, chain.sem, n)
                    for j in range(CT):
                        n = chain.add(nc.vector.bn_aggr(mv[:, j, :], stats[:, j, :]))
                    dve.wait_ge(chain.sem, n)
                    nc.vector.tensor_scalar_add(ve[:], mv[:, :, 1], EPS).then_inc(var_ready, 1)
                    dve.wait_ge(sd_ready, i + 1)
                    n = chain.add(nc.vector.reciprocal(rstd[:], sd[:]))
                    dve.wait_ge(chain.sem, n)
                    if not isinstance(i, int):
                        dve.wait_ge(turned, i - 1)
                        dve.wait_ge(x2_stored, 16 * (i - 1))
                    for j in range(CT):
                        ins = nc.vector.tensor_scalar(x2[:, r, j, :], g.h[:, ds(CT * i + j, 1), :]
                                                      .rearrange("p a n -> p (a n)"),
                                                      mv[:, j, 0:1], rstd[:, j:j + 1], ALU.subtract, ALU.mult)
                        if j < CT - 1:
                            chain.add(ins)
                        else:
                            ins.then_inc(x2_ready, 1)
                    assert chain.n == per_turn

                def read_logits(i):
                    dve.wait_ge(gated, i + 1)
                    nc.vector.tensor_tensor(g.logits[:, ds(CT * i, CT), :],
                                            ps_l[:].rearrange("p (j n) -> p j n", j=CT),
                                            gb[:].unsqueeze(1).to_broadcast([P, CT, E + 1]), ALU.add).then_inc(gate_read, 1)

                norm(0, 0)
                norm(1, 1)
                dve.wait_ge(loaded, 16 * 7)
                read_logits(0)
                with dve.Fori(0, (NCH - 2) // 2) as k:
                    for r in range(2):
                        norm(k * 2 + r + 2, r)
                        read_logits(k * 2 + r + 1)
                read_logits(NCH - 1)


class Chain:

    def __init__(self, eng, sem):
        self.eng, self.sem, self.n = eng, sem, 0

    def count(self, ins):
        ins.then_inc(self.sem, 1)
        self.n += 1

    def wait(self):
        self.eng.wait_ge(self.sem, self.n)

    def step(self, ins):
        self.count(ins)
        self.wait()


def route(nc, g, w2):
    with ExitStack() as ctx:
        sb = lambda name, shape, dt=F32: ctx.enter_context(nc.sbuf_tensor(name, shape, dt))
        ps = lambda name, shape, dt=F32: ctx.enter_context(nc.psum_tensor(name, shape, dt))
        sem = lambda name: ctx.enter_context(nc.semaphore(name))

        sh = [P, NT, E]
        ex, pr, eq, sc = sb("r_ex", sh), sb("r_prob", sh), sb("r_eq", sh), sb("r_score", sh)
        pick = [sb(f"r_pick{k}", sh) for k in range(2)]
        top = [sb(f"r_top{k}", [P, NT]) for k in range(2)]
        m = sb("r_max", [P, NT])
        first = sb("r_first", [P, NT])
        prefer = sb("r_prefer", [P, E])
        by_expert = sb("r_by_expert", [P, E, NT])
        before = sb("r_before", [P, P])
        ones = sb("r_ones", [P, P])
        go_on = sb("r_go_on", [P, E, NT])
        total = sb("r_total", [P, E, NT])
        upto = sb("r_upto", [P, E, NT])
        slot = sb("r_slot", [P, E, NT])
        tiles_f, tiles_i = sb("r_tiles_f", [P, E]), sb("r_tiles_i", [P, E], I32)
        tiles_end, tiles_start = sb("r_tiles_end", [P, E]), sb("r_tiles_start", [P, E])
        dest_f = sb("r_dest_f", [P, 2, NT])
        dest_i = sb("r_dest_i", [P, 2, NT], I32)
        part_i = sb("r_dest_part_i", [P, 2, NT], I32)
        lane, tile = sb("r_lane", [P, 2, NT]), sb("r_tile", [P, 2, NT])
        ids1 = sb("r_token_plus1", [P, NT])
        iota = sb("r_iota", [P, P])
        dummy = sb("r_dummy", [P, 1])
        hot = [sb(f"r_hot{k}", [P, P]) for k in range(2)]
        what = [sb(f"r_what{k}", [P, 2, ET]) for k in range(2)]
        over = sb("r_over", [P, ET, E])
        eid_f = sb("r_eid_f", [P, ET])
        idf, unused = sb("r_id_f", [P, ET]), sb("r_unused", [P, ET])
        ps_rank, ps_total = ps("ps_rank", [P, E * NT]), ps("ps_total", [P, E * NT])
        ps_slots = ps("ps_slots", [P, 2 * ET])

        const, v_chain, v_const = sem("r_const"), sem("r_chain"), sem("r_v_const")
        shifted, exped = sem("r_shifted"), sem("r_exped")
        picked, ranked = sem("r_picked"), sem("r_ranked")
        hot_ready = sem("r_hot_ready")
        hot_slots = sem("r_hot_slots")

        weights_in = sem("r_weights_in")

        with nc.Block() as block:

            @block.sync
            def _(sp):
                for e in range(E):
                    sp.dma_start(g.w2[:, e], w2[e].rearrange("(j k) n -> k j n", k=P)).then_inc(weights_in, 16)
                sp.wait_ge(weights_in, 16 * E)

            @block.gpsimd
            def _(pool):
                pool.iota(iota[:], [[1, P]], base=0, channel_multiplier=0,
                          allow_small_or_imprecise_dtypes=True).then_inc(const, 1)
                pool.iota(prefer[:], [[-1, E]], base=E, channel_multiplier=0,
                          allow_small_or_imprecise_dtypes=True).then_inc(const, 1)
                pool.iota(ids1[:], [[P, NT]], base=1, channel_multiplier=1,
                          allow_small_or_imprecise_dtypes=True).then_inc(const, 1)
                pool.iota(dummy[:], [[1, 1]], base=N + 1, channel_multiplier=1,
                          allow_small_or_imprecise_dtypes=True).then_inc(const, 1)
                pool.memset(before[:], 1.0).then_inc(const, 1)
                pool.memset(ones[:], 1.0).then_inc(const, 1)
                pool.memset(go_on[:], 1.0).then_inc(const, 1)
                pool.wait_ge(const, 7)
                pool.affine_select(out=before[:], in_=before[:], compare_op=ALU.is_gt, fill=0.0, base=0,
                                   pattern=[[1, P]], channel_multiplier=-1).then_inc(const, 1)
                pool.memset(go_on[:, :, 0:1], 0.0).then_inc(const, 1)

            @block.scalar
            def _(act):
                act.wait_ge(shifted, 1)
                nc.scalar.activation(ex[:], pr[:], ACT.Exp).then_inc(exped, 1)

            @block.tensor
            def _(pe):
                pe.wait_ge(const, 9)
                pe.wait_ge(picked, 1)
                mask = by_expert[:].rearrange("p e t -> p (e t)")
                nc.tensor.matmul(ps_rank[:], before[:], mask, start=True, stop=True)
                nc.tensor.matmul(ps_total[:], ones[:], mask, start=True, stop=True).then_inc(ranked, 1)

                def place(t, first=False, last=False):
                    for k in range(2):
                        pe.wait_ge(hot_ready, 2 * t + k + 1)
                        nc.tensor.matmul(ps_slots[:], hot[k][:], what[k][:].rearrange("p a j -> p (a j)"),
                                         start=(first and k == 0), stop=(last and k == 1)).then_inc(hot_slots, 1)

                place(0, first=True)
                with pe.Fori(1, NT - 1) as t:
                    place(t)
                place(NT - 1, last=True)

            @block.vector
            def _(dve):
                v = nc.vector
                c = Chain(dve, v_chain)
                wide = lambda a: a.unsqueeze(2).to_broadcast(sh)
                lg = g.logits[:, :, 0:E]
                c.step(v.tensor_reduce(m[:], lg, AX.X, ALU.max))
                v.tensor_tensor(pr[:], lg, wide(m[:]), ALU.subtract).then_inc(shifted, 1)
                dve.wait_ge(exped, 1)
                c.step(v.tensor_reduce(m[:], ex[:], AX.X, ALU.add))
                c.step(v.reciprocal(first[:], m[:]))
                c.step(v.tensor_tensor(pr[:], ex[:], wide(first[:]), ALU.mult))
                dve.wait_ge(const, 9)
                for k in range(2):
                    c.step(v.tensor_reduce(top[k][:], pr[:], AX.X, ALU.max))
                    c.step(v.tensor_tensor(eq[:], pr[:], wide(top[k][:]), ALU.is_equal))
                    c.step(v.tensor_tensor(sc[:], eq[:], prefer[:].unsqueeze(1).to_broadcast(sh), ALU.mult))
                    c.step(v.tensor_reduce(first[:], sc[:], AX.X, ALU.max))
                    c.step(v.tensor_tensor(pick[k][:], sc[:], wide(first[:]), ALU.is_equal))
                    if k == 0:
                        c.step(v.scalar_tensor_tensor(out=pr[:], in0=pick[0][:], scalar=-2.0, in1=pr[:],
                                                      op0=ALU.mult, op1=ALU.add))
                v.tensor_tensor(by_expert[:].rearrange("p e t -> p t e"), pick[0][:], pick[1][:],
                                ALU.add).then_inc(picked, 1)
                c.step(v.tensor_tensor(m[:], top[0][:], top[1][:], ALU.add))
                c.step(v.reciprocal(first[:], m[:]))
                c.step(v.tensor_tensor(top[0][:], top[0][:], first[:], ALU.mult))
                c.step(v.tensor_tensor(top[1][:], top[1][:], first[:], ALU.mult))
                dve.wait_ge(ranked, 1)
                flat = lambda a: a.rearrange("p e t -> p (e t)")
                c.step(v.tensor_copy(flat(total[:]), ps_total[:]))
                c.step(v.tensor_tensor_scan(flat(upto[:]), flat(go_on[:]), flat(total[:]), 0.0, ALU.mult, ALU.add))
                c.step(v.tensor_scalar(tiles_i[:], upto[:, :, NT - 1], float(P - 1), None, ALU.add))
                c.step(v.tensor_scalar(tiles_i[:], tiles_i[:], 7, None, ALU.arith_shift_right))
                c.step(v.tensor_copy(tiles_f[:], tiles_i[:]))
                c.step(v.tensor_tensor_scan(tiles_end[:], ones[:, 0:E], tiles_f[:], 0.0, ALU.mult, ALU.add))
                c.step(v.tensor_tensor(tiles_start[:], tiles_end[:], tiles_f[:], ALU.subtract))
                c.step(v.tensor_tensor(slot[:], upto[:], total[:], ALU.subtract))
                c.step(v.tensor_tensor(flat(slot[:]), flat(slot[:]), ps_rank[:], ALU.add))
                c.step(v.scalar_tensor_tensor(out=slot[:], in0=tiles_start[:].unsqueeze(2).to_broadcast([P, E, NT]),
                                              scalar=float(P), in1=slot[:], op0=ALU.mult, op1=ALU.add))
                for k in range(2):
                    c.step(v.tensor_tensor(eq[:], pick[k][:], slot[:].rearrange("p e t -> p t e"), ALU.mult))
                    c.step(v.tensor_reduce(dest_f[:, k, :], eq[:], AX.X, ALU.add))
                c.step(v.tensor_copy(dest_i[:], dest_f[:]))
                c.step(v.tensor_scalar(part_i[:], dest_i[:], 7, None, ALU.arith_shift_right))
                c.step(v.tensor_copy(tile[:], part_i[:]))
                c.step(v.tensor_scalar(part_i[:], dest_i[:], P - 1, None, ALU.bitwise_and))
                c.step(v.tensor_copy(lane[:], part_i[:]))
                c.step(v.tensor_tensor(over[:], iota[:, 0:ET].unsqueeze(2).to_broadcast([P, ET, E]),
                                       tiles_end[:].unsqueeze(1).to_broadcast([P, ET, E]), ALU.is_ge))
                c.step(v.tensor_reduce(eid_f[:], over[:], AX.X, ALU.add))
                c.step(v.tensor_scalar(g.expert_of[:], eid_f[:], float(E - 1), None, ALU.min))
                dve.sem_inc(hot_slots, 2)
                with dve.Fori(0, NT) as t:
                    for k in range(2):
                        dve.wait_ge(hot_slots, 2 * t + k + 1)
                        at = tile[:, k, ds(t, 1)]
                        v.tensor_scalar(hot[k][:], iota[:], lane[:, k, ds(t, 1)], None, ALU.is_equal)
                        v.tensor_scalar(what[k][:, 0, :], iota[:, 0:ET], at, ids1[:, ds(t, 1)], ALU.is_equal, ALU.mult)
                        v.tensor_scalar(what[k][:, 1, :], iota[:, 0:ET], at, top[k][:, ds(t, 1)],
                                        ALU.is_equal, ALU.mult).then_inc(hot_ready, 1)
                dve.wait_ge(hot_slots, 2 + 2 * NT)
                c.step(v.tensor_copy(idf[:], ps_slots[:, 0:ET]))
                c.step(v.tensor_copy(g.slot_weight[:], ps_slots[:, ET:2 * ET]))
                c.step(v.tensor_scalar(unused[:], idf[:], 0.0, dummy[:, 0:1], ALU.is_equal, ALU.mult))
                c.step(v.tensor_tensor(idf[:], idf[:], unused[:], ALU.add))
                c.step(v.tensor_scalar(g.slot_token[:], idf[:], -1.0, None, ALU.add))


def experts_and_spectrum(nc, g, out_rows):
    FT = F // P
    L = 2 * B
    HI = 32 + B
    LEVELS = 3
    GROUPS = P >> LEVELS
    MAP_STEPS, ADD_TILES = 2, 2
    MAPS_TURN = 1 + TB // MAP_STEPS
    CARRY = MAPS_TURN + 4
    HAND_DOWN = CARRY + GROUPS - 1
    RUN = HAND_DOWN + LEVELS + 2
    ADD = RUN + TB + 1
    ADD_END = ADD + NT // ADD_TILES
    assert ADD_END < ET and MAPS_TURN % 2 == 1 and RUN % 2 == 1 and ET % 2 == 1

    with ExitStack() as ctx:
        sb = lambda name, shape, dt=F32: ctx.enter_context(nc.sbuf_tensor(name, shape, dt))
        sem = lambda name: ctx.enter_context(nc.semaphore(name))

        a = sb("s_a", [P, L, TB])
        y = sb("s_y", [P, TB + 2, 2, 2, L])
        t = sb("s_t", [P, 2, 2, L])
        flip = sb("s_flip", [P, P])
        maps = [sb(f"s_maps{l}", [HI, P >> l, 4, 5]) for l in range(LEVELS + 1)]
        prod = sb("s_map_product", [HI, P // 2, 2, 5])
        mag, scale = sb("s_map_magnitude", [HI, P // 2, 2]), sb("s_map_scale", [HI, P // 2])
        ws = [sb(f"s_w{l}", [HI, P >> l, 2]) for l in range(LEVELS + 1)]
        wnd, wtmp = sb("s_w_fraction", [HI, P // 2, 5]), sb("s_w_tmp", [HI, P // 2, 5])
        wsq, wpr = sb("s_w_sq", [HI, P // 2, 2]), sb("s_w_products", [HI, P // 2, 2, 2])
        wnorm = sb("s_w_norm", [HI, P // 2])
        w = sb("s_w", [HI, 2])
        num, nd = sb("s_num", [HI, 5]), sb("s_nd", [HI, 5])
        sq, norm, rnorm = sb("s_sq", [HI, 2]), sb("s_norm", [HI, 1]), sb("s_rnorm", [HI, 1])
        back = sb("s_back", [P, 2, B])
        win = sb("s_w_in", [P, 2, L])
        d = sb("s_d", [P, 2, TB, L])
        sqw, qw = sb("s_sq_wide", [P, 2, L]), sb("s_q_wide", [P, L])
        z = sb("s_z", [P, 2, B, TB])
        z2, zn = sb("s_z_sq", [P, 2, B, TB]), sb("s_z_norm", [P, B, TB])
        rows = sb("s_rows", [P, 4, C])
        rows_s = sb("s_rows_scaled", [P, 3, C])

        const, loaded = sem("s_const"), sem("s_loaded")
        chained = sem("s_chain")
        maps_made, maps_turned, maps_read = sem("s_maps_made"), sem("s_maps_turned"), sem("s_maps_read")
        carried, carry_back, back_read, flipped = (
            sem("s_carried"), sem("s_carry_back"), sem("s_back_read"), sem("s_flipped"))
        finished = sem("s_finished")

        ids_in = [sb(f"e_ids_gather{r}", [P, 1], I32) for r in range(2)]
        ids_out = [sb(f"e_ids_scatter{r}", [P, 1], I32) for r in range(2)]
        xg = [sb(f"e_x{r}", [P, C]) for r in range(2)]
        xa, xb = sb("e_x_t_a", [P, P]), sb("e_x_t_b", [CB + 1, P])
        room = g.mixed[:].rearrange("p a n -> p (a n)")
        hid, hid_t = room[:, 0:F], room[:, F:2 * F]
        yt = sb("e_y", [P, C])
        yw = sb("e_y_weighted", [P, C])
        ps = lambda name, shape, dt=F32: ctx.enter_context(nc.psum_tensor(name, shape, dt))
        ps_x = ps("ps_x", [P, 2 * P])
        ps_h = ps("ps_h", [P, 1024])
        ps_ht = ps("ps_ht", [P, 1024])
        ps_y = ps("ps_y", [P, C])
        ps_m = ps("ps_maps", [P, 4 * P])
        ps_c, ps_cb = ps_m[:, 0:4 * B].rearrange("p (x n) -> p x n", x=2), ps("ps_carry_back", [P, 2 * B])

        ones_made = sem("e_ones")
        id1, id2 = sem("e_ids_gather_ready"), sem("e_ids_scatter_ready")
        gathered = [sem(f"e_gathered{r}") for r in range(2)]
        x_turned, xt_ready = sem("e_x_turned"), sem("e_xt_ready")
        hidden, gelu_done, h_turned, ht_ready = sem("e_hidden_done"), sem("e_gelu"), sem("e_h_turned"), sem("e_ht_ready")
        y_done, y_ready, yw_ready, added = sem("e_y_done"), sem("e_y_ready"), sem("e_yw_ready"), sem("e_added")

        with nc.Block() as block:

            @block.sync
            def _(sp):
                sp.dma_start(rows[:].rearrange("p a n -> p (a n)"), out_rows.to_broadcast([P, 4 * C])).then_inc(loaded, 16)

            @block.gpsimd
            def _(pool):
                pool.memset(xb[CB:CB + 1, :], 1.0).then_inc(ones_made, 1)
                pool.wait_ge(ones_made, 1)

                def gather(j, r):
                    if not isinstance(j, int) or j >= 2:
                        pool.wait_ge(x_turned, j - 1)
                    pool.tensor_copy(ids_in[r][:], g.slot_token[:, ds(j, 1)]).then_inc(id1, 1)
                    hold(pool, id1, j + 1)
                    pool.indirect_dma_start(out=xg[r][:], out_offset=None, in_=g.x2_rows[:],
                                            in_offset=bass.IndirectOffsetOnAxis(ap=ids_in[r][:, 0:1], axis=0)
                                            ).then_inc(gathered[r], 16)

                def add(j, r):
                    pool.wait_ge(added, 16 * j)
                    pool.tensor_copy(ids_out[r][:], g.slot_token[:, ds(j, 1)]).then_inc(id2, 1)
                    pool.wait_ge(id2, j + 1)
                    hold(pool, yw_ready, j + 1)
                    pool.indirect_dma_start(out=g.sums[:], in_=yw[:], in_offset=None,
                                            out_offset=bass.IndirectOffsetOnAxis(ap=ids_out[r][:, 0:1], axis=0),
                                            compute_op=ALU.add).then_inc(added, 16)

                gather(0, 0)
                gather(1, 1)
                pool.memset(flip[:], 0.0).then_inc(const, 1)
                pool.wait_ge(const, 1)
                pool.affine_select(out=flip[:], in_=flip[:], compare_op=ALU.not_equal, fill=1.0, base=-(P - 1),
                                   pattern=[[1, P]], channel_multiplier=1).then_inc(const, 1)
                gather(2, 0)
                with pool.Fori(0, (ET - 3) // 2) as k:
                    for r in range(2):
                        j = k * 2 + 1 + r
                        gather(j + 2, (1 + r) % 2)
                        add(j - 1, r)
                for j in range(ET - 3, ET):
                    add(j, j % 2)
                pool.wait_ge(added, 16 * ET)

            @block.tensor
            def _(pe):
                def turn_x(j, r):
                    pe.wait_ge(gathered[r], (j - r) * 8 + 16)
                    pe.wait_ge(xt_ready, 2 * j)
                    nc.tensor.transpose(ps_x[:, 0:P], xg[r][:, 0:P], g.ident[:])
                    nc.tensor.transpose(ps_x[0:CB, P:2 * P], xg[r][:, P:C], g.ident[:]).then_inc(x_turned, 1)

                def up(j):
                    e = pe.value_load(g.expert_of[0:1, ds(j, 1)], min_val=0, max_val=E - 1)
                    pe.wait_ge(xt_ready, 2 * j + 2)
                    pe.wait_ge(gelu_done, j)
                    for c0, c1 in ((0, 512), (512, F)):
                        nc.tensor.matmul(ps_h[:, c0:c1], xa[:], g.w1_a[:, ds(e, 1), c0:c1].rearrange("p a n -> p (a n)"),
                                         start=True, stop=False)
                        last = nc.tensor.matmul(ps_h[:, c0:c1], xb[:],
                                                g.w1_b[:, ds(e, 1), c0:c1].rearrange("p a n -> p (a n)"),
                                                start=False, stop=True)
                    last.then_inc(hidden, 1)

                def turn_h(j):
                    pe.wait_ge(gelu_done, j + 1)
                    pe.wait_ge(ht_ready, j)
                    for k in range(FT):
                        last = nc.tensor.transpose(ps_ht[:, k * P:(k + 1) * P], hid[:, k * P:(k + 1) * P], g.ident[:])
                    last.then_inc(h_turned, 1)

                def down(j):
                    e = pe.value_load(g.expert_of[0:1, ds(j, 1)], min_val=0, max_val=E - 1)
                    pe.wait_ge(ht_ready, j + 1)
                    pe.wait_ge(y_ready, j)
                    for k in range(FT):
                        last = nc.tensor.matmul(ps_y[:], hid_t[:, k * P:(k + 1) * P],
                                                g.w2[:, ds(e, 1), k, :].rearrange("p a n -> p (a n)"),
                                                start=(k == 0), stop=(k == FT - 1))
                    last.then_inc(y_done, 1)

                def tile(j, r):
                    up(j)
                    turn_x(j + 1, 1 - r)
                    down(j - 1)
                    turn_h(j)

                def turn_maps(s):
                    pe.wait_ge(maps_made, 1)
                    pe.wait_ge(maps_read, s)
                    for q in range(4):
                        src = y[:, TB + s, q % 2, q // 2, :]
                        nc.tensor.matmul(ps_m[0:B, q * P:(q + 1) * P], src[:, 0:B], g.ident[:], start=True, stop=True)
                        last = nc.tensor.matmul(ps_m[32:32 + B, q * P:(q + 1) * P], src[:, B:L], flip[:], start=True, stop=True)
                    last.then_inc(maps_turned, 1)

                def turn_carry():
                    pe.wait_ge(carried, 1)
                    for ri in range(2):
                        nc.tensor.matmul(ps_c[:, 0, ri * B:(ri + 1) * B], ws[0][0:B, :, ri], g.ident[0:B, 0:B],
                                         start=True, stop=True)
                        last = nc.tensor.matmul(ps_cb[:, ri * B:(ri + 1) * B], ws[0][32:32 + B, :, ri],
                                                g.ident[32:32 + B, 32:32 + B], start=True, stop=True)
                    last.then_inc(carry_back, 1)

                def tiles(j0, j1):
                    with pe.Fori(0, (j1 - j0) // 2) as k:
                        tile(k * 2 + j0, 1)
                        tile(k * 2 + j0 + 1, 0)

                pe.wait_ge(ones_made, 1)
                turn_x(0, 0)
                up(0)
                turn_x(1, 1)
                turn_h(0)
                tiles(1, MAPS_TURN)
                pe.wait_ge(const, 2)
                turn_maps(0)
                tile(MAPS_TURN, 1)
                turn_maps(1)
                tile(MAPS_TURN + 1, 0)
                tiles(MAPS_TURN + 2, RUN - 2)
                turn_carry()
                tile(RUN - 2, 1)
                pe.wait_ge(back_read, 1)
                nc.tensor.matmul(ps_c[:, 1, :], flip[:], back[:].rearrange("p r b -> p (r b)"),
                                 start=True, stop=True).then_inc(flipped, 1)
                tile(RUN - 1, 0)
                tiles(RUN, ET - 2)
                tile(ET - 2, 1)
                up(ET - 1)
                down(ET - 2)
                turn_h(ET - 1)
                down(ET - 1)

            @block.scalar
            def _(act):
                with act.Fori(0, ET) as j:
                    act.wait_ge(hidden, j + 1)
                    act.wait_ge(h_turned, j)
                    nc.scalar.activation(hid[:], ps_h[:, 0:F], ACT.Gelu_apprx_tanh).then_inc(gelu_done, 1)

            @block.vector
            def _(dve):
                v = nc.vector

                def copy_x(j):
                    dve.wait_ge(x_turned, j + 1)
                    dve.wait_ge(hidden, j)
                    v.tensor_copy(xa[:], ps_x[:, 0:P]).then_inc(xt_ready, 1)
                    v.tensor_copy(xb[0:CB, :], ps_x[0:CB, P:2 * P]).then_inc(xt_ready, 1)

                def copy_h(j):
                    dve.wait_ge(h_turned, j + 1)
                    dve.wait_ge(y_done, j)
                    v.tensor_copy(hid_t[:], ps_ht[:, 0:F]).then_inc(ht_ready, 1)

                def weigh(j):
                    e = dve.value_load(g.expert_of[0:1, ds(j, 1)], min_val=0, max_val=E - 1)
                    dve.wait_ge(y_done, j + 1)
                    dve.wait_ge(yw_ready, j)
                    v.tensor_tensor(yt[:], ps_y[:], g.b2[:, ds(e, 1), :].rearrange("p a n -> p (a n)"),
                                    ALU.add).then_inc(y_ready, 1)
                    dve.wait_ge(y_ready, j + 1)
                    dve.wait_ge(added, 16 * j)
                    v.tensor_scalar(yw[:], yt[:], g.slot_weight[:, ds(j, 1)], None, ALU.mult).then_inc(yw_ready, 1)

                def tile(j):
                    copy_x(j + 1)
                    weigh(j - 1)
                    copy_h(j)

                MAP_INCS, CARRY_INCS, RUN_INCS = 4, 7, 7
                c = Chain(dve, chained)

                def map_step(base, s):
                    chain = Tally(chained, base + s * MAP_INCS)

                    def then(ins):
                        dve.wait_ge(chained, chain.add(ins))
                    at = lambda k: y[:, ds(s + k, 1)]
                    mem = lambda ap: ap.rearrange("p a r c l -> p (a r c) l")
                    one = lambda ap: ap.rearrange("p a c l -> p (a c) l")
                    then(v.tensor_tensor(t[:].rearrange("p r c l -> p (r c) l"), mem(at(1)),
                                         a[:, :, ds(s, 1)].rearrange("p l a -> p a l").to_broadcast([P, 4, L]), ALU.mult))
                    then(v.tensor_tensor(t[:].rearrange("p r c l -> p (r c) l"), t[:].rearrange("p r c l -> p (r c) l"),
                                         mem(at(0)), ALU.subtract))
                    then(v.tensor_tensor(one(y[:, ds(s + 2, 1), 0]), t[:, 0], one(y[:, ds(s + 1, 1), 1]), ALU.add))
                    then(v.tensor_tensor(one(y[:, ds(s + 2, 1), 1]), t[:, 1], one(y[:, ds(s + 1, 1), 0]), ALU.subtract))

                def read_maps(s):
                    dve.wait_ge(maps_turned, s + 1)
                    e0 = 0 if s == 0 else 3
                    for p0 in (0, 32):
                        for q in range(4):
                            last = v.tensor_copy(maps[0][p0:p0 + B, :, 2 * (q // 2), e0 + q % 2],
                                                 ps_m[p0:p0 + B, q * P:(q + 1) * P])
                            if (p0, q) != (32, 3):
                                c.count(last)
                    last.then_inc(maps_read, 1)
                    dve.wait_ge(maps_read, s + 1)
                    c.wait()

                def times_i(l):
                    plain, turned = maps[l][:, :, 0::2, :], maps[l][:, :, 1::2, :]
                    c.count(v.tensor_copy(turned[:, :, :, 1:3], plain[:, :, :, 0:2]))
                    c.count(v.tensor_copy(turned[:, :, :, 4], plain[:, :, :, 3]))
                    c.step(v.tensor_scalar(turned[:, :, :, 0::3], plain[:, :, :, 1::3], -1.0, None, ALU.mult))

                def join(l):
                    n = P >> (l + 1)
                    left, right = maps[l][:, 0::2], maps[l][:, 1::2]
                    out = maps[l + 1][:, :, 0::2, :]
                    tmp = prod[:, 0:n]
                    for q, e in enumerate((3, 4, 0, 1)):
                        dst = out if q == 0 else tmp
                        c.step(v.tensor_tensor(dst, right[:, :, q:q + 1, :].to_broadcast([HI, n, 2, 5]),
                                               left[:, :, 0::2, e:e + 1].to_broadcast([HI, n, 2, 5]), ALU.mult))
                        if q:
                            c.step(v.tensor_tensor(out, out, tmp, ALU.add))
                    p16 = maps[l + 1][:, :, 0, 3:5]
                    c.step(v.scalar_tensor_tensor(out=mag[:, 0:n], in0=p16, scalar=-1.0, in1=p16, op0=ALU.mult, op1=ALU.max))
                    c.step(v.tensor_tensor(scale[:, 0:n], mag[:, 0:n, 0], mag[:, 0:n, 1], ALU.max))
                    c.step(v.reciprocal(scale[:, 0:n], scale[:, 0:n]))
                    c.step(v.tensor_tensor(out, out, scale[:, 0:n].unsqueeze(2).unsqueeze(3).to_broadcast([HI, n, 2, 5]),
                                           ALU.mult))
                    c.step(v.tensor_scalar(out[:, :, :, 2], out[:, :, :, 0], -1.0, None, ALU.mult))
                    times_i(l + 1)

                def carry_step(base, n):
                    chain = Tally(chained, base + n * CARRY_INCS)

                    def then(ins):
                        dve.wait_ge(chained, chain.add(ins))
                    of = lambda k: maps[LEVELS][:, ds(n, 1), k, :].rearrange("p a e -> p (a e)")
                    then(v.scalar_tensor_tensor(out=num[:], in0=of(2), scalar=w[:, 0:1], in1=of(0), op0=ALU.mult, op1=ALU.add))
                    then(v.scalar_tensor_tensor(out=nd[:], in0=of(3), scalar=w[:, 1:2], in1=num[:], op0=ALU.mult, op1=ALU.add))
                    then(v.tensor_tensor_reduce(sq[:], nd[:, 3:5], nd[:, 3:5], 1.0, 0.0, ALU.mult, ALU.add, norm[:]))
                    then(v.reciprocal(rnorm[:], norm[:]))
                    then(v.tensor_tensor_reduce(sq[:], nd[:, 0:2], nd[:, 3:5], rnorm[:, 0:1], 0.0, ALU.mult, ALU.add, w[:, 0:1]))
                    then(v.tensor_tensor_reduce(sq[:], nd[:, 1:3], nd[:, 3:5], rnorm[:, 0:1], 0.0, ALU.mult, ALU.add, w[:, 1:2]))
                    then(v.tensor_copy(ws[LEVELS][:, ds(n + 1, 1), :].rearrange("p a r -> p (a r)"), w[:]))

                def hand_down(l):
                    n = P >> (l + 1)
                    pair, first = ws[l + 1], maps[l][:, 0::2]
                    nd_, tmp, sq_, pr_, nn = wnd[:, 0:n], wtmp[:, 0:n], wsq[:, 0:n], wpr[:, 0:n], wnorm[:, 0:n]
                    c.step(v.tensor_copy(ws[l][:, 0::2, :], pair[:]))
                    for ri in range(2):
                        c.step(v.tensor_tensor(tmp, first[:, :, 2 + ri, :], pair[:, :, ri:ri + 1].to_broadcast([HI, n, 5]), ALU.mult))
                        c.step(v.tensor_tensor(nd_, tmp, first[:, :, 0, :] if ri == 0 else nd_, ALU.add))
                    c.step(v.tensor_tensor(sq_, nd_[:, :, 3:5], nd_[:, :, 3:5], ALU.mult))
                    c.step(v.tensor_tensor(nn, sq_[:, :, 0], sq_[:, :, 1], ALU.add))
                    c.step(v.reciprocal(nn, nn))
                    for ri in range(2):
                        c.step(v.tensor_tensor(pr_[:, :, ri, :], nd_[:, :, ri:ri + 2], nd_[:, :, 3:5], ALU.mult))
                    c.step(v.tensor_tensor(sq_, pr_[:, :, :, 0], pr_[:, :, :, 1], ALU.add))
                    c.step(v.tensor_tensor(ws[l][:, 1::2, :], sq_, nn.unsqueeze(2).to_broadcast([HI, n, 2]), ALU.mult))

                def run_step(base, s):
                    chain = Tally(chained, base + s * RUN_INCS)

                    def then(ins):
                        dve.wait_ge(chained, chain.add(ins))
                    re, im = (d[:, ri, ds(s, 1), :].rearrange("p a l -> p (a l)") for ri in range(2))
                    then(v.tensor_tensor(re, a[:, :, ds(s, 1)].rearrange("p l a -> p (l a)"), win[:, 0, :], ALU.subtract))
                    then(v.tensor_scalar(im, win[:, 1, :], -1.0, -1.0, ALU.mult, ALU.add))
                    both = d[:, :, ds(s, 1), :].rearrange("p r a l -> p r (a l)")
                    then(v.tensor_tensor(sqw[:], both, both, ALU.mult))
                    then(v.tensor_tensor(qw[:], sqw[:, 0, :], sqw[:, 1, :], ALU.add))
                    then(v.reciprocal(qw[:], qw[:]))
                    then(v.tensor_tensor(win[:, 0, :], re, qw[:], ALU.mult))
                    then(v.scalar_tensor_tensor(out=win[:, 1, :], in0=im, scalar=-1.0, in1=qw[:], op0=ALU.mult, op1=ALU.mult))

                def features(c):
                    for ri in range(2):
                        c.step(v.tensor_tensor(z[:, ri], d[:, ri, :, 0:B].rearrange("p s b -> p b s"),
                                               d[:, ri, ::-1, B:L].rearrange("p s b -> p b s"), ALU.add))
                    c.step(v.tensor_tensor(z[:, 0], z[:, 0], a[:, 0:B, :], ALU.subtract))
                    c.step(v.tensor_scalar(z[:, 1], z[:, 1], 1.0, None, ALU.add))
                    c.step(v.tensor_tensor(z2[:], z[:], z[:], ALU.mult))
                    c.step(v.tensor_tensor(zn[:], z2[:, 0], z2[:, 1], ALU.add))
                    c.step(v.reciprocal(zn[:], zn[:]))
                    c.step(v.tensor_tensor(z[:, 0], z[:, 0], zn[:], ALU.mult))
                    c.step(v.scalar_tensor_tensor(out=z[:, 1], in0=z[:, 1], scalar=-1.0, in1=zn[:], op0=ALU.mult, op1=ALU.mult))
                    c.step(v.tensor_scalar(z[:], z[:], FEAT_CLAMP, -FEAT_CLAMP, ALU.min, ALU.max))

                def add_features(k):
                    zf = z[:].rearrange("p r b c -> p r (b c)")
                    for ri in range(2):
                        if ri:
                            dve.wait_ge(finished, (2 * k + 1) * ADD_TILES)
                        for q in range(ADD_TILES):
                            tt = k * ADD_TILES + q
                            hr = g.h[:, ds(tt, 1), :].rearrange("p a n -> p (a n)")
                            v.scalar_tensor_tensor(out=hr, in0=rows_s[:, ri, :], scalar=zf[:, ri, ds(tt, 1)], in1=hr,
                                                   op0=ALU.mult, op1=ALU.add).then_inc(finished, 1)

                dve.wait_ge(loaded, 16)
                c.step(v.tensor_tensor(rows_s[:], rows[:, 0:3], rows[:, 3:4].to_broadcast([P, 3, C]), ALU.mult))
                c.step(v.tensor_tensor(g.b2[:], g.b2[:], rows_s[:, 2:3].to_broadcast([P, E, C]), ALU.add))
                copy_x(0)
                logit = g.logits[:, :, E].rearrange("p (b c) -> p b c", b=B)
                for lanes, src in ((a[:, 0:B, :], logit), (a[:, B:L, :], logit[:, :, ::-1])):
                    c.step(v.tensor_scalar(lanes, src, V_MAX, -V_MAX, ALU.min, ALU.max))
                c.step(v.tensor_scalar(a[:], a[:], -2.0, None, ALU.add))
                c.step(v.memset(y[:, 0:2], 0.0))
                c.step(v.memset(y[:, 0, 0, 1, :], 1.0))
                c.step(v.memset(y[:, 1, 0, 0, :], 1.0))
                copy_x(1)
                copy_h(0)
                base = c.n
                with dve.Fori(1, MAPS_TURN) as j:
                    tile(j)
                    for q in range(MAP_STEPS):
                        map_step(base, (j - 1) * MAP_STEPS + q)
                c.n = base + MAP_INCS * TB
                v.memset(w[:], 0.0).then_inc(maps_made, 1)
                for l in range(LEVELS + 1):
                    c.step(v.memset(ws[l][:], 0.0))
                c.step(v.memset(maps[0][:], 0.0))
                c.step(v.memset(maps[0][:, :, 0, 3], 1.0))
                c.step(v.memset(maps[0][:, :, 2, 0], 1.0))
                tile(MAPS_TURN)
                read_maps(0)
                tile(MAPS_TURN + 1)
                read_maps(1)
                c.step(v.tensor_scalar(maps[0][:, :, 0::2, 2], maps[0][:, :, 0::2, 0], -1.0, None, ALU.mult))
                times_i(0)
                tile(MAPS_TURN + 2)
                join(0)
                tile(MAPS_TURN + 3)
                for l in range(1, LEVELS):
                    join(l)
                base = c.n
                with dve.Fori(CARRY, HAND_DOWN) as j:
                    tile(j)
                    carry_step(base, j - CARRY)
                c.n = base + CARRY_INCS * (GROUPS - 1)
                for l in range(LEVELS - 1, -1, -1):
                    tile(HAND_DOWN + LEVELS - 1 - l)
                    hand_down(l)
                v.memset(sq[:], 0.0).then_inc(carried, 1)
                tile(RUN - 2)
                dve.wait_ge(carry_back, 1)
                c.step(v.tensor_copy(win[:, :, 0:B], ps_c[:, 0, :].rearrange("p (r b) -> p r b", r=2)))
                v.tensor_copy(back[:], ps_cb[:].rearrange("p (r b) -> p r b", r=2)).then_inc(back_read, 1)
                tile(RUN - 1)
                dve.wait_ge(flipped, 1)
                c.step(v.tensor_copy(win[:, :, B:L], ps_c[:, 1, :].rearrange("p (r b) -> p r b", r=2)))
                base = c.n
                with dve.Fori(RUN, RUN + TB) as j:
                    tile(j)
                    run_step(base, j - RUN)
                c.n = base + RUN_INCS * TB
                tile(ADD - 1)
                features(c)
                with dve.Fori(ADD, ADD_END) as j:
                    tile(j)
                    add_features(j - ADD)
                for j in range(ADD_END, ET - 1):
                    tile(j)
                weigh(ET - 2)
                copy_h(ET - 1)
                weigh(ET - 1)


def finish(nc, g, out):
    with ExitStack() as ctx:
        sem = lambda name: ctx.enter_context(nc.semaphore(name))
        part = ctx.enter_context(nc.sbuf_tensor("f_sums", [P, NCH, CT, C], F32))
        sums_in = [sem(f"f_sums_in{i}") for i in range(NCH)]
        done, stored = sem("f_done"), sem("f_stored")
        with nc.Block() as block:

            @block.sync
            def _(sp):
                for i in range(NCH):
                    sp.dma_start(part[:, i], g.sums[i * CW:(i + 1) * CW].rearrange("(t p) n -> p t n", p=P)).then_inc(sums_in[i], 16)
                for i in range(NCH):
                    b, c0 = i // QC, (i % QC) * CT
                    sp.wait_ge(done, i + 1)
                    sp.dma_start(out[b].rearrange("(p c) n -> p c n", c=TB)[:, c0:c0 + CT, :],
                                 g.h[:, i * CT:(i + 1) * CT, :]).then_inc(stored, 16)
                sp.wait_ge(stored, 16 * NCH)

            @block.vector
            def _(dve):
                for i in range(NCH):
                    dve.wait_ge(sums_in[i], 16)
                    hc = g.h[:, i * CT:(i + 1) * CT, :]
                    nc.vector.tensor_tensor(hc, hc, part[:, i], ALU.add).then_inc(done, 1)


def build(nc, x, tok_table, pos_rev, pos_rev_t, carry_t, w_qkv, w_out, gate_rows, gate_bias, w1, b1, w2, b2_rows,
          out_rows, out):
    g = Chip()
    g.qk_parts = nc.dram_tensor("qk_parts", [3, 2 * C, N], BF16)
    g.x2_rows = nc.dram_tensor("x2_rows", [N + P, C], F32)
    g.sums = nc.dram_tensor("expert_sums", [N + P, C], F32)
    with ExitStack() as keep:
        sb = lambda ctx, name, shape, dt=F32: ctx.enter_context(nc.sbuf_tensor(name, shape, dt))
        g.ident = sb(keep, "ident", [P, P])
        g.h = sb(keep, "h", [P, NT, C])
        g.logits = sb(keep, "logits", [P, NT, E + 1])
        g.expert_of = sb(keep, "expert_of", [P, ET], I32)
        g.slot_token = sb(keep, "slot_token", [P, ET], I32)
        g.slot_weight = sb(keep, "slot_weight", [P, ET])
        g.mixed = sb(keep, "mixed_all", [P, NG, S])
        with ExitStack() as attn:
            g.spread = sb(attn, "spread", [P, P])
            g.v = sb(attn, "v_all", [P, NT, C])
            embed_and_project(nc, g, x, tok_table, pos_rev, pos_rev_t, carry_t, w_qkv)
            attention(nc, g)
        g.b2 = sb(keep, "b2_all", [P, E, C])
        g.w1_a, g.w1_b = sb(keep, "w1_a", [P, E, F]), sb(keep, "w1_b", [CB + 1, E, F])
        g.w2 = sb(keep, "w2_all", [P, E, F // P, C])
        mix_heads_and_gate(nc, g, w_out, gate_rows, gate_bias, w1, b1, b2_rows)
        route(nc, g, w2)
        experts_and_spectrum(nc, g, out_rows)
        finish(nc, g, out)


def kernel(**inputs):
    import numpy as _np
    import concourse.bacc as _bacc
    from concourse import mybir as _mybir
    from concourse.bass_utils import run_bass_kernel_spmd as _run

    I = {k: _np.asarray(v) for k, v in inputs.items()}
    pos = I["L0_tok_pos_table"][::-1]
    feeds = {
        "x": I["x"],
        "tok_table": I["L0_tok_tok_table"],
        "pos_rev": pos,
        "pos_rev_t": pos.T,
        "carry_t": I["L0_tok_carry_W"].T,
        "w_qkv": I["L0_attn_w_qkv"],
        "w_out": I["L0_attn_w_out"],
        "gate_rows": _np.concatenate([I["L0_ffn_gate_w"], I["L0_ffn_v_w"][:, None]], axis=1),
        "gate_bias": _np.concatenate([I["L0_ffn_gate_b"], I["L0_ffn_v_b"].reshape(1)])[None, :],
        "w1": I["L0_ffn_w1"],
        "b1": I["L0_ffn_b1"],
        "w2": I["L0_ffn_w2"],
        "b2_rows": I["L0_ffn_b2"].reshape(1, -1),
        "out_rows": _np.concatenate([I["L0_ffn_out_w"], I["L0_ffn_out_b"][None], I["L0_ffn_bk_scale"][None]]).reshape(1, -1),
    }
    nc = _bacc.Bacc("TRN2", target_bir_lowering=False, num_devices=1)
    arrays, args = {}, []
    for name, a in feeds.items():
        a = _np.ascontiguousarray(a)
        arrays[f"in_{name}_dram"] = a
        args.append(nc.dram_tensor(f"in_{name}_dram", a.shape, _mybir.dt.from_np(a.dtype), kind="ExternalInput").ap())
    args.append(nc.dram_tensor("out_0_dram", (B, S, C), _mybir.dt.from_np(_np.dtype("float32")), kind="ExternalOutput").ap())
    build(nc, *args)
    r = _run(nc, [arrays], core_ids=[0])
    return r.results[0]["out_0_dram"]
```

```python
import numpy as np

import concourse.bass as bass
from concourse import mybir
from contextlib import ExitStack

F32 = mybir.dt.float32
BF16 = mybir.dt.bfloat16
I32 = mybir.dt.int32
ALU = mybir.AluOpType
ACT = mybir.ActivationFunctionType
AX = mybir.AxisListType

P = 128
B, S, C = 2, 2048, 192
H, D = 12, 16
E, F = 8, 768
N = B * S
CB = C - P
TB = S // P
NT = B * TB
CT = 4
CW = CT * P
NCH = N // CW
QC = S // CW
HG = 4
NG = B * (H // HG)
STEPS = NG * QC
STEPS_B = STEPS // B
KT = S // P
ET = (2 * N + E * (P - 1)) // P
EPS = 1e-5
SCALE = float(C) ** -0.5
V_MAX = 3.0
FEAT_CLAMP = 10.0

Q_PIECE = [0, 0, 0, 1, 1, 2]
K_PIECE = [0, 1, 2, 0, 1, 0]
KR = len(Q_PIECE) * D
MR = 3


class Tally:

    def __init__(self, sem, base=0):
        self.sem, self.base, self.n = sem, base, 0

    def add(self, ins, k=1):
        ins.then_inc(self.sem, k)
        self.n += k
        return self.base + self.n


def ds(start, n):
    return bass.ds(start, n)


def hold(eng, sem, value):
    eng.wait_ge(sem, value)
    eng.nop(nofuse=True)


class Chip:
    pass


def start_k(sp, g, gg):
    row = C + (gg % (NG // B)) * HG * D
    col = (gg // (NG // B)) * S
    for n, part in enumerate(K_PIECE):
        sp.dma_start(g.k6[n * D:(n + 1) * D, ds(gg % 2, 1), :, :].rearrange("r a h n -> r (a h) n"),
                     g.qk_parts[part, ds(row, HG * D), ds(col, S)].rearrange("(h r) n -> r h n", r=D)
                     ).then_inc(g.k_in, 16)


def start_q(sp, g, i):
    row = ((i // QC) % (NG // B)) * HG * D
    col = (i // STEPS_B) * S + (i % QC) * CW
    for n, part in enumerate(Q_PIECE):
        sp.dma_start(g.q6[n * D:(n + 1) * D, ds(i % 4, 1), :, :].rearrange("r a h n -> r (a h) n"),
                     g.qk_parts[part, ds(row, HG * D), ds(col, CW)].rearrange("(h r) n -> r h n", r=D)
                     ).then_inc(g.q_in, 16)


def embed_and_project(nc, g, x, tok_table, pos_rev, pos_rev_t, carry_t, w_qkv):
    with ExitStack() as ctx:
        sb = lambda name, shape, dt=F32: ctx.enter_context(nc.sbuf_tensor(name, shape, dt))
        ps = lambda name, shape, dt=F32: ctx.enter_context(nc.psum_tensor(name, shape, dt))
        sem = lambda name: ctx.enter_context(nc.semaphore(name))

        idx = sb("token_ids", [P, B, TB], I32)
        wqk_a, wqk_b = sb("wqk_a", [P, 2 * C]), sb("wqk_b", [CB, 2 * C])
        ct_a, ct_b = sb("carry_a", [P, C]), sb("carry_b", [CB, C])
        prt_a, prt_b = sb("pos_t_a", [P, 16]), sb("pos_t_b", [CB, 16])
        room = g.mixed[:].rearrange("p a n -> p (a n)")
        prow, pos = (room[:, k * TB * C:(k + 1) * TB * C].rearrange("p (c n) -> p c n", c=TB) for k in range(2))
        zt_a, zt_b = sb("high_digit_a", [P, 8]), sb("high_digit_b", [CB, 8])
        yt_a, yt_b = sb("two_digits_a", [P, 8, 16]), sb("two_digits_b", [CB, 8, 16])
        stats = sb("ln_stats", [P, CT, 6])
        mv = sb("ln_mean_var", [P, CT, 2])
        ve = sb("ln_var_eps", [P, CT])
        sd = sb("ln_sd", [P, CT])
        rstd = sb("ln_rstd", [P, CT])
        x1 = sb("x1", [P, 2, CT, C])
        xa, xb = sb("x1_t_a", [P, 2, CW]), sb("x1_t_b", [CB, 2, CW])
        parts = sb("qk_parts_sb", [P, 2, 3, 3, CW], BF16)
        rem = sb("qk_rem", [P, 3, CW])

        ps_ta, ps_tb = ps("ps_ta", [P, CW]), ps("ps_tb", [CB, CW])
        ps_qk = [ps(f"ps_qk{m}", [P, CW]) for m in range(3)]
        ps_v = [ps(f"ps_v{m}", [P, 2 * C]) for m in range(2)]

        loaded, pos_loaded = sem("a_loaded"), sem("a_pos_loaded")
        prow_in, prow_rest_in = sem("a_pos_rows_in"), sem("a_pos_rows_rest_in")
        ids_in = sem("a_ids_in")
        gathered = [sem("a_gathered0"), sem("a_gathered1")]
        const_made = sem("a_const_made")
        pe_pos = sem("a_pe_pos")
        act_pos = sem("a_act_pos")
        v_chain = sem("a_v_chain")
        pos_ready = sem("a_pos_ready")
        pos_made = sem("a_pos_made")
        var_ready = sem("a_var_ready")
        sd_ready = sem("a_sd_ready")
        x1_ready = sem("a_x1_ready")
        turned = sem("a_turned")
        xt_ready = sem("a_xt_ready")
        projected = sem("a_projected")
        v_projected = sem("a_v_projected")
        piece1 = sem("a_piece1")
        rem1 = sem("a_rem1")
        piece2 = sem("a_piece2")
        piece3 = sem("a_piece3")
        v_copied = sem("a_v_copied")
        stored = sem("a_stored")

        with nc.Block() as block:

            @block.sync
            def _(sp):
                sp.dma_start(idx[:], x.rearrange("b (p c) -> p b c", c=TB)).then_inc(ids_in, 16)
                for dst, src in ((ct_a[:], carry_t[0:P]), (ct_b[:], carry_t[P:C]), (prt_a[:], pos_rev_t[0:P]),
                                 (prt_b[:], pos_rev_t[P:C])):
                    sp.dma_start(dst, src).then_inc(pos_loaded, 16)
                def load_rows(q, done):
                    sp.dma_start(prow[:, q * CT:(q + 1) * CT].rearrange("p c n -> p (c n)"),
                                 pos_rev[q * CT:(q + 1) * CT].rearrange("(a c) n -> a (c n)", a=1).to_broadcast([P, CT * C])
                                 ).then_inc(done, 16)

                load_rows(0, prow_in)
                for dst, src in ((wqk_a[:], w_qkv[0:P, 0:2 * C]), (wqk_b[:], w_qkv[P:C, 0:2 * C])):
                    sp.dma_start(dst, src).then_inc(loaded, 16)
                for q in range(1, QC):
                    load_rows(q, prow_rest_in)

                def store(i):
                    for m in range(3):
                        sp.wait_ge(piece1, 3 * i + m + 1)
                        sp.wait_ge(piece2, 3 * i + m + 1)
                        sp.wait_ge(piece3, 3 * i + m + 1)
                        sp.dma_start(g.qk_parts[:, P * m:P * (m + 1), ds(i * CW, CW)].rearrange("t p n -> p t n"),
                                     parts[:, ds(i % 2, 1), m].rearrange("p a t n -> p (a t) n")).then_inc(stored, 16)
                    hold(sp, stored, 48 * i + 48)

                with sp.Fori(0, QC) as i:
                    store(i)
                start_k(sp, g, 0)
                start_q(sp, g, 0)
                with sp.Fori(QC, NCH) as i:
                    store(i)

            @block.gpsimd
            def _(pool):
                pool.memset(g.ident[:], 0.0).then_inc(const_made, 1)
                pool.memset(g.spread[:], 0.0).then_inc(const_made, 1)
                pool.wait_ge(const_made, 2)
                pool.affine_select(out=g.ident[:], in_=g.ident[:], compare_op=ALU.not_equal, fill=1.0, base=0,
                                   pattern=[[-1, P]], channel_multiplier=1).then_inc(const_made, 1)
                sel = g.spread[:].rearrange("p (h r) -> p h r", h=HG)
                pool.affine_select(out=sel, in_=sel, compare_op=ALU.not_equal, fill=1.0, base=-D,
                                   pattern=[[-32, HG], [0, 32]], channel_multiplier=1).then_inc(const_made, 1)
                pool.wait_ge(ids_in, 16)
                for i in range(NCH):
                    if i >= 2:
                        pool.wait_ge(gathered[i % 2], 16 * CT * (i // 2))
                    for t in range(CT * i, CT * (i + 1)):
                        pool.indirect_dma_start(
                            out=g.h[:, t, :], out_offset=None, in_=tok_table,
                            in_offset=bass.IndirectOffsetOnAxis(ap=idx[:, t // TB, t % TB:t % TB + 1], axis=0),
                        ).then_inc(gathered[i % 2], 16)

            @block.tensor
            def _(pe):
                pe.wait_ge(pos_loaded, 16 * 4)
                pe.wait_ge(const_made, 4)
                for dst, m0, m1 in ((ps_ta[:, 0:8], 0, P), (ps_tb[:, 0:8], P, C)):
                    nc.tensor.matmul(dst, ct_a[:, m0:m1], prt_a[:, 8:16], start=True, stop=False)
                    nc.tensor.matmul(dst, ct_b[:, m0:m1], prt_b[:, 8:16], start=False, stop=True).then_inc(pe_pos, 1)
                pe.wait_ge(pos_ready, 2)
                nc.tensor.matmul(ps_v[0][:, 0:C], yt_a[:].rearrange("p a r -> p (a r)"), ct_a[:], start=True, stop=False)
                nc.tensor.matmul(ps_v[0][:, 0:C], yt_b[:].rearrange("p a r -> p (a r)"), ct_b[:], start=False,
                                 stop=True).then_inc(pe_pos, 1)

                def turn_x(i, r):
                    pe.wait_ge(x1_ready, i + 1)
                    pe.wait_ge(xt_ready, 2 * i)
                    for j in range(CT):
                        nc.tensor.transpose(ps_ta[:, j * P:(j + 1) * P], x1[:, r, j, 0:P], g.ident[:])
                        last = nc.tensor.transpose(ps_tb[:, j * P:(j + 1) * P], x1[:, r, j, P:C], g.ident[:])
                    last.then_inc(turned, 1)

                def project(i, r, first=False, more=True):
                    pe.wait_ge(xt_ready, 2 * i + 2)
                    for m in range(3):
                        if not first:
                            pe.wait_ge(rem1, 3 * (i - 1) + m + 1)
                        nc.tensor.matmul(ps_qk[m][:], wqk_a[:, m * P:(m + 1) * P], xa[:, r], start=True, stop=False)
                        nc.tensor.matmul(ps_qk[m][:], wqk_b[:, m * P:(m + 1) * P], xb[:, r], start=False,
                                         stop=True).then_inc(projected, 1)
                    if more:
                        turn_x(i + 1, 1 - r)
                    pe.wait_ge(v_copied, 2 * i)
                    if first:
                        pe.wait_ge(pos_made, QC)
                    for j in range(CT):
                        dst = ps_v[j // 2][:, (j % 2) * C:(j % 2 + 1) * C]
                        nc.tensor.matmul(dst, xa[:, r, j * P:(j + 1) * P], wqk_a[:, C:2 * C], start=True, stop=False)
                        last = nc.tensor.matmul(dst, xb[:, r, j * P:(j + 1) * P], wqk_b[:, C:2 * C], start=False, stop=True)
                    last.then_inc(v_projected, 1)

                turn_x(0, 0)
                pe.wait_ge(loaded, 16 * 2)
                project(0, 0, first=True)
                with pe.Fori(0, (NCH - 2) // 2) as k:
                    project(k * 2 + 1, 1)
                    project(k * 2 + 2, 0)
                project(NCH - 1, 1, more=False)

            @block.scalar
            def _(act):
                act.wait_ge(pe_pos, 1)
                nc.scalar.activation(zt_a[:], ps_ta[:, 0:8], ACT.Copy).then_inc(act_pos, 1)
                act.wait_ge(pe_pos, 2)
                nc.scalar.activation(zt_b[:], ps_tb[:, 0:8], ACT.Copy).then_inc(act_pos, 1)

                def root(i):
                    act.wait_ge(var_ready, i + 1)
                    nc.scalar.activation(sd[:], ve[:], ACT.Sqrt).then_inc(sd_ready, 1)

                def copy_x(i):
                    act.wait_ge(turned, i + 1)
                    if not isinstance(i, int):
                        act.wait_ge(v_projected, i - 1)
                    row = lambda a: a[:, ds(i % 2, 1), :].rearrange("p a n -> p (a n)")
                    nc.scalar.activation(row(xa), ps_ta[:], ACT.Copy).then_inc(xt_ready, 1)
                    nc.scalar.activation(row(xb), ps_tb[:], ACT.Copy).then_inc(xt_ready, 1)

                def chunk(i, first=False, more=True):
                    part = lambda m, n: parts[:, ds(i % 2, 1), m, n, :].rearrange("p a n -> p (a n)")
                    if more:
                        root(i + 1)
                    if not first:
                        act.wait_ge(stored, 48 * (i - 1))
                    for m in range(3):
                        act.wait_ge(projected, 3 * i + m + 1)
                        nc.scalar.activation(part(m, 0), ps_qk[m][:], ACT.Copy).then_inc(piece1, 1)
                    if more:
                        copy_x(i + 1)
                    for m in range(3):
                        act.wait_ge(rem1, 3 * i + m + 1)
                        nc.scalar.activation(part(m, 1), rem[:, m, :], ACT.Copy).then_inc(piece2, 1)
                    act.wait_ge(v_projected, i + 1)
                    for m in range(2):
                        nc.scalar.activation(g.v[:, ds(CT * i + 2 * m, 2), :],
                                             ps_v[m][:].rearrange("p (j n) -> p j n", j=2), ACT.Copy).then_inc(v_copied, 1)

                root(0)
                copy_x(0)
                chunk(0, first=True)
                with act.Fori(1, NCH - 1) as i:
                    chunk(i)
                chunk(NCH - 1, more=False)

            @block.vector
            def _(dve):
                for k, (dst, z, r, n) in enumerate(((yt_a, zt_a, prt_a, P), (yt_b, zt_b, prt_b, CB))):
                    dve.wait_ge(act_pos, k + 1)
                    dve.wait_ge(pos_loaded, 16 * 4)
                    nc.vector.tensor_tensor(dst[:], z[:].unsqueeze(2).to_broadcast([n, 8, 16]),
                                            r[:].unsqueeze(1).to_broadcast([n, 8, 16]), ALU.add).then_inc(pos_ready, 1)
                dve.wait_ge(pe_pos, 3)

                def make_pos(q):
                    nc.vector.tensor_tensor(pos[:, q * CT:(q + 1) * CT],
                                            ps_v[0][:, 0:C].unsqueeze(1).to_broadcast([P, CT, C]),
                                            prow[:, q * CT:(q + 1) * CT], ALU.add).then_inc(pos_made, 1)

                dve.wait_ge(prow_in, 16)
                make_pos(0)
                per_turn = 9 + CT

                def embed(i, r):
                    chain = Tally(v_chain, i * per_turn)
                    dve.wait_ge(gathered[r], (i - r) * 8 * CT + 16 * CT)
                    hc = g.h[:, ds(CT * i, CT), :]
                    n = chain.add(nc.vector.tensor_tensor(hc, hc, pos[:, ds((i % QC) * CT, CT), :], ALU.add))
                    hold(dve, chain.sem, n)
                    for j in range(CT):
                        n = chain.add(nc.vector.bn_stats(stats[:, j, :], g.h[:, ds(CT * i + j, 1), :]
                                                         .rearrange("p a n -> p (a n)")))
                    hold(dve, chain.sem, n)
                    for j in range(CT):
                        n = chain.add(nc.vector.bn_aggr(mv[:, j, :], stats[:, j, :]))
                    dve.wait_ge(chain.sem, n)
                    nc.vector.tensor_scalar_add(ve[:], mv[:, :, 1], EPS).then_inc(var_ready, 1)
                    dve.wait_ge(sd_ready, i + 1)
                    n = chain.add(nc.vector.reciprocal(rstd[:], sd[:]))
                    dve.wait_ge(chain.sem, n)
                    if not isinstance(i, int):
                        dve.wait_ge(turned, i - 1)
                    for j in range(CT):
                        ins = nc.vector.tensor_scalar(x1[:, r, j, :], g.h[:, ds(CT * i + j, 1), :]
                                                      .rearrange("p a n -> p (a n)"),
                                                      mv[:, j, 0:1], rstd[:, j:j + 1], ALU.subtract, ALU.mult)
                        if j < CT - 1:
                            chain.add(ins)
                        else:
                            ins.then_inc(x1_ready, 1)
                    assert chain.n == per_turn

                def cut(i, r):
                    dve.wait_ge(piece3, 3 * i)
                    for m in range(3):
                        dve.wait_ge(piece1, 3 * i + m + 1)
                        nc.vector.tensor_tensor(rem[:, m, :], ps_qk[m][:], parts[:, r, m, 0, :],
                                                ALU.subtract).then_inc(rem1, 1)
                    for m in range(3):
                        dve.wait_ge(piece2, 3 * i + m + 1)
                        nc.vector.tensor_tensor(parts[:, r, m, 2, :], rem[:, m, :], parts[:, r, m, 1, :],
                                                ALU.subtract).then_inc(piece3, 1)

                dve.wait_ge(pos_made, 1)
                embed(0, 0)
                dve.wait_ge(prow_rest_in, 16 * (QC - 1))
                for q in range(1, QC):
                    make_pos(q)
                dve.wait_ge(pos_made, QC)
                embed(1, 1)
                cut(0, 0)
                with dve.Fori(0, (NCH - 2) // 2) as k:
                    embed(k * 2 + 2, 0)
                    cut(k * 2 + 1, 1)
                    embed(k * 2 + 3, 1)
                    cut(k * 2 + 2, 0)
                cut(NCH - 1, 1)


def attention(nc, g, w_out, gate_rows, gate_bias):
    TURN = KT * HG
    SWEEP = 2 * KT
    HALF = S // 2
    LEAD = KT // 2

    with ExitStack() as ctx:
        sb = lambda name, shape, dt=F32: ctx.enter_context(nc.sbuf_tensor(name, shape, dt))
        ps = lambda name, shape, dt=F32: ctx.enter_context(nc.psum_tensor(name, shape, dt))
        sem = lambda name: ctx.enter_context(nc.semaphore(name))

        k6, q6 = g.k6, g.q6
        probs = sb("probs", [P, 2, HG, CW])
        vcur = sb("v_group", [P, KT, HG, 2 * D])
        half_max = sb("half_max", [P, KT, 2])
        row_max = sb("row_max", [P, KT])
        neg = sb("neg_rest", [KT, P])
        neg_parts = sb("neg_max_parts", [KT, 3, P], BF16)
        mixed = sb("mixed", [P, CW])
        zeros = sb("zero_rows", [P, C])
        sums, inv = sb("weight_sums", [P, CW // 32]), sb("inv_sums", [P, CW // 32])
        inv_rows = sb("inv_sum_rows", [P, CW])

        ps_score = [ps(f"ps_score{k}", [P, CW]) for k in range(2)]
        ps_sweep = [ps(f"ps_sweep{k}", [P, HALF]) for k in range(2)]
        ps_out = ps("ps_out", [P, CW])
        ps_misc = ps("ps_misc", [P, CW])

        k_in, q_in, m_in = g.k_in, g.q_in, sem("b_m_in")
        ones_made = sem("b_ones_made")
        zeros_made, sums_zeroed, weights_in = sem("b_zeros_made"), sem("b_sums_zeroed"), sem("b_weights_in")
        scored = sem("b_scored")
        score_slots = sem("b_score_slots")
        prob_slots = sem("b_prob_slots")
        swept = sem("b_swept")
        sweep_slots = sem("b_sweep_slots")
        max_ready = sem("b_max_ready")
        max_turned = sem("b_max_turned")
        neg_chain = sem("b_neg_chain")
        neg_ready = sem("b_neg_ready")
        v_ready = sem("b_v_ready")
        out_copied = sem("b_out_copied")
        sums_in, inv_ready, inv_back = sem("b_sums_in"), sem("b_inv_ready"), sem("b_inv_back")
        spread = sem("b_spread")
        normed = sem("b_normed")

        def load_k(sp, gg):
            start_k(sp, g, gg)
            hold(sp, k_in, (gg + 1) * 96)

        def load_q(sp, i):
            start_q(sp, g, i)
            hold(sp, q_in, (i + 1) * 96)


        def roomy(i, kt):
            return isinstance(i, int) and i * KT + kt >= (STEPS - 1) * KT - LEAD

        def score_bank(i, kt, h):
            if roomy(i, kt) and h >= 2:
                return ps_sweep[h % 2][:, 0:CW]
            return ps_score[h % 2][:]

        def invert_sums(sp, m):
            hold(sp, out_copied, m + 1)
            for h in range(HG):
                sp.dma_start(sums[32 * h:32 * (h + 1), :], mixed[32 * h + D:32 * h + D + 1, :]).then_inc(sums_in, 16)
            hold(sp, inv_ready, m + 1)
            hold(sp, spread, m)
            for h in range(HG):
                sp.dma_start(inv_rows[32 * h + D:32 * h + D + 1, :], inv[32 * h:32 * (h + 1), :]).then_inc(inv_back, 16)

        with nc.Block() as block:

            @block.sync
            def _(sp):
                sp.wait_ge(k_in, 96)
                sp.wait_ge(q_in, 96)
                load_q(sp, 1)
                load_k(sp, 1)
                load_q(sp, 2)
                load_q(sp, 3)
                sp.wait_ge(zeros_made, 2)
                sp.dma_start(g.sums[0:N].rearrange("(t p) n -> p t n", p=P),
                             zeros[:].unsqueeze(1).to_broadcast([P, NT, C])).then_inc(sums_zeroed, 16)
                sp.dma_start(g.sums[N:N + P], zeros[:]).then_inc(sums_zeroed, 16)
                sp.dma_start(g.x2_rows[N:N + P], zeros[:]).then_inc(sums_zeroed, 16)
                for h in range(HG):
                    sp.dma_start(g.w_out[32 * h:32 * h + D],
                                 w_out.rearrange("(a h r) n -> h r a n", h=HG, r=D)[h]).then_inc(weights_in, 16)
                sp.dma_start(g.gate_w_a[:], gate_rows[0:P]).then_inc(weights_in, 16)
                sp.dma_start(g.gate_w_b[:], gate_rows[P:C]).then_inc(weights_in, 16)
                sp.dma_start(g.gate_b[:], gate_bias.to_broadcast([P, E + 1])).then_inc(weights_in, 16)

                def turn(i):
                    hold(sp, scored, (i - 3) * TURN)
                    load_q(sp, i)
                    invert_sums(sp, i - 4)

                with sp.Fori(1, NG - 1) as gg:
                    for r in range(QC):
                        turn(gg * QC + r)
                    load_k(sp, gg + 1)
                with sp.Fori(STEPS - QC, STEPS) as i:
                    turn(i)
                with sp.Fori(STEPS - QC, STEPS - 1) as i:
                    invert_sums(sp, i)
                sp.wait_ge(sums_zeroed, 48)
                sp.wait_ge(weights_in, 16 * 7)

            @block.gpsimd
            def _(pool):
                pool.memset(vcur[:, :, :, D:2 * D], 1.0).then_inc(ones_made, 1)
                pool.memset(inv_rows[:], 0.0).then_inc(ones_made, 1)
                pool.memset(zeros[:], 0.0).then_inc(zeros_made, 1)
                pool.memset(g.w_out[:], 0.0).then_inc(zeros_made, 1)

                def neg_rows(i):
                    pool.wait_ge(neg_ready, i + 1)
                    for part in range(MR):
                        pool.dma_start(q6[KR + part:KR + part + 1, ds(i % 4, 1), :, :].rearrange("r a h n -> r (a h n)"),
                                       neg_parts[:, part, :]).then_inc(m_in, 16)

                def copy_v(i, kt):
                    b, hg = i // STEPS_B, (i // QC) % (NG // B)
                    pool.tensor_copy(vcur[:, kt, :, 0:D],
                                     g.v[:, ds(b * TB + kt, 1), ds(hg * HG * D, HG * D)]
                                     .rearrange("p a (h d) -> p (a h) d", h=HG)).then_inc(v_ready, 1)

                for kt in range(KT):
                    copy_v(0, kt)
                pool.wait_ge(v_ready, KT)
                pool.memset(k6[KR:KR + MR, :, :, :], 1.0).then_inc(ones_made, 1)
                pool.wait_ge(ones_made, 3)
                neg_rows(0)

                with pool.Fori(0, STEPS - 1) as i:
                    for kt in range(KT):
                        pool.wait_ge(prob_slots, 2 + i * KT + kt + 1)
                        copy_v(i + 1, kt)
                        if kt == 11:
                            neg_rows(i + 1)

            @block.tensor
            def _(pe):
                def score(i, kt, h):
                    u = i * TURN + kt * HG + h
                    if not roomy(i, kt):
                        pe.wait_ge(score_slots, u + 1)
                    elif roomy(i, kt - 1):
                        pe.wait_ge(score_slots, u - 1)
                    elif h < 2:
                        pe.wait_ge(score_slots, u + 1)
                    else:
                        pe.wait_ge(sweep_slots, 2 + STEPS * SWEEP)
                    nc.tensor.matmul(score_bank(i, kt, h),
                                     k6[0:KR + MR, ds((i // QC) % 2, 1), h, kt * P:(kt + 1) * P].rearrange("p a n -> p (a n)"),
                                     q6[0:KR + MR, ds(i % 4, 1), h, :].rearrange("p a n -> p (a n)"),
                                     start=True, stop=True).then_inc(scored, 1)

                def sweep(i, kt):
                    h, t = kt // CT, kt % CT
                    for half in range(2):
                        pe.wait_ge(sweep_slots, i * SWEEP + 2 * kt + half + 1)
                        for c in range(2):
                            k0 = half * HALF + c * CW
                            ins = nc.tensor.matmul(ps_sweep[half][:, c * CW:(c + 1) * CW],
                                                   q6[0:KR, ds(i % 4, 1), h, t * P:(t + 1) * P].rearrange("p a n -> p (a n)"),
                                                   k6[0:KR, ds((i // QC) % 2, 1), h, k0:k0 + CW].rearrange("p a n -> p (a n)"),
                                                   start=True, stop=True)
                        ins.then_inc(swept, 1)

                def mix(i, kt):
                    pe.wait_ge(score_slots, 2 + i * TURN + (kt + 1) * HG)
                    pe.wait_ge(v_ready, i * KT + kt + 1)
                    if kt == 0:
                        pe.wait_ge(out_copied, i)
                    for h in range(HG):
                        ins = nc.tensor.matmul(ps_out[32 * h:32 * (h + 1), :], vcur[:, kt, h, :], probs[:, kt % 2, h, :],
                                               start=(kt == 0), stop=(kt == KT - 1))
                    ins.then_inc(prob_slots, 1)

                def turn_max(i):
                    pe.wait_ge(max_ready, i + 1)
                    nc.tensor.transpose(ps_misc[0:KT, 0:P], row_max[:], g.ident[:]).then_inc(max_turned, 1)

                def spread_sums(i):
                    pe.wait_ge(inv_back, 64 * (i + 1))
                    nc.tensor.matmul(ps_misc[:], g.spread[:], inv_rows[:], start=True, stop=True).then_inc(spread, 1)

                def turn(i, first=False, ahead=2):
                    pe.wait_ge(m_in, (i + 1) * 48)
                    for kt in range(KT):
                        early = 4 if roomy(i, kt) else 2
                        for h in range(early):
                            score(i, kt, h)
                        if kt > 0:
                            mix(i, kt - 1)
                        elif not first:
                            mix(i - 1, KT - 1)
                        for h in range(early, HG):
                            score(i, kt, h)
                        if kt < KT - LEAD:
                            if ahead >= 1:
                                sweep(i + 1, kt + LEAD)
                        elif ahead == 2:
                            if kt == KT - LEAD:
                                pe.wait_ge(q_in, (i + 3) * 96)
                                pe.wait_ge(k_in, ((i + 2) // QC + 1) * 96)
                            sweep(i + 2, kt - (KT - LEAD))
                        if kt == 6 and not first:
                            pe.wait_ge(neg_ready, i + 1)
                            spread_sums(i - 1)
                        if kt == 10 and ahead >= 1:
                            if not first:
                                pe.wait_ge(normed, 2 * i)
                            turn_max(i + 1)

                pe.wait_ge(k_in, 96)
                pe.wait_ge(q_in, 96)
                for kt in range(KT):
                    sweep(0, kt)
                pe.wait_ge(q_in, 192)
                for kt in range(LEAD):
                    sweep(1, kt)
                    if kt == 1:
                        turn_max(0)
                pe.wait_ge(ones_made, 3)
                turn(0, first=True)
                with pe.Fori(0, (STEPS - 4) // 2) as k:
                    turn(k * 2 + 1)
                    turn(k * 2 + 2)
                turn(STEPS - 3)
                turn(STEPS - 2, ahead=1)
                turn(STEPS - 1, ahead=0)
                mix(STEPS - 1, KT - 1)
                pe.wait_ge(out_copied, STEPS)
                nc.tensor.matmul(ps_misc[:], g.spread[:], mixed[:], start=True, stop=True).then_inc(spread, 1)

            @block.scalar
            def _(act):
                act.sem_inc(score_slots, 2)

                def copy_out(i):
                    act.wait_ge(prob_slots, 2 + (i + 1) * KT)
                    act.wait_ge(normed, 2 * i)
                    nc.scalar.activation(mixed[:], ps_out[:], ACT.Copy).then_inc(out_copied, 1)

                def turn(i, first=False):
                    for kt in range(KT):
                        act.wait_ge(prob_slots, i * KT + kt + 1)
                        for h in range(HG):
                            act.wait_ge(scored, i * TURN + kt * HG + h + 1)
                            nc.scalar.activation(probs[:, kt % 2, h, :], score_bank(i, kt, h), ACT.Exp,
                                                 scale=SCALE).then_inc(score_slots, 1)
                        if kt == 0 and not first:
                            copy_out(i - 1)

                turn(0, first=True)
                turn(1)
                with act.Fori(1, STEPS // 2 - 1) as k:
                    turn(k * 2)
                    turn(k * 2 + 1)
                turn(STEPS - 2)
                turn(STEPS - 1)
                copy_out(STEPS - 1)

            @block.vector
            def _(dve):
                dve.sem_inc(sweep_slots, 2)
                dve.sem_inc(prob_slots, 2)

                def row_tile(i, kt):
                    if kt == 0:
                        dve.wait_ge(max_ready, i)
                    for half in range(2):
                        dve.wait_ge(swept, i * SWEEP + 2 * kt + half + 1)
                        nc.vector.tensor_reduce(half_max[:, kt, half:half + 1], ps_sweep[half][:], AX.X,
                                                ALU.max).then_inc(sweep_slots, 1)

                def whole_rows(i):
                    dve.wait_ge(sweep_slots, 2 + (i + 1) * SWEEP)
                    dve.wait_ge(max_turned, i)
                    nc.vector.tensor_reduce(row_max[:], half_max[:], AX.X, ALU.max).then_inc(max_ready, 1)

                def cut_max(i, first_half):
                    chain = Tally(neg_chain, i * 3 + (0 if first_half else 2))
                    mt = ps_misc[0:KT, 0:P]
                    if first_half:
                        dve.wait_ge(max_turned, i + 1)
                        dve.wait_ge(m_in, i * 48)
                        n = chain.add(nc.vector.tensor_scalar(neg_parts[:, 0, :], mt, -1.0, None, ALU.mult))
                        dve.wait_ge(neg_chain, n)
                        n = chain.add(nc.vector.scalar_tensor_tensor(out=neg[:], in0=mt, scalar=-1.0, in1=neg_parts[:, 0, :],
                                                                     op0=ALU.mult, op1=ALU.subtract))
                        dve.wait_ge(neg_chain, n)
                    else:
                        n = chain.add(nc.vector.tensor_copy(neg_parts[:, 1, :], neg[:]))
                        dve.wait_ge(neg_chain, n)
                        nc.vector.tensor_tensor(neg_parts[:, 2, :], neg[:], neg_parts[:, 1, :],
                                                ALU.subtract).then_inc(neg_ready, 1)

                def invert(i):
                    dve.wait_ge(sums_in, 64 * (i + 1))
                    dve.wait_ge(inv_back, 64 * i)
                    nc.vector.reciprocal(inv[:], sums[:]).then_inc(inv_ready, 1)

                def normalise(i, half):
                    dve.wait_ge(spread, i + 1)
                    h0, w = half * (CW // 2), CW // 2
                    nc.vector.tensor_tensor(g.mixed[:, ds(i // QC, 1), ds((i % QC) * CW + h0, w)]
                                            .rearrange("p a n -> p (a n)"), mixed[:, h0:h0 + w], ps_misc[:, h0:h0 + w],
                                            ALU.mult).then_inc(normed, 1)

                def turn(i, first=False, ahead=2):
                    for kt in range(KT):
                        if kt < KT - LEAD:
                            if ahead >= 1:
                                row_tile(i + 1, kt + LEAD)
                                if kt == KT - LEAD - 1:
                                    whole_rows(i + 1)
                        elif ahead == 2:
                            row_tile(i + 2, kt - (KT - LEAD))
                        if not first:
                            if kt == 2:
                                invert(i - 1)
                            if kt in (7, 8):
                                normalise(i - 1, kt - 7)
                        if ahead >= 1 and kt in (11, 12):
                            cut_max(i + 1, kt == 11)

                for kt in range(KT):
                    row_tile(0, kt)
                whole_rows(0)
                for kt in range(LEAD):
                    row_tile(1, kt)
                    if kt in (1, 2):
                        cut_max(0, kt == 1)
                turn(0, first=True)
                with dve.Fori(0, (STEPS - 4) // 2) as k:
                    turn(k * 2 + 1)
                    turn(k * 2 + 2)
                turn(STEPS - 3)
                turn(STEPS - 2, ahead=1)
                turn(STEPS - 1, ahead=0)
                dve.wait_ge(spread, STEPS)
                for half in range(2):
                    cols = slice(half * (CW // 2), (half + 1) * (CW // 2))
                    nc.vector.reciprocal(inv_rows[:, cols], ps_misc[:, cols]).then_inc(inv_ready, 1)
                    dve.wait_ge(inv_ready, STEPS + half)
                    nc.vector.tensor_tensor(g.mixed[:, NG - 1, (QC - 1) * CW + cols.start:(QC - 1) * CW + cols.stop],
                                            mixed[:, cols], inv_rows[:, cols], ALU.mult).then_inc(normed, 1)


def mix_heads_and_gate(nc, g, w1, b1, b2_rows):
    with ExitStack() as ctx:
        sb = lambda name, shape, dt=F32: ctx.enter_context(nc.sbuf_tensor(name, shape, dt))
        ps = lambda name, shape, dt=F32: ctx.enter_context(nc.psum_tensor(name, shape, dt))
        sem = lambda name: ctx.enter_context(nc.semaphore(name))
        HGS = NG // B

        wo, gw_a, gw_b, gb = g.w_out, g.gate_w_a, g.gate_w_b, g.gate_b
        heads = sb("heads", [P, HGS, CW])
        stats, mv = sb("ln2_stats", [P, CT, 6]), sb("ln2_mean_var", [P, CT, 2])
        ve, sd, rstd = sb("ln2_var_eps", [P, CT]), sb("ln2_sd", [P, CT]), sb("ln2_rstd", [P, CT])
        x2 = sb("x2", [P, 2, CT, C])
        xa, xb = sb("x2_t_a", [P, CW]), sb("x2_t_b", [CB, CW])

        ps_o = [[ps(f"ps_o{r}{k}", [P, 2 * C]) for k in range(2)] for r in range(2)]
        ps_ta, ps_tb = ps("ps2_ta", [P, CW]), ps("ps2_tb", [CB, CW])
        ps_l = ps("ps_logits", [P, CT * (E + 1)])

        weights_in = sem("c_weights_in")
        heads_ready, mixed_out = sem("c_heads_ready"), sem("c_mixed_out")
        chained, var_ready, sd_ready = sem("c_chain"), sem("c_var_ready"), sem("c_sd_ready")
        x2_ready, turned, xt_ready = sem("c_x2_ready"), sem("c_turned"), sem("c_xt_ready")
        gated, gate_read, x2_stored = sem("c_gated"), sem("c_gate_read"), sem("c_x2_stored")

        with nc.Block() as block:

            @block.sync
            def _(sp):
                sp.dma_start(g.b2[:].rearrange("p e n -> p (e n)"), b2_rows.to_broadcast([P, E * C])).then_inc(weights_in, 16)
                sp.dma_start(g.w1_b[CB:CB + 1], b1.rearrange("(a e) f -> a e f", a=1)).then_inc(weights_in, 16)
                assert E == NCH
                with sp.Fori(0, NCH) as i:
                    hold(sp, x2_ready, i + 1)
                    sp.dma_start(g.x2_rows[ds(i * CW, CW)].rearrange("(t p) n -> p t n", p=P),
                                 x2[:, ds(i % 2, 1)].rearrange("p a t n -> p (a t) n")).then_inc(x2_stored, 16)
                    sp.dma_start(g.w1_a[:, ds(i, 1), :], w1[ds(i, 1), 0:P, :].rearrange("e k f -> k e f")).then_inc(weights_in, 16)
                    sp.dma_start(g.w1_b[0:CB, ds(i, 1), :], w1[ds(i, 1), P:C, :].rearrange("e k f -> k e f")).then_inc(weights_in, 16)
                    hold(sp, x2_stored, 16 * i + 16)
                sp.wait_ge(weights_in, 16 * (2 + 2 * E))

            @block.scalar
            def _(act):
                def copy_heads(i):
                    act.wait_ge(mixed_out, i)
                    nc.scalar.activation(heads[:], g.mixed[:, ds((i // QC) * HGS, HGS), ds((i % QC) * CW, CW)],
                                         ACT.Copy).then_inc(heads_ready, 1)

                def root(i):
                    act.wait_ge(var_ready, i + 1)
                    nc.scalar.activation(sd[:], ve[:], ACT.Sqrt).then_inc(sd_ready, 1)

                def copy_x(i):
                    act.wait_ge(turned, i + 1)
                    act.wait_ge(gated, i)
                    nc.scalar.activation(xa[:], ps_ta[:], ACT.Copy).then_inc(xt_ready, 1)
                    nc.scalar.activation(xb[:], ps_tb[:], ACT.Copy).then_inc(xt_ready, 1)

                copy_heads(0)
                copy_heads(1)
                root(0)
                copy_heads(2)
                with act.Fori(0, NCH - 3) as i:
                    root(i + 1)
                    copy_x(i)
                    copy_heads(i + 3)
                for i in range(NCH - 3, NCH):
                    if i < NCH - 1:
                        root(i + 1)
                    copy_x(i)

            @block.tensor
            def _(pe):
                def mix(i, r):
                    pe.wait_ge(heads_ready, i + 1)
                    if not isinstance(i, int):
                        pe.wait_ge(x2_ready, i - 1)
                    for j in range(CT):
                        for a in range(HGS):
                            last = nc.tensor.matmul(ps_o[r][j // 2][:, (j % 2) * C:(j % 2 + 1) * C],
                                                    heads[:, a, j * P:(j + 1) * P], wo[:, a, :],
                                                    start=(a == 0), stop=(a == HGS - 1))
                    last.then_inc(mixed_out, 1)

                def turn_x(i, r):
                    pe.wait_ge(x2_ready, i + 1)
                    pe.wait_ge(xt_ready, 2 * i)
                    for j in range(CT):
                        nc.tensor.transpose(ps_ta[:, j * P:(j + 1) * P], x2[:, r, j, 0:P], g.ident[:])
                        last = nc.tensor.transpose(ps_tb[:, j * P:(j + 1) * P], x2[:, r, j, P:C], g.ident[:])
                    last.then_inc(turned, 1)

                def gate(i):
                    pe.wait_ge(xt_ready, 2 * i + 2)
                    pe.wait_ge(gate_read, i)
                    for j in range(CT):
                        dst = ps_l[:, j * (E + 1):(j + 1) * (E + 1)]
                        nc.tensor.matmul(dst, xa[:, j * P:(j + 1) * P], gw_a[:], start=True, stop=False)
                        last = nc.tensor.matmul(dst, xb[:, j * P:(j + 1) * P], gw_b[:], start=False, stop=True)
                    last.then_inc(gated, 1)

                mix(0, 0)
                mix(1, 1)
                with pe.Fori(0, (NCH - 2) // 2) as k:
                    for r in range(2):
                        turn_x(k * 2 + r, r)
                        mix(k * 2 + r + 2, r)
                        gate(k * 2 + r)
                for r in range(2):
                    turn_x(NCH - 2 + r, r)
                    gate(NCH - 2 + r)

            @block.vector
            def _(dve):
                per_turn = 2 + 2 * CT + 1 + CT - 1

                def norm(i, r):
                    chain = Tally(chained, i * per_turn)
                    dve.wait_ge(mixed_out, i + 1)
                    for k in range(2):
                        hk = g.h[:, ds(CT * i + 2 * k, 2), :]
                        n = chain.add(nc.vector.tensor_tensor(hk, ps_o[r][k][:].rearrange("p (j n) -> p j n", j=2), hk, ALU.add))
                    hold(dve, chain.sem, n)
                    for j in range(CT):
                        n = chain.add(nc.vector.bn_stats(stats[:, j, :], g.h[:, ds(CT * i + j, 1), :]
                                                         .rearrange("p a n -> p (a n)")))
                    hold(dve, chain.sem, n)
                    for j in range(CT):
                        n = chain.add(nc.vector.bn_aggr(mv[:, j, :], stats[:, j, :]))
                    dve.wait_ge(chain.sem, n)
                    nc.vector.tensor_scalar_add(ve[:], mv[:, :, 1], EPS).then_inc(var_ready, 1)
                    dve.wait_ge(sd_ready, i + 1)
                    n = chain.add(nc.vector.reciprocal(rstd[:], sd[:]))
                    dve.wait_ge(chain.sem, n)
                    if not isinstance(i, int):
                        dve.wait_ge(turned, i - 1)
                        dve.wait_ge(x2_stored, 16 * (i - 1))
                    for j in range(CT):
                        ins = nc.vector.tensor_scalar(x2[:, r, j, :], g.h[:, ds(CT * i + j, 1), :]
                                                      .rearrange("p a n -> p (a n)"),
                                                      mv[:, j, 0:1], rstd[:, j:j + 1], ALU.subtract, ALU.mult)
                        if j < CT - 1:
                            chain.add(ins)
                        else:
                            ins.then_inc(x2_ready, 1)
                    assert chain.n == per_turn

                def read_logits(i):
                    dve.wait_ge(gated, i + 1)
                    nc.vector.tensor_tensor(g.logits[:, ds(CT * i, CT), :],
                                            ps_l[:].rearrange("p (j n) -> p j n", j=CT),
                                            gb[:].unsqueeze(1).to_broadcast([P, CT, E + 1]), ALU.add).then_inc(gate_read, 1)

                norm(0, 0)
                norm(1, 1)
                read_logits(0)
                with dve.Fori(0, (NCH - 2) // 2) as k:
                    for r in range(2):
                        norm(k * 2 + r + 2, r)
                        read_logits(k * 2 + r + 1)
                read_logits(NCH - 1)


class Chain:

    def __init__(self, eng, sem):
        self.eng, self.sem, self.n = eng, sem, 0

    def count(self, ins):
        ins.then_inc(self.sem, 1)
        self.n += 1

    def wait(self):
        self.eng.wait_ge(self.sem, self.n)

    def step(self, ins):
        self.count(ins)
        self.wait()


def route(nc, g, w2):
    with ExitStack() as ctx:
        sb = lambda name, shape, dt=F32: ctx.enter_context(nc.sbuf_tensor(name, shape, dt))
        ps = lambda name, shape, dt=F32: ctx.enter_context(nc.psum_tensor(name, shape, dt))
        sem = lambda name: ctx.enter_context(nc.semaphore(name))

        sh = [P, NT, E]
        ex, pr, eq, sc = sb("r_ex", sh), sb("r_prob", sh), sb("r_eq", sh), sb("r_score", sh)
        pick = [sb(f"r_pick{k}", sh) for k in range(2)]
        top = [sb(f"r_top{k}", [P, NT]) for k in range(2)]
        m = sb("r_max", [P, NT])
        first = sb("r_first", [P, NT])
        prefer = sb("r_prefer", [P, E])
        by_expert = sb("r_by_expert", [P, E, NT])
        before = sb("r_before", [P, P])
        ones = sb("r_ones", [P, P])
        go_on = sb("r_go_on", [P, E, NT])
        total = sb("r_total", [P, E, NT])
        upto = sb("r_upto", [P, E, NT])
        slot = sb("r_slot", [P, E, NT])
        tiles_f, tiles_i = sb("r_tiles_f", [P, E]), sb("r_tiles_i", [P, E], I32)
        tiles_end, tiles_start = sb("r_tiles_end", [P, E]), sb("r_tiles_start", [P, E])
        dest_f = sb("r_dest_f", [P, 2, NT])
        dest_i = sb("r_dest_i", [P, 2, NT], I32)
        part_i = sb("r_dest_part_i", [P, 2, NT], I32)
        lane, tile = sb("r_lane", [P, 2, NT]), sb("r_tile", [P, 2, NT])
        ids1 = sb("r_token_plus1", [P, NT])
        iota = sb("r_iota", [P, P])
        dummy = sb("r_dummy", [P, 1])
        off = [[sb(f"r_off{r}{k}", [P, P]) for k in range(2)] for r in range(2)]
        hot = [[sb(f"r_hot{r}{k}", [P, P]) for k in range(2)] for r in range(2)]
        what = [[sb(f"r_what{r}{k}", [P, 2, ET]) for k in range(2)] for r in range(2)]
        over = sb("r_over", [P, ET, E])
        eid_f = sb("r_eid_f", [P, ET])
        idf, unused = sb("r_id_f", [P, ET]), sb("r_unused", [P, ET])
        ps_rank, ps_total = ps("ps_rank", [P, E * NT]), ps("ps_total", [P, E * NT])
        ps_slots = ps("ps_slots", [P, 2 * ET])

        const, v_chain = sem("r_const"), sem("r_chain")
        shifted, exped = sem("r_shifted"), sem("r_exped")
        picked, ranked = sem("r_picked"), sem("r_ranked")
        placed, off_ready = sem("r_placed"), sem("r_off_ready")
        hot_ready, what_ready = sem("r_hot_ready"), sem("r_what_ready")
        hot_slots = sem("r_hot_slots")

        weights_in = sem("r_weights_in")

        with nc.Block() as block:

            @block.sync
            def _(sp):
                for e in range(E):
                    sp.dma_start(g.w2[:, e], w2[e].rearrange("(j k) n -> k j n", k=P)).then_inc(weights_in, 16)
                sp.wait_ge(weights_in, 16 * E)

            @block.gpsimd
            def _(pool):
                pool.iota(iota[:], [[1, P]], base=0, channel_multiplier=0,
                          allow_small_or_imprecise_dtypes=True).then_inc(const, 1)
                pool.iota(prefer[:], [[-1, E]], base=E, channel_multiplier=0,
                          allow_small_or_imprecise_dtypes=True).then_inc(const, 1)
                pool.iota(ids1[:], [[P, NT]], base=1, channel_multiplier=1,
                          allow_small_or_imprecise_dtypes=True).then_inc(const, 1)
                pool.iota(dummy[:], [[1, 1]], base=N + 1, channel_multiplier=1,
                          allow_small_or_imprecise_dtypes=True).then_inc(const, 1)
                pool.memset(before[:], 1.0).then_inc(const, 1)
                pool.memset(ones[:], 1.0).then_inc(const, 1)
                pool.memset(go_on[:], 1.0).then_inc(const, 1)
                pool.wait_ge(const, 7)
                pool.affine_select(out=before[:], in_=before[:], compare_op=ALU.is_gt, fill=0.0, base=0,
                                   pattern=[[1, P]], channel_multiplier=-1).then_inc(const, 1)
                pool.memset(go_on[:, :, 0:1], 0.0).then_inc(const, 1)

            @block.scalar
            def _(act):
                act.wait_ge(shifted, 1)
                nc.scalar.activation(ex[:], pr[:], ACT.Exp).then_inc(exped, 1)
                act.wait_ge(placed, 1)
                act.wait_ge(const, 9)
                with act.Fori(0, NT // 2) as th:
                    for r in range(2):
                        t = th * 2 + r
                        for k in range(2):
                            act.wait_ge(hot_slots, 2 * t + k + 1)
                            nc.scalar.activation(off[r][k][:], iota[:], ACT.Abs, bias=lane[:, k, ds(t, 1)]).then_inc(off_ready, 1)
                        for k in range(2):
                            act.wait_ge(off_ready, 2 * t + k + 1)
                            nc.scalar.activation(hot[r][k][:], off[r][k][:], ACT.Relu, scale=-1.0,
                                                 bias=ones[:, 0:1]).then_inc(hot_ready, 1)

            @block.tensor
            def _(pe):
                pe.wait_ge(const, 9)
                pe.wait_ge(picked, 1)
                mask = by_expert[:].rearrange("p e t -> p (e t)")
                nc.tensor.matmul(ps_rank[:], before[:], mask, start=True, stop=True)
                nc.tensor.matmul(ps_total[:], ones[:], mask, start=True, stop=True).then_inc(ranked, 1)

                def place(t, r, first=False, last=False):
                    for k in range(2):
                        pe.wait_ge(hot_ready, 2 * t + k + 1)
                        pe.wait_ge(what_ready, 2 * t + k + 1)
                        nc.tensor.matmul(ps_slots[:], hot[r][k][:], what[r][k][:].rearrange("p a j -> p (a j)"),
                                         start=(first and k == 0), stop=(last and k == 1)).then_inc(hot_slots, 1)

                place(0, 0, first=True)
                place(1, 1)
                with pe.Fori(1, NT // 2 - 1) as th:
                    place(th * 2, 0)
                    place(th * 2 + 1, 1)
                place(NT - 2, 0)
                place(NT - 1, 1, last=True)

            @block.vector
            def _(dve):
                v = nc.vector
                c = Chain(dve, v_chain)
                wide = lambda a: a.unsqueeze(2).to_broadcast(sh)
                lg = g.logits[:, :, 0:E]
                c.step(v.tensor_reduce(m[:], lg, AX.X, ALU.max))
                v.tensor_tensor(pr[:], lg, wide(m[:]), ALU.subtract).then_inc(shifted, 1)
                dve.wait_ge(exped, 1)
                c.step(v.tensor_reduce(m[:], ex[:], AX.X, ALU.add))
                c.step(v.reciprocal(first[:], m[:]))
                c.step(v.tensor_tensor(pr[:], ex[:], wide(first[:]), ALU.mult))
                dve.wait_ge(const, 9)
                for k in range(2):
                    c.step(v.tensor_reduce(top[k][:], pr[:], AX.X, ALU.max))
                    c.step(v.tensor_tensor(eq[:], pr[:], wide(top[k][:]), ALU.is_equal))
                    c.step(v.tensor_tensor(sc[:], eq[:], prefer[:].unsqueeze(1).to_broadcast(sh), ALU.mult))
                    c.step(v.tensor_reduce(first[:], sc[:], AX.X, ALU.max))
                    c.step(v.tensor_tensor(pick[k][:], sc[:], wide(first[:]), ALU.is_equal))
                    if k == 0:
                        c.step(v.scalar_tensor_tensor(out=pr[:], in0=pick[0][:], scalar=-2.0, in1=pr[:],
                                                      op0=ALU.mult, op1=ALU.add))
                v.tensor_tensor(by_expert[:].rearrange("p e t -> p t e"), pick[0][:], pick[1][:],
                                ALU.add).then_inc(picked, 1)
                c.step(v.tensor_tensor(m[:], top[0][:], top[1][:], ALU.add))
                c.step(v.reciprocal(first[:], m[:]))
                c.step(v.tensor_tensor(top[0][:], top[0][:], first[:], ALU.mult))
                c.step(v.tensor_tensor(top[1][:], top[1][:], first[:], ALU.mult))
                dve.wait_ge(ranked, 1)
                flat = lambda a: a.rearrange("p e t -> p (e t)")
                c.step(v.tensor_copy(flat(total[:]), ps_total[:]))
                c.step(v.tensor_tensor_scan(flat(upto[:]), flat(go_on[:]), flat(total[:]), 0.0, ALU.mult, ALU.add))
                c.step(v.tensor_scalar(tiles_i[:], upto[:, :, NT - 1], float(P - 1), None, ALU.add))
                c.step(v.tensor_scalar(tiles_i[:], tiles_i[:], 7, None, ALU.arith_shift_right))
                c.step(v.tensor_copy(tiles_f[:], tiles_i[:]))
                c.step(v.tensor_tensor_scan(tiles_end[:], ones[:, 0:E], tiles_f[:], 0.0, ALU.mult, ALU.add))
                c.step(v.tensor_tensor(tiles_start[:], tiles_end[:], tiles_f[:], ALU.subtract))
                c.step(v.tensor_tensor(slot[:], upto[:], total[:], ALU.subtract))
                c.step(v.tensor_tensor(flat(slot[:]), flat(slot[:]), ps_rank[:], ALU.add))
                c.step(v.scalar_tensor_tensor(out=slot[:], in0=tiles_start[:].unsqueeze(2).to_broadcast([P, E, NT]),
                                              scalar=float(P), in1=slot[:], op0=ALU.mult, op1=ALU.add))
                for k in range(2):
                    c.step(v.tensor_tensor(eq[:], pick[k][:], slot[:].rearrange("p e t -> p t e"), ALU.mult))
                    c.step(v.tensor_reduce(dest_f[:, k, :], eq[:], AX.X, ALU.add))
                c.step(v.tensor_copy(dest_i[:], dest_f[:]))
                c.step(v.tensor_scalar(part_i[:], dest_i[:], 7, None, ALU.arith_shift_right))
                c.step(v.tensor_copy(tile[:], part_i[:]))
                c.step(v.tensor_scalar(part_i[:], dest_i[:], P - 1, None, ALU.bitwise_and))
                c.step(v.tensor_scalar(lane[:], part_i[:], -1.0, None, ALU.mult))
                dve.sem_inc(hot_slots, 4)
                dve.sem_inc(placed, 1)
                c.step(v.tensor_tensor(over[:], iota[:, 0:ET].unsqueeze(2).to_broadcast([P, ET, E]),
                                       tiles_end[:].unsqueeze(1).to_broadcast([P, ET, E]), ALU.is_ge))
                c.step(v.tensor_reduce(eid_f[:], over[:], AX.X, ALU.add))
                c.step(v.tensor_scalar(g.expert_of[:], eid_f[:], float(E - 1), None, ALU.min))
                with dve.Fori(0, NT // 2) as th:
                    for r in range(2):
                        t = th * 2 + r
                        for k in range(2):
                            dve.wait_ge(hot_slots, 2 * t + k + 1)
                            at = tile[:, k, ds(t, 1)]
                            v.tensor_scalar(what[r][k][:, 0, :], iota[:, 0:ET], at, ids1[:, ds(t, 1)], ALU.is_equal, ALU.mult)
                            v.tensor_scalar(what[r][k][:, 1, :], iota[:, 0:ET], at, top[k][:, ds(t, 1)],
                                            ALU.is_equal, ALU.mult).then_inc(what_ready, 1)
                dve.wait_ge(hot_slots, 4 + 2 * NT)
                c.step(v.tensor_copy(idf[:], ps_slots[:, 0:ET]))
                c.step(v.tensor_copy(g.slot_weight[:], ps_slots[:, ET:2 * ET]))
                c.step(v.tensor_scalar(unused[:], idf[:], 0.0, dummy[:, 0:1], ALU.is_equal, ALU.mult))
                c.step(v.tensor_tensor(idf[:], idf[:], unused[:], ALU.add))
                c.step(v.tensor_scalar(g.slot_token[:], idf[:], -1.0, None, ALU.add))


def experts_and_spectrum(nc, g, out_rows):
    FT = F // P
    L = 2 * B
    HI = 32 + B
    LEVELS = 3
    GROUPS = P >> LEVELS
    MAP_STEPS, ADD_TILES = 2, 4
    MAPS_TURN = 1 + TB // MAP_STEPS
    JOIN = MAPS_TURN + 3
    CARRY = JOIN + 6
    HAND_DOWN = CARRY + GROUPS - 1
    HAND_OUT = HAND_DOWN + LEVELS + 1
    RUN = HAND_OUT + 4
    ADD = RUN + TB + 1
    ADD_END = ADD + NT // ADD_TILES
    assert ADD_END < ET and MAPS_TURN % 2 == 1 and HAND_OUT % 2 == 1 and ET % 2 == 1

    with ExitStack() as ctx:
        sb = lambda name, shape, dt=F32: ctx.enter_context(nc.sbuf_tensor(name, shape, dt))
        sem = lambda name: ctx.enter_context(nc.semaphore(name))

        a = sb("s_a", [P, L, TB])
        y = sb("s_y", [P, TB + 2, 2, 2, L])
        t = sb("s_t", [P, 2, 2, L])
        flip = sb("s_flip", [P, P])
        maps = [sb(f"s_maps{l}", [HI, P >> l, 4, 5]) for l in range(LEVELS + 1)]
        prod = sb("s_map_product", [HI, P // 2, 2, 5])
        mag, scale = sb("s_map_magnitude", [HI, P // 2, 2]), sb("s_map_scale", [HI, P // 2])
        ws = [sb(f"s_w{l}", [HI, P >> l, 2]) for l in range(LEVELS + 1)]
        wnd, wtmp = sb("s_w_fraction", [HI, P // 2, 5]), sb("s_w_tmp", [HI, P // 2, 5])
        wsq, wpr = sb("s_w_sq", [HI, P // 2, 2]), sb("s_w_products", [HI, P // 2, 2, 2])
        wnorm = sb("s_w_norm", [HI, P // 2])
        w = sb("s_w", [HI, 2])
        num, nd = sb("s_num", [HI, 5]), sb("s_nd", [HI, 5])
        sq, norm, rnorm = sb("s_sq", [HI, 2]), sb("s_norm", [HI, 1]), sb("s_rnorm", [HI, 1])
        back = sb("s_back", [P, 2, B])
        win = sb("s_w_in", [P, 2, L])
        d = sb("s_d", [P, 2, TB, L])
        sqw, qw = sb("s_sq_wide", [P, 2, L]), sb("s_q_wide", [P, L])
        z = sb("s_z", [P, 2, B, TB])
        z2, zn = sb("s_z_sq", [P, 2, B, TB]), sb("s_z_norm", [P, B, TB])
        rows = sb("s_rows", [P, 4, C])
        rows_s = sb("s_rows_scaled", [P, 3, C])

        const, loaded = sem("s_const"), sem("s_loaded")
        chained = sem("s_chain")
        maps_made, maps_turned, maps_read = sem("s_maps_made"), sem("s_maps_turned"), sem("s_maps_read")
        carried, carry_back, back_read, flipped = (
            sem("s_carried"), sem("s_carry_back"), sem("s_back_read"), sem("s_flipped"))
        finished = sem("s_finished")

        ids_in = [sb(f"e_ids_gather{r}", [P, 1], I32) for r in range(2)]
        ids_out = [sb(f"e_ids_scatter{r}", [P, 1], I32) for r in range(2)]
        xg = [sb(f"e_x{r}", [P, C]) for r in range(2)]
        xa, xb = sb("e_x_t_a", [P, P]), sb("e_x_t_b", [CB + 1, P])
        room = g.mixed[:].rearrange("p a n -> p (a n)")
        hid, wa, wb = (room[:, 2 * k * F:2 * (k + 1) * F].rearrange("p (r n) -> p r n", r=2) for k in range(3))
        yt = sb("e_y", [P, C])
        yw = sb("e_y_weighted", [P, C])
        ps = lambda name, shape, dt=F32: ctx.enter_context(nc.psum_tensor(name, shape, dt))
        ps_x = ps("ps_x", [P, 2 * P])
        ps_h = ps("ps_h", [P, 1024])
        ps_y = ps("ps_y", [P, C])
        ps_m = ps("ps_maps", [P, 4 * P])
        ps_c, ps_cb = ps_m[:, 0:4 * B].rearrange("p (x n) -> p x n", x=2), ps("ps_carry_back", [P, 2 * B])

        ones_made = sem("e_ones")
        id1, id2 = sem("e_ids_gather_ready"), sem("e_ids_scatter_ready")
        gathered = [sem(f"e_gathered{r}") for r in range(2)]
        x_turned, xt_ready = sem("e_x_turned"), sem("e_xt_ready")
        w1_ready = sem("e_w1_ready")
        hidden, gelu_done = sem("e_hidden_done"), sem("e_gelu")
        y_done, y_ready, yw_ready, added = sem("e_y_done"), sem("e_y_ready"), sem("e_yw_ready"), sem("e_added")

        with nc.Block() as block:

            @block.sync
            def _(sp):
                sp.dma_start(rows[:].rearrange("p a n -> p (a n)"), out_rows.to_broadcast([P, 4 * C])).then_inc(loaded, 16)

            @block.gpsimd
            def _(pool):
                pool.memset(xb[CB:CB + 1, :], 1.0).then_inc(ones_made, 1)
                pool.wait_ge(ones_made, 1)

                def gather(j, r):
                    if not isinstance(j, int) or j >= 2:
                        pool.wait_ge(x_turned, j - 1)
                    pool.tensor_copy(ids_in[r][:], g.slot_token[:, ds(j, 1)]).then_inc(id1, 1)
                    hold(pool, id1, j + 1)
                    pool.indirect_dma_start(out=xg[r][:], out_offset=None, in_=g.x2_rows[:],
                                            in_offset=bass.IndirectOffsetOnAxis(ap=ids_in[r][:, 0:1], axis=0)
                                            ).then_inc(gathered[r], 16)

                def add(j, r):
                    pool.wait_ge(added, 16 * j)
                    pool.tensor_copy(ids_out[r][:], g.slot_token[:, ds(j, 1)]).then_inc(id2, 1)
                    pool.wait_ge(id2, j + 1)
                    hold(pool, yw_ready, j + 1)
                    pool.indirect_dma_start(out=g.sums[:], in_=yw[:], in_offset=None,
                                            out_offset=bass.IndirectOffsetOnAxis(ap=ids_out[r][:, 0:1], axis=0),
                                            compute_op=ALU.add).then_inc(added, 16)

                gather(0, 0)
                gather(1, 1)
                pool.memset(flip[:], 0.0).then_inc(const, 1)
                pool.wait_ge(const, 1)
                pool.affine_select(out=flip[:], in_=flip[:], compare_op=ALU.not_equal, fill=1.0, base=-(P - 1),
                                   pattern=[[1, P]], channel_multiplier=1).then_inc(const, 1)
                gather(2, 0)
                with pool.Fori(0, (ET - 3) // 2) as k:
                    for r in range(2):
                        j = k * 2 + 1 + r
                        gather(j + 2, (1 + r) % 2)
                        add(j - 1, r)
                for j in range(ET - 3, ET):
                    add(j, j % 2)
                pool.wait_ge(added, 16 * ET)

            @block.tensor
            def _(pe):
                def turn_x(j, r):
                    pe.wait_ge(gathered[r], (j - r) * 8 + 16)
                    pe.wait_ge(xt_ready, 2 * j)
                    nc.tensor.transpose(ps_x[:, 0:P], xg[r][:, 0:P], g.ident[:])
                    nc.tensor.transpose(ps_x[0:CB, P:2 * P], xg[r][:, P:C], g.ident[:]).then_inc(x_turned, 1)

                def up(j, r):
                    pe.wait_ge(xt_ready, 2 * j + 2)
                    pe.wait_ge(w1_ready, 2 * j + 2)
                    pe.wait_ge(gelu_done, j)
                    for k in range(FT):
                        cols = slice(k * P, (k + 1) * P)
                        nc.tensor.matmul(ps_h[:, cols], wa[:, r, cols], xa[:], start=True, stop=False)
                        last = nc.tensor.matmul(ps_h[:, cols], wb[0:CB + 1, r, cols], xb[:], start=False, stop=True)
                    last.then_inc(hidden, 1)

                def down(j, r):
                    e = pe.value_load(g.expert_of[0:1, ds(j, 1)], min_val=0, max_val=E - 1)
                    pe.wait_ge(gelu_done, j + 1)
                    pe.wait_ge(y_ready, j)
                    for k in range(FT):
                        last = nc.tensor.matmul(ps_y[:], hid[:, r, k * P:(k + 1) * P],
                                                g.w2[:, ds(e, 1), k, :].rearrange("p a n -> p (a n)"),
                                                start=(k == 0), stop=(k == FT - 1))
                    last.then_inc(y_done, 1)

                def tile(j, r):
                    up(j, r)
                    turn_x(j + 1, 1 - r)
                    down(j - 1, 1 - r)

                def turn_maps(s):
                    pe.wait_ge(maps_made, 1)
                    pe.wait_ge(maps_read, s)
                    for q in range(4):
                        src = y[:, TB + s, q % 2, q // 2, :]
                        nc.tensor.matmul(ps_m[0:B, q * P:(q + 1) * P], src[:, 0:B], g.ident[:], start=True, stop=True)
                        last = nc.tensor.matmul(ps_m[32:32 + B, q * P:(q + 1) * P], src[:, B:L], flip[:], start=True, stop=True)
                    last.then_inc(maps_turned, 1)

                def turn_carry():
                    pe.wait_ge(carried, 1)
                    for ri in range(2):
                        nc.tensor.matmul(ps_c[:, 0, ri * B:(ri + 1) * B], ws[0][0:B, :, ri], g.ident[0:B, 0:B],
                                         start=True, stop=True)
                        last = nc.tensor.matmul(ps_cb[:, ri * B:(ri + 1) * B], ws[0][32:32 + B, :, ri],
                                                g.ident[32:32 + B, 32:32 + B], start=True, stop=True)
                    last.then_inc(carry_back, 1)

                def tiles(j0, j1):
                    fours = (j1 - j0) // 4
                    with pe.Fori(0, fours) as k:
                        for q in range(4):
                            tile(k * 4 + j0 + q, (q + 1) % 2)
                    for j in range(j0 + 4 * fours, j1):
                        tile(j, j % 2)

                pe.wait_ge(ones_made, 1)
                turn_x(0, 0)
                up(0, 0)
                turn_x(1, 1)
                tiles(1, MAPS_TURN)
                tile(MAPS_TURN, 1)
                pe.wait_ge(const, 2)
                turn_maps(0)
                tile(MAPS_TURN + 1, 0)
                turn_maps(1)
                tiles(MAPS_TURN + 2, HAND_OUT)
                tile(HAND_OUT, 1)
                turn_carry()
                tile(HAND_OUT + 1, 0)
                tile(HAND_OUT + 2, 1)
                pe.wait_ge(back_read, 1)
                nc.tensor.matmul(ps_c[:, 1, :], flip[:], back[:].rearrange("p r b -> p (r b)"),
                                 start=True, stop=True).then_inc(flipped, 1)
                tile(HAND_OUT + 3, 0)
                tiles(RUN, ET - 2)
                tile(ET - 2, 1)
                up(ET - 1, 0)
                down(ET - 2, 1)
                down(ET - 1, 0)

            @block.scalar
            def _(act):
                of = lambda buf, j: buf[:, ds(j % 2, 1), :].rearrange("p a n -> p (a n)")

                def copy_w1(j):
                    e = act.value_load(g.expert_of[0:1, ds(j, 1)], min_val=0, max_val=E - 1)
                    nc.scalar.activation(of(wa, j), g.w1_a[:, ds(e, 1), :].rearrange("p a n -> p (a n)"),
                                         ACT.Copy).then_inc(w1_ready, 1)
                    nc.scalar.activation(of(wb[0:CB + 1], j), g.w1_b[:, ds(e, 1), :].rearrange("p a n -> p (a n)"),
                                         ACT.Copy).then_inc(w1_ready, 1)

                def gelu(j, first=False):
                    act.wait_ge(hidden, j + 1)
                    if not first:
                        act.wait_ge(y_done, j - 1)
                    nc.scalar.activation(of(hid, j), ps_h[:, 0:F], ACT.Gelu_apprx_tanh).then_inc(gelu_done, 1)

                copy_w1(0)
                copy_w1(1)
                gelu(0, first=True)
                copy_w1(2)
                with act.Fori(1, ET - 2) as j:
                    gelu(j)
                    copy_w1(j + 2)
                gelu(ET - 2)
                gelu(ET - 1)

            @block.vector
            def _(dve):
                v = nc.vector

                def copy_x(j):
                    dve.wait_ge(x_turned, j + 1)
                    dve.wait_ge(hidden, j)
                    v.tensor_copy(xa[:], ps_x[:, 0:P]).then_inc(xt_ready, 1)
                    v.tensor_copy(xb[0:CB, :], ps_x[0:CB, P:2 * P]).then_inc(xt_ready, 1)

                def weigh(j):
                    e = dve.value_load(g.expert_of[0:1, ds(j, 1)], min_val=0, max_val=E - 1)
                    dve.wait_ge(y_done, j + 1)
                    dve.wait_ge(yw_ready, j)
                    v.tensor_tensor(yt[:], ps_y[:], g.b2[:, ds(e, 1), :].rearrange("p a n -> p (a n)"),
                                    ALU.add).then_inc(y_ready, 1)
                    dve.wait_ge(y_ready, j + 1)
                    dve.wait_ge(added, 16 * j)
                    v.tensor_scalar(yw[:], yt[:], g.slot_weight[:, ds(j, 1)], None, ALU.mult).then_inc(yw_ready, 1)

                def tile(j):
                    copy_x(j + 1)
                    weigh(j - 1)

                MAP_INCS, CARRY_INCS, RUN_INCS = 4, 7, 7
                c = Chain(dve, chained)

                def map_step(base, s):
                    chain = Tally(chained, base + s * MAP_INCS)

                    def then(ins):
                        dve.wait_ge(chained, chain.add(ins))
                    at = lambda k: y[:, ds(s + k, 1)]
                    mem = lambda ap: ap.rearrange("p a r c l -> p (a r c) l")
                    one = lambda ap: ap.rearrange("p a c l -> p (a c) l")
                    then(v.tensor_tensor(t[:].rearrange("p r c l -> p (r c) l"), mem(at(1)),
                                         a[:, :, ds(s, 1)].rearrange("p l a -> p a l").to_broadcast([P, 4, L]), ALU.mult))
                    then(v.tensor_tensor(t[:].rearrange("p r c l -> p (r c) l"), t[:].rearrange("p r c l -> p (r c) l"),
                                         mem(at(0)), ALU.subtract))
                    then(v.tensor_tensor(one(y[:, ds(s + 2, 1), 0]), t[:, 0], one(y[:, ds(s + 1, 1), 1]), ALU.add))
                    then(v.tensor_tensor(one(y[:, ds(s + 2, 1), 1]), t[:, 1], one(y[:, ds(s + 1, 1), 0]), ALU.subtract))

                def read_maps(s):
                    dve.wait_ge(maps_turned, s + 1)
                    e0 = 0 if s == 0 else 3
                    for p0 in (0, 32):
                        for q in range(4):
                            last = v.tensor_copy(maps[0][p0:p0 + B, :, 2 * (q // 2), e0 + q % 2],
                                                 ps_m[p0:p0 + B, q * P:(q + 1) * P])
                            if (p0, q) != (32, 3):
                                c.count(last)
                    last.then_inc(maps_read, 1)
                    dve.wait_ge(maps_read, s + 1)
                    c.wait()

                def times_i(l):
                    plain, turned = maps[l][:, :, 0::2, :], maps[l][:, :, 1::2, :]
                    c.count(v.tensor_copy(turned[:, :, :, 1:3], plain[:, :, :, 0:2]))
                    c.count(v.tensor_copy(turned[:, :, :, 4], plain[:, :, :, 3]))
                    c.step(v.tensor_scalar(turned[:, :, :, 0::3], plain[:, :, :, 1::3], -1.0, None, ALU.mult))

                def multiply(l, part):
                    n = P >> (l + 1)
                    left, right = maps[l][:, 0::2], maps[l][:, 1::2]
                    out, tmp = maps[l + 1][:, :, 0::2, :], prod[:, 0:n]
                    for q in (2 * part, 2 * part + 1):
                        e = (3, 4, 0, 1)[q]
                        c.step(v.tensor_tensor(tmp if q else out, right[:, :, q:q + 1, :].to_broadcast([HI, n, 2, 5]),
                                               left[:, :, 0::2, e:e + 1].to_broadcast([HI, n, 2, 5]), ALU.mult))
                        if q:
                            c.step(v.tensor_tensor(out, out, tmp, ALU.add))

                def rescale(l):
                    n = P >> l
                    out, p16 = maps[l][:, :, 0::2, :], maps[l][:, :, 0, 3:5]
                    c.step(v.scalar_tensor_tensor(out=mag[:, 0:n], in0=p16, scalar=-1.0, in1=p16, op0=ALU.mult, op1=ALU.max))
                    c.step(v.tensor_tensor(scale[:, 0:n], mag[:, 0:n, 0], mag[:, 0:n, 1], ALU.max))
                    c.step(v.reciprocal(scale[:, 0:n], scale[:, 0:n]))
                    c.step(v.tensor_tensor(out, out, scale[:, 0:n].unsqueeze(2).unsqueeze(3).to_broadcast([HI, n, 2, 5]),
                                           ALU.mult))
                    c.step(v.tensor_scalar(out[:, :, :, 2], out[:, :, :, 0], -1.0, None, ALU.mult))
                    times_i(l)

                def carry_step(base, n):
                    chain = Tally(chained, base + n * CARRY_INCS)

                    def then(ins):
                        dve.wait_ge(chained, chain.add(ins))
                    of = lambda k: maps[LEVELS][:, ds(n, 1), k, :].rearrange("p a e -> p (a e)")
                    then(v.scalar_tensor_tensor(out=num[:], in0=of(2), scalar=w[:, 0:1], in1=of(0), op0=ALU.mult, op1=ALU.add))
                    then(v.scalar_tensor_tensor(out=nd[:], in0=of(3), scalar=w[:, 1:2], in1=num[:], op0=ALU.mult, op1=ALU.add))
                    then(v.tensor_tensor_reduce(sq[:], nd[:, 3:5], nd[:, 3:5], 1.0, 0.0, ALU.mult, ALU.add, norm[:]))
                    then(v.reciprocal(rnorm[:], norm[:]))
                    then(v.tensor_tensor_reduce(sq[:], nd[:, 0:2], nd[:, 3:5], rnorm[:, 0:1], 0.0, ALU.mult, ALU.add, w[:, 0:1]))
                    then(v.tensor_tensor_reduce(sq[:], nd[:, 1:3], nd[:, 3:5], rnorm[:, 0:1], 0.0, ALU.mult, ALU.add, w[:, 1:2]))
                    then(v.tensor_copy(ws[LEVELS][:, ds(n + 1, 1), :].rearrange("p a r -> p (a r)"), w[:]))

                def hand_down(l, fraction=True, quotient=True):
                    n = P >> (l + 1)
                    pair, first = ws[l + 1], maps[l][:, 0::2]
                    nd_, tmp, sq_, pr_, nn = wnd[:, 0:n], wtmp[:, 0:n], wsq[:, 0:n], wpr[:, 0:n], wnorm[:, 0:n]
                    if fraction:
                        c.step(v.tensor_copy(ws[l][:, 0::2, :], pair[:]))
                        for ri in range(2):
                            c.step(v.tensor_tensor(tmp, first[:, :, 2 + ri, :], pair[:, :, ri:ri + 1].to_broadcast([HI, n, 5]),
                                                   ALU.mult))
                            c.step(v.tensor_tensor(nd_, tmp, first[:, :, 0, :] if ri == 0 else nd_, ALU.add))
                    if quotient:
                        c.step(v.tensor_tensor(sq_, nd_[:, :, 3:5], nd_[:, :, 3:5], ALU.mult))
                        c.step(v.tensor_tensor(nn, sq_[:, :, 0], sq_[:, :, 1], ALU.add))
                        c.step(v.reciprocal(nn, nn))
                        for ri in range(2):
                            c.step(v.tensor_tensor(pr_[:, :, ri, :], nd_[:, :, ri:ri + 2], nd_[:, :, 3:5], ALU.mult))
                        c.step(v.tensor_tensor(sq_, pr_[:, :, :, 0], pr_[:, :, :, 1], ALU.add))
                        c.step(v.tensor_tensor(ws[l][:, 1::2, :], sq_, nn.unsqueeze(2).to_broadcast([HI, n, 2]), ALU.mult))

                def run_step(base, s):
                    chain = Tally(chained, base + s * RUN_INCS)

                    def then(ins):
                        dve.wait_ge(chained, chain.add(ins))
                    re, im = (d[:, ri, ds(s, 1), :].rearrange("p a l -> p (a l)") for ri in range(2))
                    then(v.tensor_tensor(re, a[:, :, ds(s, 1)].rearrange("p l a -> p (l a)"), win[:, 0, :], ALU.subtract))
                    then(v.tensor_scalar(im, win[:, 1, :], -1.0, -1.0, ALU.mult, ALU.add))
                    both = d[:, :, ds(s, 1), :].rearrange("p r a l -> p r (a l)")
                    then(v.tensor_tensor(sqw[:], both, both, ALU.mult))
                    then(v.tensor_tensor(qw[:], sqw[:, 0, :], sqw[:, 1, :], ALU.add))
                    then(v.reciprocal(qw[:], qw[:]))
                    then(v.tensor_tensor(win[:, 0, :], re, qw[:], ALU.mult))
                    then(v.scalar_tensor_tensor(out=win[:, 1, :], in0=im, scalar=-1.0, in1=qw[:], op0=ALU.mult, op1=ALU.mult))

                def features(c):
                    for ri in range(2):
                        c.step(v.tensor_tensor(z[:, ri], d[:, ri, :, 0:B].rearrange("p s b -> p b s"),
                                               d[:, ri, ::-1, B:L].rearrange("p s b -> p b s"), ALU.add))
                    c.step(v.tensor_tensor(z[:, 0], z[:, 0], a[:, 0:B, :], ALU.subtract))
                    c.step(v.tensor_scalar(z[:, 1], z[:, 1], 1.0, None, ALU.add))
                    c.step(v.tensor_tensor(z2[:], z[:], z[:], ALU.mult))
                    c.step(v.tensor_tensor(zn[:], z2[:, 0], z2[:, 1], ALU.add))
                    c.step(v.reciprocal(zn[:], zn[:]))
                    c.step(v.tensor_tensor(z[:, 0], z[:, 0], zn[:], ALU.mult))
                    c.step(v.scalar_tensor_tensor(out=z[:, 1], in0=z[:, 1], scalar=-1.0, in1=zn[:], op0=ALU.mult, op1=ALU.mult))
                    c.step(v.tensor_scalar(z[:], z[:], FEAT_CLAMP, -FEAT_CLAMP, ALU.min, ALU.max))

                def add_features(k):
                    zf = z[:].rearrange("p r b c -> p r (b c)")
                    for ri in range(2):
                        if ri:
                            dve.wait_ge(finished, (2 * k + 1) * ADD_TILES)
                        for q in range(ADD_TILES):
                            tt = k * ADD_TILES + q
                            hr = g.h[:, ds(tt, 1), :].rearrange("p a n -> p (a n)")
                            v.scalar_tensor_tensor(out=hr, in0=rows_s[:, ri, :], scalar=zf[:, ri, ds(tt, 1)], in1=hr,
                                                   op0=ALU.mult, op1=ALU.add).then_inc(finished, 1)

                logit = g.logits[:, :, E].rearrange("p (b c) -> p b c", b=B)
                for lanes, src in ((a[:, 0:B, :], logit), (a[:, B:L, :], logit[:, :, ::-1])):
                    c.step(v.tensor_scalar(lanes, src, V_MAX, -V_MAX, ALU.min, ALU.max))
                c.step(v.tensor_scalar(a[:], a[:], -2.0, None, ALU.add))
                c.step(v.memset(y[:, 0:2], 0.0))
                c.step(v.memset(y[:, 0, 0, 1, :], 1.0))
                c.step(v.memset(y[:, 1, 0, 0, :], 1.0))
                copy_x(0)
                for l in range(LEVELS + 1):
                    c.count(v.memset(ws[l][:], 0.0))
                c.step(v.memset(maps[0][:], 0.0))
                c.count(v.memset(maps[0][:, :, 0, 3], 1.0))
                c.count(v.memset(maps[0][:, :, 2, 0], 1.0))
                c.step(v.memset(w[:], 0.0))
                copy_x(1)
                dve.wait_ge(loaded, 16)
                c.step(v.tensor_tensor(rows_s[:], rows[:, 0:3], rows[:, 3:4].to_broadcast([P, 3, C]), ALU.mult))
                c.step(v.tensor_tensor(g.b2[:], g.b2[:], rows_s[:, 2:3].to_broadcast([P, E, C]), ALU.add))
                base = c.n
                with dve.Fori(1, MAPS_TURN) as j:
                    tile(j)
                    for q in range(MAP_STEPS):
                        map_step(base, (j - 1) * MAP_STEPS + q)
                c.n = base + MAP_INCS * TB
                v.memset(sq[:], 0.0).then_inc(maps_made, 1)
                tile(MAPS_TURN)
                tile(MAPS_TURN + 1)
                read_maps(0)
                tile(MAPS_TURN + 2)
                read_maps(1)
                c.step(v.tensor_scalar(maps[0][:, :, 0::2, 2], maps[0][:, :, 0::2, 0], -1.0, None, ALU.mult))
                times_i(0)
                tile(JOIN)
                multiply(0, 0)
                tile(JOIN + 1)
                multiply(0, 1)
                tile(JOIN + 2)
                rescale(1)
                tile(JOIN + 3)
                multiply(1, 0)
                multiply(1, 1)
                tile(JOIN + 4)
                rescale(2)
                tile(JOIN + 5)
                for l in range(2, LEVELS):
                    multiply(l, 0)
                    multiply(l, 1)
                    rescale(l + 1)
                base = c.n
                with dve.Fori(CARRY, HAND_DOWN) as j:
                    tile(j)
                    carry_step(base, j - CARRY)
                c.n = base + CARRY_INCS * (GROUPS - 1)
                for l in range(LEVELS - 1, 0, -1):
                    tile(HAND_DOWN + LEVELS - 1 - l)
                    hand_down(l)
                tile(HAND_OUT - 2)
                hand_down(0, quotient=False)
                tile(HAND_OUT - 1)
                hand_down(0, fraction=False)
                v.memset(sq[:], 0.0).then_inc(carried, 1)
                tile(HAND_OUT)
                tile(HAND_OUT + 1)
                dve.wait_ge(carry_back, 1)
                c.step(v.tensor_copy(win[:, :, 0:B], ps_c[:, 0, :].rearrange("p (r b) -> p r b", r=2)))
                v.tensor_copy(back[:], ps_cb[:].rearrange("p (r b) -> p r b", r=2)).then_inc(back_read, 1)
                tile(HAND_OUT + 2)
                tile(HAND_OUT + 3)
                dve.wait_ge(flipped, 1)
                c.step(v.tensor_copy(win[:, :, B:L], ps_c[:, 1, :].rearrange("p (r b) -> p r b", r=2)))
                base = c.n
                with dve.Fori(RUN, RUN + TB) as j:
                    tile(j)
                    run_step(base, j - RUN)
                c.n = base + RUN_INCS * TB
                tile(ADD - 1)
                features(c)
                with dve.Fori(ADD, ADD_END) as j:
                    tile(j)
                    add_features(j - ADD)
                for j in range(ADD_END, ET - 1):
                    tile(j)
                weigh(ET - 2)
                weigh(ET - 1)


def finish(nc, g, out):
    with ExitStack() as ctx:
        sem = lambda name: ctx.enter_context(nc.semaphore(name))
        part = ctx.enter_context(nc.sbuf_tensor("f_sums", [P, NCH, CT, C], F32))
        sums_in = [sem(f"f_sums_in{i}") for i in range(NCH)]
        done, stored = sem("f_done"), sem("f_stored")
        with nc.Block() as block:

            @block.sync
            def _(sp):
                for i in range(NCH):
                    sp.dma_start(part[:, i], g.sums[i * CW:(i + 1) * CW].rearrange("(t p) n -> p t n", p=P)).then_inc(sums_in[i], 16)
                for i in range(NCH):
                    b, c0 = i // QC, (i % QC) * CT
                    sp.wait_ge(done, i + 1)
                    sp.dma_start(out[b].rearrange("(p c) n -> p c n", c=TB)[:, c0:c0 + CT, :],
                                 g.h[:, i * CT:(i + 1) * CT, :]).then_inc(stored, 16)
                sp.wait_ge(stored, 16 * NCH)

            @block.vector
            def _(dve):
                for i in range(NCH):
                    dve.wait_ge(sums_in[i], 16)
                    hc = g.h[:, i * CT:(i + 1) * CT, :]
                    nc.vector.tensor_tensor(hc, hc, part[:, i], ALU.add).then_inc(done, 1)


def build(nc, x, tok_table, pos_rev, pos_rev_t, carry_t, w_qkv, w_out, gate_rows, gate_bias, w1, b1, w2, b2_rows,
          out_rows, out):
    g = Chip()
    g.qk_parts = nc.dram_tensor("qk_parts", [3, 2 * C, N], BF16)
    g.x2_rows = nc.dram_tensor("x2_rows", [N + P, C], F32)
    g.sums = nc.dram_tensor("expert_sums", [N + P, C], F32)
    with ExitStack() as keep:
        sb = lambda ctx, name, shape, dt=F32: ctx.enter_context(nc.sbuf_tensor(name, shape, dt))
        g.ident = sb(keep, "ident", [P, P])
        g.h = sb(keep, "h", [P, NT, C])
        g.logits = sb(keep, "logits", [P, NT, E + 1])
        g.expert_of = sb(keep, "expert_of", [P, ET], I32)
        g.slot_token = sb(keep, "slot_token", [P, ET], I32)
        g.slot_weight = sb(keep, "slot_weight", [P, ET])
        g.mixed = sb(keep, "mixed_all", [P, NG, S])
        g.w_out = sb(keep, "w_out_rows", [P, NG // B, C])
        g.gate_w_a, g.gate_w_b = sb(keep, "gate_w_a", [P, E + 1]), sb(keep, "gate_w_b", [CB, E + 1])
        g.gate_b = sb(keep, "gate_b_rows", [P, E + 1])
        with ExitStack() as attn:
            g.spread = sb(attn, "spread", [P, P])
            g.v = sb(attn, "v_all", [P, NT, C])
            g.k6 = sb(attn, "k_pieces", [P, 2, HG, S], BF16)
            g.q6 = sb(attn, "q_pieces", [P, 4, HG, CW], BF16)
            g.k_in, g.q_in = attn.enter_context(nc.semaphore("k_in")), attn.enter_context(nc.semaphore("q_in"))
            embed_and_project(nc, g, x, tok_table, pos_rev, pos_rev_t, carry_t, w_qkv)
            attention(nc, g, w_out, gate_rows, gate_bias)
        g.b2 = sb(keep, "b2_all", [P, E, C])
        g.w1_a, g.w1_b = sb(keep, "w1_a", [P, E, F]), sb(keep, "w1_b", [CB + 1, E, F])
        g.w2 = sb(keep, "w2_all", [P, E, F // P, C])
        mix_heads_and_gate(nc, g, w1, b1, b2_rows)
        route(nc, g, w2)
        experts_and_spectrum(nc, g, out_rows)
        finish(nc, g, out)


def kernel(**inputs):
    import numpy as _np
    import concourse.bacc as _bacc
    from concourse import mybir as _mybir
    from concourse.bass_utils import run_bass_kernel_spmd as _run

    I = {k: _np.asarray(v) for k, v in inputs.items()}
    pos = I["L0_tok_pos_table"][::-1]
    feeds = {
        "x": I["x"],
        "tok_table": I["L0_tok_tok_table"],
        "pos_rev": pos,
        "pos_rev_t": pos.T,
        "carry_t": I["L0_tok_carry_W"].T,
        "w_qkv": I["L0_attn_w_qkv"],
        "w_out": I["L0_attn_w_out"],
        "gate_rows": _np.concatenate([I["L0_ffn_gate_w"], I["L0_ffn_v_w"][:, None]], axis=1),
        "gate_bias": _np.concatenate([I["L0_ffn_gate_b"], I["L0_ffn_v_b"].reshape(1)])[None, :],
        "w1": I["L0_ffn_w1"],
        "b1": I["L0_ffn_b1"],
        "w2": I["L0_ffn_w2"],
        "b2_rows": I["L0_ffn_b2"].reshape(1, -1),
        "out_rows": _np.concatenate([I["L0_ffn_out_w"], I["L0_ffn_out_b"][None], I["L0_ffn_bk_scale"][None]]).reshape(1, -1),
    }
    nc = _bacc.Bacc("TRN2", target_bir_lowering=False, num_devices=1)
    arrays, args = {}, []
    for name, a in feeds.items():
        a = _np.ascontiguousarray(a)
        arrays[f"in_{name}_dram"] = a
        args.append(nc.dram_tensor(f"in_{name}_dram", a.shape, _mybir.dt.from_np(a.dtype), kind="ExternalInput").ap())
    args.append(nc.dram_tensor("out_0_dram", (B, S, C), _mybir.dt.from_np(_np.dtype("float32")), kind="ExternalOutput").ap())
    build(nc, *args)
    r = _run(nc, [arrays], core_ids=[0])
    return r.results[0]["out_0_dram"]
```
